# Optimizing a Trainium2 kernel written in Bass

```python
import numpy as np
import jax
import jax.numpy as jnp

def _softmax(x, axis=-1):
    return jax.nn.softmax(x, axis=axis)

def _gelu(x):
    return jax.nn.gelu(x, approximate=True)

def _silu(x):
    return jax.nn.silu(x)

def _sigmoid(x):
    return jax.nn.sigmoid(x)

def _layernorm(x, axis=-1, eps=1e-05):
    m = jnp.mean(x, axis=axis, keepdims=True)
    v = jnp.var(x, axis=axis, keepdims=True)
    return (x - m) / jnp.sqrt(v + eps)

def _scatter_add(tgt, idx, src, axis=0):
    return tgt.at[idx].add(src)

def _segment_sum(src, seg, n):
    return jax.ops.segment_sum(src, seg, n)
kernel_name = 'mk_perceiver_d2_seqx_r2_f3629b'

def setup_inputs(seed: int=0):
    np.random.seed(seed)
    _w = jnp.asarray

    def _rec_inputs():
        import jax
        import jax.numpy as jnp
        _rk = jax.random.key(seed)
        x = -9.806e-05 + 1 * jax.random.normal(jax.random.fold_in(_rk, 1), (8, 64, 512), jnp.float32)
        _lenS = 64 - jax.random.randint(jax.random.fold_in(_rk, 7), (8,), 0, max(1, 64 // 4) + 1, jnp.int32)
        _lenS2 = 1601 - jax.random.randint(jax.random.fold_in(_rk, 8), (8,), 0, max(1, 1601 // 4) + 1, jnp.int32)
        _ctx_1024P = jax.random.normal(jax.random.fold_in(_rk, 11), (8, 16, 512), jnp.float32)
        _ctx_1024c = jax.random.dirichlet(jax.random.fold_in(_rk, 511), 0.3 * jnp.ones((16,), jnp.float32), (8, 1601))
        _ctx_1024t = jnp.einsum('bsk,bkd->bsd', _ctx_1024c, _ctx_1024P)
        _ctx_1024t = _ctx_1024t * jax.lax.rsqrt(jnp.mean(jnp.square(_ctx_1024t)) + 1e-12) * 0.953939
        ctx_1024 = -1.52775e-05 + 0.999936 * (_ctx_1024t + 0.3 * jax.random.normal(jax.random.fold_in(_rk, 611), (8, 1601, 512), jnp.float32))
        _validS = jnp.arange(64)[None, :] < _lenS[:, None]
        _validS2 = jnp.arange(1601)[None, :] < _lenS2[:, None]
        _causal = jnp.tril(jnp.ones((64, 64), dtype=bool))
        mask_SxS2_ik0 = jnp.where(jnp.broadcast_to(_validS2[0:1, :], (64, 1601)), 0, 1).astype(jnp.int32)
        return (x, ctx_1024, mask_SxS2_ik0)
    x, ctx_1024, mask_SxS2_ik0 = _rec_inputs()

    def _L0_xattn_setup():
        import jax, jax.numpy as jnp
        import numpy as np
        D = 512
        NUM_ITERS = 3
        EPS = 1e-06
        SCALE = D ** (-0.5)

        def rmsnorm(x, w, eps=EPS):
            return x * jax.lax.rsqrt(jnp.mean(x * x, axis=-1, keepdims=True) + eps) * w

        def gru_cell(x, h, wih, whh, bih, bhh):
            gx = x @ wih.T + bih
            gh = h @ whh.T + bhh
            xr, xz, xn = jnp.split(gx, 3, axis=-1)
            hr, hz, hn = jnp.split(gh, 3, axis=-1)
            r = jax.nn.sigmoid(xr + hr)
            z = jax.nn.sigmoid(xz + hz)
            n = jnp.tanh(xn + r * hn)
            return (1.0 - z) * n + z * h
        key = jax.random.key(seed)
        ks = jax.random.split(key, 8)
        B, K, M, d = (8, 64, 2048, D)
        w_std = d ** (-0.5)
        return {'slots': jax.random.normal(ks[0], (B, K, d), jnp.float32), 'P': jax.random.normal(ks[1], (B, M, d), jnp.float32), 'Wq': jax.random.normal(ks[2], (d, d), jnp.float32) * w_std, 'Wk': jax.random.normal(ks[3], (d, d), jnp.float32) * w_std, 'Wv': jax.random.normal(ks[4], (d, d), jnp.float32) * w_std, 'gru_wih': jax.random.normal(ks[5], (3 * d, d), jnp.float32) * w_std, 'gru_whh': jax.random.normal(ks[6], (3 * d, d), jnp.float32) * w_std, 'gru_bih': jnp.zeros((3 * d,), jnp.float32), 'gru_bhh': jnp.zeros((3 * d,), jnp.float32), 'slot_norm_w': jnp.ones((d,), jnp.float32), 'input_norm_w': jnp.ones((d,), jnp.float32)}
    _L0_xattn_all = _L0_xattn_setup()
    _L0_xattn_in = {k: v for k, v in _L0_xattn_all.items() if k in ('Wq', 'Wk', 'Wv', 'gru_wih', 'gru_whh', 'gru_bih', 'gru_bhh', 'slot_norm_w', 'input_norm_w')}
    del _L0_xattn_all

    def _L0_attn_setup():
        import jax, jax.numpy as jnp
        import numpy as np
        D_MODEL = 512
        D_STATE = 16
        BATCH = 4
        SEQ = 1024

        def layer_norm(x, w, b, eps=1e-05):
            mu = jnp.mean(x, axis=-1, keepdims=True)
            var = jnp.mean((x - mu) ** 2, axis=-1, keepdims=True)
            return (x - mu) / jnp.sqrt(var + eps) * w + b

        def linear(x, w, b):
            return jnp.einsum('...i,oi->...o', x, w) + b

        def ssm_scan(x, A, B_mat, C_mat, D_vec):
            Bsz, L, D = x.shape
            N = A.shape[1]
            h0 = jnp.zeros((Bsz, D, N), x.dtype)

            def step(h, xt):
                h = A[None] * h + B_mat[None] * xt[..., None]
                yt = jnp.einsum('dn,bdn->bd', C_mat, h) + D_vec * xt
                return (h, yt)
            _, ys = jax.lax.scan(step, h0, jnp.swapaxes(x, 0, 1))
            return jnp.swapaxes(ys, 0, 1)
        key = jax.random.key(seed)
        ks = jax.random.split(key, 10)
        d, n, h = (D_MODEL, D_STATE, 4 * D_MODEL)
        inp = {'x': jax.random.normal(ks[0], (BATCH, SEQ, d), dtype=jnp.float32), 'ln_w': jnp.ones((d,), jnp.float32), 'ln_b': jnp.zeros((d,), jnp.float32), 'A_log': jnp.log(jax.random.uniform(ks[1], (d, n), dtype=jnp.float32) + 0.0001), 'B_mat': jax.random.normal(ks[2], (d, n), dtype=jnp.float32), 'C_mat': jax.random.normal(ks[3], (d, n), dtype=jnp.float32), 'D_vec': jax.random.normal(ks[4], (d,), dtype=jnp.float32), 'out_w': jax.random.normal(ks[5], (d, d), dtype=jnp.float32) * (1.0 / np.sqrt(d)), 'out_b': jnp.zeros((d,), jnp.float32), 'ln2_w': jnp.ones((d,), jnp.float32), 'ln2_b': jnp.zeros((d,), jnp.float32), 'ffn1_w': jax.random.normal(ks[6], (h, d), dtype=jnp.float32) * (1.0 / np.sqrt(d)), 'ffn1_b': jnp.zeros((h,), jnp.float32), 'ffn2_w': jax.random.normal(ks[7], (d, h), dtype=jnp.float32) * (1.0 / np.sqrt(h)), 'ffn2_b': jnp.zeros((d,), jnp.float32)}
        return inp
    _L0_attn_all = _L0_attn_setup()
    _L0_attn_in = {k: v for k, v in _L0_attn_all.items() if k in ('ln_w', 'ln_b', 'A_log', 'B_mat', 'C_mat', 'D_vec', 'out_w', 'out_b', 'ln2_w', 'ln2_b', 'ffn1_w', 'ffn1_b', 'ffn2_w', 'ffn2_b')}
    del _L0_attn_all

    def _L0_ffn_setup():
        import jax, jax.numpy as jnp
        import numpy as np
        DIM, HEADS, EXPERTS, DFF = (512, 16, 8, 2048)
        EPS = 1e-05

        def layernorm(x, g, b):
            mu = jnp.mean(x, -1, keepdims=True)
            var = jnp.mean(jnp.square(x - mu), -1, keepdims=True)
            return (x - mu) * jax.lax.rsqrt(var + EPS) * g + b
        key = jax.random.key(seed)
        ks = jax.random.split(key, 12)
        s = lambda d: 1.0 / np.sqrt(d)
        return {'x': jax.random.normal(ks[0], (2, 1024, DIM), jnp.float32), 'conv_w': jax.random.normal(ks[1], (DIM, DIM, 3), jnp.float32) * s(DIM * 3), 'conv_b': jnp.zeros((DIM,), jnp.float32), 'wqkv': jax.random.normal(ks[2], (3 * DIM, DIM), jnp.float32) * s(DIM), 'bqkv': jnp.zeros((3 * DIM,), jnp.float32), 'wo': jax.random.normal(ks[3], (DIM, DIM), jnp.float32) * s(DIM), 'bo': jnp.zeros((DIM,), jnp.float32), 'ln1_g': jnp.ones((DIM,), jnp.float32), 'ln1_b': jnp.zeros((DIM,), jnp.float32), 'gate_w': jax.random.normal(ks[4], (DIM, EXPERTS), jnp.float32) * s(DIM), 'gate_b': jnp.zeros((EXPERTS,), jnp.float32), 'w1': jax.random.normal(ks[5], (EXPERTS, DIM, DFF), jnp.float32) * s(DIM), 'b1': jnp.zeros((EXPERTS, DFF), jnp.float32), 'w2': jax.random.normal(ks[6], (EXPERTS, DFF, DIM), jnp.float32) * s(DFF), 'b2': jnp.zeros((EXPERTS, DIM), jnp.float32), 'ln2_g': jnp.ones((DIM,), jnp.float32), 'ln2_b': jnp.zeros((DIM,), jnp.float32)}
    _L0_ffn_all = _L0_ffn_setup()
    _L0_ffn_in = {k: v for k, v in _L0_ffn_all.items() if k in ('conv_w', 'conv_b', 'wqkv', 'bqkv', 'wo', 'bo', 'ln1_g', 'ln1_b', 'gate_w', 'gate_b', 'w1', 'b1', 'w2', 'b2', 'ln2_g', 'ln2_b')}
    del _L0_ffn_all

    def _L1_xattn_setup():
        import jax, jax.numpy as jnp
        import numpy as np
        B, S, D, H = (2, 1024, 512, 16)
        HD = D // H
        DENSITY = 0.1
        key = jax.random.key(seed)
        ks = jax.random.split(key, 12)
        scale = 0.02
        inp = {'query': jax.random.normal(ks[0], (B, S, D), jnp.float32), 'key': jax.random.normal(ks[1], (B, S, D), jnp.float32), 'value': jax.random.normal(ks[2], (B, S, D), jnp.float32)}
        m = jax.random.uniform(ks[3], (S, S)) < DENSITY
        m = m.at[jnp.arange(S), jnp.arange(S)].set(True)
        inp['mask'] = m.astype(jnp.int32)
        inp['Wq'] = jax.random.normal(ks[4], (D, D), jnp.float32) * scale
        inp['bq'] = jax.random.normal(ks[5], (D,), jnp.float32) * scale
        inp['Wk'] = jax.random.normal(ks[6], (D, D), jnp.float32) * scale
        inp['bk'] = jax.random.normal(ks[7], (D,), jnp.float32) * scale
        inp['Wv'] = jax.random.normal(ks[8], (D, D), jnp.float32) * scale
        inp['bv'] = jax.random.normal(ks[9], (D,), jnp.float32) * scale
        inp['Wo'] = jax.random.normal(ks[10], (D, D), jnp.float32) * scale
        inp['bo'] = jax.random.normal(ks[11], (D,), jnp.float32) * scale
        return inp
    _L1_xattn_all = _L1_xattn_setup()
    _L1_xattn_in = {k: v for k, v in _L1_xattn_all.items() if k in ('Wq', 'bq', 'Wk', 'bk', 'Wv', 'bv', 'Wo', 'bo')}
    del _L1_xattn_all

    def _L1_attn_setup():
        import jax, jax.numpy as jnp
        import numpy as np
        import math
        D_MODEL = 512
        NUM_HEADS = 16
        D_HEAD = D_MODEL // NUM_HEADS
        SEQ = 1024
        BATCH = 2
        THETA = 10000.0
        SCALE = 1.0 / math.sqrt(D_HEAD)

        def rope_cos_sin(seq_len, d_head, theta):
            inv_freq = 1.0 / theta ** (jnp.arange(0, d_head, 2, dtype=jnp.float32) / d_head)
            t = jnp.arange(seq_len, dtype=jnp.float32)
            ang = jnp.outer(t, inv_freq)
            return (jnp.cos(ang), jnp.sin(ang))

        def apply_rope(x, cos, sin):
            B, S, H, Dh = x.shape
            xr = x.reshape(B, S, H, Dh // 2, 2)
            x0, x1 = (xr[..., 0], xr[..., 1])
            c = cos[None, :, None, :]
            s = sin[None, :, None, :]
            out = jnp.stack([x0 * c - x1 * s, x0 * s + x1 * c], axis=-1)
            return out.reshape(B, S, H, Dh)
        key = jax.random.key(seed)
        ks = jax.random.split(key, 9)
        w_std = 0.02
        return {'qkv': jax.random.normal(ks[0], (BATCH, SEQ, D_MODEL), jnp.float32), 'Wq': jax.random.normal(ks[1], (D_MODEL, D_MODEL), jnp.float32) * w_std, 'bq': jax.random.normal(ks[2], (D_MODEL,), jnp.float32) * w_std, 'Wk': jax.random.normal(ks[3], (D_MODEL, D_MODEL), jnp.float32) * w_std, 'bk': jax.random.normal(ks[4], (D_MODEL,), jnp.float32) * w_std, 'Wv': jax.random.normal(ks[5], (D_MODEL, D_MODEL), jnp.float32) * w_std, 'bv': jax.random.normal(ks[6], (D_MODEL,), jnp.float32) * w_std, 'Wo': jax.random.normal(ks[7], (D_MODEL, D_MODEL), jnp.float32) * w_std, 'bo': jax.random.normal(ks[8], (D_MODEL,), jnp.float32) * w_std}
    _L1_attn_all = _L1_attn_setup()
    _L1_attn_in = {k: v for k, v in _L1_attn_all.items() if k in ('Wq', 'bq', 'Wk', 'bk', 'Wv', 'bv', 'Wo', 'bo')}
    del _L1_attn_all

    def _L1_ffn_setup():
        import jax, jax.numpy as jnp
        import numpy as np
        NUM_EXPERTS = 8
        CAPACITY_FACTOR = 1.0
        key = jax.random.key(seed)
        k1, k2, k3, k4 = jax.random.split(key, 4)
        B, S, D, E, F = (8, 1024, 512, NUM_EXPERTS, 2048)
        x = jax.random.normal(k1, (B, S, D), dtype=jnp.float32)
        router_w = jax.random.normal(k2, (D, E), dtype=jnp.float32) * D ** (-0.5)
        w1 = jax.random.normal(k3, (E, D, F), dtype=jnp.float32) * D ** (-0.5)
        w2 = jax.random.normal(k4, (E, F, D), dtype=jnp.float32) * F ** (-0.5)
        return {'x': x, 'router_w': router_w, 'w1': w1, 'w2': w2}
    _L1_ffn_all = _L1_ffn_setup()
    _L1_ffn_in = {k: v for k, v in _L1_ffn_all.items() if k in ('router_w', 'w1', 'w2')}
    del _L1_ffn_all
    return {'x': x, 'ctx_1024': ctx_1024, 'mask_SxS2_ik0': mask_SxS2_ik0, 'L0_xattn_Wq': _L0_xattn_in['Wq'], 'L0_xattn_Wk': _L0_xattn_in['Wk'], 'L0_xattn_Wv': _L0_xattn_in['Wv'], 'L0_xattn_gru_wih': _L0_xattn_in['gru_wih'], 'L0_xattn_gru_whh': _L0_xattn_in['gru_whh'], 'L0_xattn_gru_bih': _L0_xattn_in['gru_bih'], 'L0_xattn_gru_bhh': _L0_xattn_in['gru_bhh'], 'L0_xattn_slot_norm_w': _L0_xattn_in['slot_norm_w'], 'L0_xattn_input_norm_w': _L0_xattn_in['input_norm_w'], 'L0_attn_ln_w': _L0_attn_in['ln_w'], 'L0_attn_ln_b': _L0_attn_in['ln_b'], 'L0_attn_A_log': _L0_attn_in['A_log'], 'L0_attn_B_mat': _L0_attn_in['B_mat'], 'L0_attn_C_mat': _L0_attn_in['C_mat'], 'L0_attn_D_vec': _L0_attn_in['D_vec'], 'L0_attn_out_w': _L0_attn_in['out_w'], 'L0_attn_out_b': _L0_attn_in['out_b'], 'L0_attn_ln2_w': _L0_attn_in['ln2_w'], 'L0_attn_ln2_b': _L0_attn_in['ln2_b'], 'L0_attn_ffn1_w': _L0_attn_in['ffn1_w'], 'L0_attn_ffn1_b': _L0_attn_in['ffn1_b'], 'L0_attn_ffn2_w': _L0_attn_in['ffn2_w'], 'L0_attn_ffn2_b': _L0_attn_in['ffn2_b'], 'L0_ffn_conv_w': _L0_ffn_in['conv_w'], 'L0_ffn_conv_b': _L0_ffn_in['conv_b'], 'L0_ffn_wqkv': _L0_ffn_in['wqkv'], 'L0_ffn_bqkv': _L0_ffn_in['bqkv'], 'L0_ffn_wo': _L0_ffn_in['wo'], 'L0_ffn_bo': _L0_ffn_in['bo'], 'L0_ffn_ln1_g': _L0_ffn_in['ln1_g'], 'L0_ffn_ln1_b': _L0_ffn_in['ln1_b'], 'L0_ffn_gate_w': _L0_ffn_in['gate_w'], 'L0_ffn_gate_b': _L0_ffn_in['gate_b'], 'L0_ffn_w1': _L0_ffn_in['w1'], 'L0_ffn_b1': _L0_ffn_in['b1'], 'L0_ffn_w2': _L0_ffn_in['w2'], 'L0_ffn_b2': _L0_ffn_in['b2'], 'L0_ffn_ln2_g': _L0_ffn_in['ln2_g'], 'L0_ffn_ln2_b': _L0_ffn_in['ln2_b'], 'L1_xattn_Wq': _L1_xattn_in['Wq'], 'L1_xattn_bq': _L1_xattn_in['bq'], 'L1_xattn_Wk': _L1_xattn_in['Wk'], 'L1_xattn_bk': _L1_xattn_in['bk'], 'L1_xattn_Wv': _L1_xattn_in['Wv'], 'L1_xattn_bv': _L1_xattn_in['bv'], 'L1_xattn_Wo': _L1_xattn_in['Wo'], 'L1_xattn_bo': _L1_xattn_in['bo'], 'L1_attn_Wq': _L1_attn_in['Wq'], 'L1_attn_bq': _L1_attn_in['bq'], 'L1_attn_Wk': _L1_attn_in['Wk'], 'L1_attn_bk': _L1_attn_in['bk'], 'L1_attn_Wv': _L1_attn_in['Wv'], 'L1_attn_bv': _L1_attn_in['bv'], 'L1_attn_Wo': _L1_attn_in['Wo'], 'L1_attn_bo': _L1_attn_in['bo'], 'L1_ffn_router_w': _L1_ffn_in['router_w'], 'L1_ffn_w1': _L1_ffn_in['w1'], 'L1_ffn_w2': _L1_ffn_in['w2']}

def reference(x, ctx_1024, mask_SxS2_ik0, L0_xattn_Wq, L0_xattn_Wk, L0_xattn_Wv, L0_xattn_gru_wih, L0_xattn_gru_whh, L0_xattn_gru_bih, L0_xattn_gru_bhh, L0_xattn_slot_norm_w, L0_xattn_input_norm_w, L0_attn_ln_w, L0_attn_ln_b, L0_attn_A_log, L0_attn_B_mat, L0_attn_C_mat, L0_attn_D_vec, L0_attn_out_w, L0_attn_out_b, L0_attn_ln2_w, L0_attn_ln2_b, L0_attn_ffn1_w, L0_attn_ffn1_b, L0_attn_ffn2_w, L0_attn_ffn2_b, L0_ffn_conv_w, L0_ffn_conv_b, L0_ffn_wqkv, L0_ffn_bqkv, L0_ffn_wo, L0_ffn_bo, L0_ffn_ln1_g, L0_ffn_ln1_b, L0_ffn_gate_w, L0_ffn_gate_b, L0_ffn_w1, L0_ffn_b1, L0_ffn_w2, L0_ffn_b2, L0_ffn_ln2_g, L0_ffn_ln2_b, L1_xattn_Wq, L1_xattn_bq, L1_xattn_Wk, L1_xattn_bk, L1_xattn_Wv, L1_xattn_bv, L1_xattn_Wo, L1_xattn_bo, L1_attn_Wq, L1_attn_bq, L1_attn_Wk, L1_attn_bk, L1_attn_Wv, L1_attn_bv, L1_attn_Wo, L1_attn_bo, L1_ffn_router_w, L1_ffn_w1, L1_ffn_w2):
    import jax
    import jax.numpy as jnp

    def _L0_xattn_ref(slots, P, Wq, Wk, Wv, gru_wih, gru_whh, gru_bih, gru_bhh, slot_norm_w, input_norm_w):
        import jax, jax.numpy as jnp
        import numpy as np
        D = 512
        NUM_ITERS = 3
        EPS = 1e-06
        SCALE = D ** (-0.5)

        def rmsnorm(x, w, eps=EPS):
            return x * jax.lax.rsqrt(jnp.mean(x * x, axis=-1, keepdims=True) + eps) * w

        def gru_cell(x, h, wih, whh, bih, bhh):
            gx = x @ wih.T + bih
            gh = h @ whh.T + bhh
            xr, xz, xn = jnp.split(gx, 3, axis=-1)
            hr, hz, hn = jnp.split(gh, 3, axis=-1)
            r = jax.nn.sigmoid(xr + hr)
            z = jax.nn.sigmoid(xz + hz)
            n = jnp.tanh(xn + r * hn)
            return (1.0 - z) * n + z * h
        Pn = rmsnorm(P, input_norm_w)
        k_proj = Pn @ Wk.T
        v_proj = Pn @ Wv.T
        for _ in range(NUM_ITERS):
            sn = rmsnorm(slots, slot_norm_w)
            q_proj = sn @ Wq.T
            scores = jnp.einsum('bkd,bmd->bkm', q_proj, k_proj) * SCALE
            attn = jax.nn.softmax(scores, axis=-2)
            attn = attn / (jnp.sum(attn, axis=-1, keepdims=True) + EPS)
            updates = jnp.einsum('bkm,bmd->bkd', attn, v_proj)
            slots = gru_cell(updates, slots, gru_wih, gru_whh, gru_bih, gru_bhh)
        return slots

    def _L0_attn_ref(x, ln_w, ln_b, A_log, B_mat, C_mat, D_vec, out_w, out_b, ln2_w, ln2_b, ffn1_w, ffn1_b, ffn2_w, ffn2_b):
        import jax, jax.numpy as jnp
        import numpy as np
        D_MODEL = 512
        D_STATE = 16
        BATCH = 4
        SEQ = 1024

        def layer_norm(x, w, b, eps=1e-05):
            mu = jnp.mean(x, axis=-1, keepdims=True)
            var = jnp.mean((x - mu) ** 2, axis=-1, keepdims=True)
            return (x - mu) / jnp.sqrt(var + eps) * w + b

        def linear(x, w, b):
            return jnp.einsum('...i,oi->...o', x, w) + b

        def ssm_scan(x, A, B_mat, C_mat, D_vec):
            Bsz, L, D = x.shape
            N = A.shape[1]
            h0 = jnp.zeros((Bsz, D, N), x.dtype)

            def step(h, xt):
                h = A[None] * h + B_mat[None] * xt[..., None]
                yt = jnp.einsum('dn,bdn->bd', C_mat, h) + D_vec * xt
                return (h, yt)
            _, ys = jax.lax.scan(step, h0, jnp.swapaxes(x, 0, 1))
            return jnp.swapaxes(ys, 0, 1)
        res = x
        xn = layer_norm(x, ln_w, ln_b)
        A = jax.nn.sigmoid(A_log)
        y = ssm_scan(xn, A, B_mat, C_mat, D_vec)
        y = jax.nn.silu(y)
        y = linear(y, out_w, out_b)
        x1 = res + y
        res2 = x1
        xn2 = layer_norm(x1, ln2_w, ln2_b)
        hdn = jax.nn.gelu(linear(xn2, ffn1_w, ffn1_b), approximate=False)
        out = res2 + linear(hdn, ffn2_w, ffn2_b)
        return out

    def _L0_ffn_ref(x, conv_w, conv_b, wqkv, bqkv, wo, bo, ln1_g, ln1_b, gate_w, gate_b, w1, b1, w2, b2, ln2_g, ln2_b):
        import jax, jax.numpy as jnp
        import numpy as np
        DIM, HEADS, EXPERTS, DFF = (512, 16, 8, 2048)
        EPS = 1e-05

        def layernorm(x, g, b):
            mu = jnp.mean(x, -1, keepdims=True)
            var = jnp.mean(jnp.square(x - mu), -1, keepdims=True)
            return (x - mu) * jax.lax.rsqrt(var + EPS) * g + b
        B, S, D = x.shape
        H, dh = (HEADS, D // HEADS)
        xt = jnp.transpose(x, (0, 2, 1))
        xt = jax.lax.conv_general_dilated(xt, conv_w, (1,), [(1, 1)], dimension_numbers=('NCH', 'OIH', 'NCH'))
        x = jnp.transpose(xt + conv_b[None, :, None], (0, 2, 1))
        qkv = x @ wqkv.T + bqkv
        q, k, v = jnp.split(qkv, 3, axis=-1)
        q = q.reshape(B, S, H, dh).transpose(0, 2, 1, 3)
        k = k.reshape(B, S, H, dh).transpose(0, 2, 1, 3)
        v = v.reshape(B, S, H, dh).transpose(0, 2, 1, 3)
        scores = jnp.einsum('bhqd,bhkd->bhqk', q, k) / jnp.sqrt(jnp.float32(dh))
        attn = jax.nn.softmax(scores, axis=-1)
        ctx = jnp.einsum('bhqk,bhkd->bhqd', attn, v)
        ctx = ctx.transpose(0, 2, 1, 3).reshape(B, S, D)
        attn_out = ctx @ wo.T + bo
        x = layernorm(x + attn_out, ln1_g, ln1_b)
        probs = jax.nn.softmax(x @ gate_w + gate_b, axis=-1)
        h = jax.nn.relu(jnp.einsum('bsd,edf->bsef', x, w1) + b1)
        y = jnp.einsum('bsef,efd->bsed', h, w2) + b2
        moe_out = jnp.einsum('bse,bsed->bsd', probs, y)
        x = layernorm(x + moe_out, ln2_g, ln2_b)
        return x

    def _L1_xattn_ref(query, key, value, mask, Wq, bq, Wk, bk, Wv, bv, Wo, bo):
        import jax, jax.numpy as jnp
        import numpy as np
        B, S, D, H = (2, 1024, 512, 16)
        HD = D // H
        DENSITY = 0.1
        b = query.shape[0]
        q = (query @ Wq + bq).reshape(b, -1, H, HD).transpose(0, 2, 1, 3)
        k = (key @ Wk + bk).reshape(b, -1, H, HD).transpose(0, 2, 1, 3)
        v = (value @ Wv + bv).reshape(b, -1, H, HD).transpose(0, 2, 1, 3)
        keep = mask.astype(bool)
        scores = jnp.einsum('bhsd,bhtd->bhst', q, k) / jnp.sqrt(jnp.asarray(HD, q.dtype))
        neg = jnp.finfo(scores.dtype).min
        scores = jnp.where(keep[None, None], scores, neg)
        w = jax.nn.softmax(scores, axis=-1)
        w = jnp.where(keep[None, None], w, jnp.asarray(0, w.dtype))
        out = jnp.einsum('bhst,bhtd->bhsd', w, v)
        out = out.transpose(0, 2, 1, 3).reshape(b, -1, D)
        return out @ Wo + bo

    def _L1_attn_ref(qkv, Wq, bq, Wk, bk, Wv, bv, Wo, bo):
        import jax, jax.numpy as jnp
        import numpy as np
        import math
        D_MODEL = 512
        NUM_HEADS = 16
        D_HEAD = D_MODEL // NUM_HEADS
        SEQ = 1024
        BATCH = 2
        THETA = 10000.0
        SCALE = 1.0 / math.sqrt(D_HEAD)

        def rope_cos_sin(seq_len, d_head, theta):
            inv_freq = 1.0 / theta ** (jnp.arange(0, d_head, 2, dtype=jnp.float32) / d_head)
            t = jnp.arange(seq_len, dtype=jnp.float32)
            ang = jnp.outer(t, inv_freq)
            return (jnp.cos(ang), jnp.sin(ang))

        def apply_rope(x, cos, sin):
            B, S, H, Dh = x.shape
            xr = x.reshape(B, S, H, Dh // 2, 2)
            x0, x1 = (xr[..., 0], xr[..., 1])
            c = cos[None, :, None, :]
            s = sin[None, :, None, :]
            out = jnp.stack([x0 * c - x1 * s, x0 * s + x1 * c], axis=-1)
            return out.reshape(B, S, H, Dh)
        B, S, D = qkv.shape
        cos, sin = rope_cos_sin(S, D_HEAD, THETA)
        q = (qkv @ Wq.T + bq).reshape(B, S, NUM_HEADS, D_HEAD)
        k = (qkv @ Wk.T + bk).reshape(B, S, NUM_HEADS, D_HEAD)
        v = (qkv @ Wv.T + bv).reshape(B, S, NUM_HEADS, D_HEAD)
        q = apply_rope(q, cos, sin)
        k = apply_rope(k, cos, sin)
        scores = jnp.einsum('bqhd,bkhd->bhqk', q, k) * SCALE
        causal = jnp.triu(jnp.ones((S, S), dtype=bool), k=1)
        scores = jnp.where(causal[None, None], -1e+30, scores)
        attn = jax.nn.softmax(scores, axis=-1)
        out = jnp.einsum('bhqk,bkhd->bqhd', attn, v).reshape(B, S, D)
        return out @ Wo.T + bo

    def _L1_ffn_ref(x, router_w, w1, w2):
        import jax, jax.numpy as jnp
        import numpy as np
        NUM_EXPERTS = 8
        CAPACITY_FACTOR = 1.0
        B, S, D = x.shape
        E = router_w.shape[1]
        T = B * S
        C = int(CAPACITY_FACTOR * T / E)
        x_flat = x.reshape(T, D)
        logits = x_flat @ router_w
        probs = jax.nn.softmax(logits, axis=-1)
        expert_idx = jnp.argmax(probs, axis=-1)
        gate = jnp.take_along_axis(probs, expert_idx[:, None], axis=1)[:, 0]
        onehot = jax.nn.one_hot(expert_idx, E, dtype=jnp.float32)
        pos_all = jnp.cumsum(onehot, axis=0) - 1.0
        pos = jnp.take_along_axis(pos_all, expert_idx[:, None], axis=1)[:, 0]
        pos = pos.astype(jnp.int32)
        keep = (pos < C).astype(x_flat.dtype)
        pos_c = jnp.clip(pos, 0, C - 1)
        expert_in = jnp.zeros((E, C, D), dtype=x_flat.dtype)
        expert_in = expert_in.at[expert_idx, pos_c].add(x_flat * keep[:, None])
        hidden = jax.nn.gelu(jnp.einsum('ecd,edf->ecf', expert_in, w1))
        expert_out = jnp.einsum('ecf,efd->ecd', hidden, w2)
        y = expert_out[expert_idx, pos_c] * (gate * keep)[:, None]
        return y.reshape(B, S, D)
    x = x + _L0_xattn_ref(_layernorm(x, axis=-1), ctx_1024, L0_xattn_Wq, L0_xattn_Wk, L0_xattn_Wv, L0_xattn_gru_wih, L0_xattn_gru_whh, L0_xattn_gru_bih, L0_xattn_gru_bhh, L0_xattn_slot_norm_w, L0_xattn_input_norm_w)
    x = x + _L0_attn_ref(_layernorm(x, axis=-1), L0_attn_ln_w, L0_attn_ln_b, L0_attn_A_log, L0_attn_B_mat, L0_attn_C_mat, L0_attn_D_vec, L0_attn_out_w, L0_attn_out_b, L0_attn_ln2_w, L0_attn_ln2_b, L0_attn_ffn1_w, L0_attn_ffn1_b, L0_attn_ffn2_w, L0_attn_ffn2_b)
    x = x + _L0_ffn_ref(_layernorm(x, axis=-1), L0_ffn_conv_w, L0_ffn_conv_b, L0_ffn_wqkv, L0_ffn_bqkv, L0_ffn_wo, L0_ffn_bo, L0_ffn_ln1_g, L0_ffn_ln1_b, L0_ffn_gate_w, L0_ffn_gate_b, L0_ffn_w1, L0_ffn_b1, L0_ffn_w2, L0_ffn_b2, L0_ffn_ln2_g, L0_ffn_ln2_b)
    x = x + _L1_xattn_ref(_layernorm(x, axis=-1), ctx_1024, ctx_1024, mask_SxS2_ik0, L1_xattn_Wq, L1_xattn_bq, L1_xattn_Wk, L1_xattn_bk, L1_xattn_Wv, L1_xattn_bv, L1_xattn_Wo, L1_xattn_bo)
    x = x + _L1_attn_ref(_layernorm(x, axis=-1), L1_attn_Wq, L1_attn_bq, L1_attn_Wk, L1_attn_bk, L1_attn_Wv, L1_attn_bv, L1_attn_Wo, L1_attn_bo)
    x = x + _L1_ffn_ref(_layernorm(x, axis=-1), L1_ffn_router_w, L1_ffn_w1, L1_ffn_w2)
    return x

_drawn_inputs = setup_inputs


def setup_inputs(seed=0):
    import zlib

    import numpy as np

    out = dict(_drawn_inputs(seed))
    spreads = {'L0_xattn_gru_bih': (0.0, 0.1),
     'L0_xattn_gru_bhh': (0.0, 0.1),
     'L0_xattn_slot_norm_w': (1.0, 0.6),
     'L0_xattn_input_norm_w': (1.0, 0.2),
     'L0_attn_ln_w': (1.0, 0.2),
     'L0_attn_ln_b': (0.0, 0.1),
     'L0_attn_out_b': (0.0, 0.32),
     'L0_attn_ln2_w': (1.0, 0.2),
     'L0_attn_ln2_b': (0.0, 0.458),
     'L0_attn_ffn1_b': (0.0, 0.473),
     'L0_attn_ffn2_b': (0.0, 0.319),
     'L0_ffn_conv_b': (0.0, 0.272),
     'L0_ffn_bqkv': (0.0, 0.351),
     'L0_ffn_bo': (0.0, 0.352),
     'L0_ffn_ln1_g': (1.0, 0.2),
     'L0_ffn_ln1_b': (0.0, 0.33),
     'L0_ffn_gate_b': (0.0, 0.8),
     'L0_ffn_b1': (0.0, 0.8),
     'L0_ffn_b2': (0.0, 0.626),
     'L0_ffn_ln2_g': (1.0, 0.2),
     'L0_ffn_ln2_b': (0.0, 0.339)}
    factors = {'L1_xattn_Wq': 8.0,
     'L1_xattn_bq': 64.0,
     'L1_xattn_Wk': 8.0,
     'L1_xattn_bk': 200.0,
     'L1_xattn_bv': 26.727,
     'L1_xattn_bo': 8.0,
     'L1_attn_Wq': 8.0,
     'L1_attn_bq': 178.072,
     'L1_attn_Wk': 8.0,
     'L1_attn_bk': 200.0,
     'L1_attn_bv': 26.283,
     'L1_attn_bo': 8.0}
    for name, (base, spread) in spreads.items():
        noise = np.random.default_rng([zlib.crc32(name.encode()), seed]).standard_normal(out[name].shape)
        drawn = base * np.exp(spread * noise) if base else spread * noise
        out[name] = jnp.asarray(drawn.astype(out[name].dtype))
    for name, factor in factors.items():
        out[name] = (out[name] * factor).astype(out[name].dtype)
    return out
```

```python
import numpy as np
import concourse.bass as bass
from concourse import mybir
from contextlib import ExitStack, contextmanager

FP32, BF16, I32 = mybir.dt.float32, mybir.dt.bfloat16, mybir.dt.int32
ALU, ACT, AX = mybir.AluOpType, mybir.ActivationFunctionType, mybir.AxisListType

B, S, D = 8, 64, 512
T = B * S
P = 128
KC = D // P
M = 1601
MT = -(-M // P)
MP = MT * P
MLAST = M - (MT - 1) * P
HALF = [(0, 7), (7, MT - 7)]
H, HD = 16, 32
G = H // KC
E_, F = 8, 2048
FS = F // D
CAP = T // E_
N_STATE = 16
RING = 4
MB = MP // 4
NEG = -1e30

S1_TILES = ["wq", "wk", "wv"] + [f"{w}{g}" for g in range(3) for w in ("wih", "whh")]
SMALL = [f"s1.{n}" for n in S1_TILES]
SMALL += ["s2.out"] + [f"s2.{w}{j}" for j in range(FS) for w in ("ffn1_", "ffn2_")]
SMALL += [f"s3.conv{k}" for k in range(3)] + ["s3.wq", "s3.wk", "s3.wv", "s3.wo"]
SMALL += ["s4.wq", "s4.wk", "s4.wv", "s4.wo", "s5.wq", "s5.wk", "s5.wv", "s5.wo"]
AT = {n: i for i, n in enumerate(SMALL)}

VECS = [("slot_w", 4), ("in_w", 4), ("bih", 12), ("bhh", 12), ("ln_w", 4), ("ln_b", 4), ("D", 4), ("out_b", 4),
        ("ln2_w", 4), ("ln2_b", 4), ("ffn1_b", 16), ("ffn2_b", 4), ("conv_b", 4), ("bqkv", 12), ("bo3", 4),
        ("ln1_g", 4), ("ln1_b", 4), ("ln2_g", 4), ("ln2b3", 4), ("b1", 16 * E_), ("b2", 4 * E_),
        ("bq4", 4), ("bk4", 4), ("bo4", 4), ("bq5", 4), ("bk5", 4), ("bo5", 4)]
VAT, _n = {}, 0
for _k, _w in VECS:
    VAT[_k] = _n
    _n += _w
NVEC = _n
ROWS = [("gate_b", 8), ("bv3", D), ("bv4", D), ("bv5", D), ("iota_slot", D), ("iota_e", 4 * E_)]
RAT, _n = {}, 0
for _k, _w in ROWS:
    RAT[_k] = _n
    _n += _w
NROW = _n
SQ = ["ident", "ones_d", "ones", "blockmask", "causal", "earlier", "rot"]


class Marks:

    def __init__(self):
        self.at, self.per = {}, {}


class Steps:

    def __init__(self, sems, own_key, marks, new):
        self.sems, self.own_key, self.marks, self.new = sems, own_key, marks, new
        self.count, self.i, self.inside = {}, None, None

    def load(self, key, name=None, by=16):
        self.count[key] = self.count.get(key, 0) + by
        if name:
            self.new.at[name] = (key, self.count[key], self.inside)
        return self.sems[key], by

    def step(self, name=None):
        return self.load(self.own_key, name, 1)

    def same(self, name, other=None):
        self.new.at[name] = self.new.at[other] if other else (self.own_key, self.count[self.own_key], self.inside)

    def done(self, name, back=0):
        key, n, loop = self.marks.at.get(name, (self.own_key, 1, None))
        per, reps = self.marks.per.get((loop, key), (0, 1))
        if loop is None:
            return self.sems[key], n
        if loop == self.inside:
            assert n - per * back >= 0, (name, n, per)
            return self.sems[key], n - per * back + self.i * per
        return self.sems[key], n + per * (reps - 1)

    def last(self, *names, back=0):
        last = {}
        for name in names:
            key, n, _ = self.marks.at.get(name, (self.own_key, 1, None))
            if n >= last.get(key, (0, None))[0]:
                last[key] = n, name
        return [self.done(name, back) for _, name in last.values()]

    def own(self):
        n = self.count.get(self.own_key, 0)
        if self.inside is not None:
            n = n + self.i * self.marks.per.get((self.inside, self.own_key), (0, 1))[0]
        return self.sems[self.own_key], n

    @contextmanager
    def loop(self, eng, name, reps):
        before = dict(self.count)
        with eng.Fori(0, reps) as i:
            self.i, self.inside = i, name
            yield i
        self.i, self.inside = None, None
        for key, n in list(self.count.items()):
            per = n - before.get(key, 0)
            if per:
                self.new.per[name, key] = (per, reps)
                self.count[key] = n + per * (reps - 1)


def sem_names():
    return (["tensor_done", "scalar_done", "vector_done", "pool_done", "consts_loaded", "mask_loaded", "out_stored"]
            + [f"weights_loaded{s}" for s in range(RING)]
            + [f"{c}_loaded{h}" for c in ("ctxT", "ctxN") for h in (0, 1)])


def build(nc, marks, new, t, stages=(1, 2, 3, 4, 5, 6)):
    ctx = ExitStack()
    with ctx:
        def sb(name, shape, dt=FP32):
            return ctx.enter_context(nc.sbuf_tensor(name, shape, dt))

        X = sb("X", [P, KC, T])
        TS = [sb(f"T{k}", [P, KC, T]) for k in range(6)]
        ring = [sb(f"ring{s}", [P, KC, D]) for s in range(RING)]
        RA, RB, RC = (sb(n, [P, MT * D]) for n in ("RA", "RB", "RC"))
        n0 = HALF[0][1]
        CT = [RA[:, 0:KC * n0 * P].rearrange("p (c m) -> p c m", c=KC),
              RA[:, KC * n0 * P:KC * MP].rearrange("p (c m) -> p c m", c=KC)]
        CN = [RB[:, 0:n0 * D].rearrange("p (m d) -> p m d", d=D),
              RB[:, n0 * D:MT * D].rearrange("p (m d) -> p m d", d=D)]
        RA4 = [RA[:, k * 2048:(k + 1) * 2048].rearrange("p (c m) -> p c m", c=KC) for k in range(3)]
        RB4 = [RB[:, k * 2048:(k + 1) * 2048].rearrange("p (c m) -> p c m", c=KC) for k in range(3)]
        RC4 = [RC[:, k * 2048:(k + 1) * 2048].rearrange("p (c m) -> p c m", c=KC) for k in range(3)]
        sq = sb("sq", [P, len(SQ), P])
        C = {n: sq[:, k, :] for k, n in enumerate(SQ)}
        vec = sb("vec", [P, NVEC])
        rows = sb("rows", [P, NROW])
        gw = sb("gw", [P, 2, KC, E_])
        kconv = sb("kconv", [P, KC, S])
        RN = sb("RN", [P, B, MT])
        bsum = sb("bsum", [P, 12])
        inws = sb("inws", [P, 4])
        rstd = sb("rstd", [P, T])
        misc = sb("misc", [P, 512])
        idb = sb("idb", [P, P], BF16)
        PR = sb("PR", [P, MP])
        PTs = sb("PTs", [P, MT, P])
        maskneg = sb("maskneg", [P, MP], BF16)
        QB = sb("QB", [P, KC, P])
        PS = ctx.enter_context(nc.psum_tensor("PS", [P, 8, 512], FP32))

        def v(name, c=0):
            k = VAT[name] + c
            return vec[:, k:k + 1]

        def row(name, n):
            return rows[:, RAT[name]:RAT[name] + n]

        sems = {n: ctx.enter_context(nc.semaphore(n)) for n in sem_names()}
        block = ctx.enter_context(nc.Block())

        def bank(k, n=512):
            return PS[:, k, 0:n]

        EXPERT = ["a0", "a1", "b0", "a2", "b1", "a3", "b2", "b3"]
        order = []
        if 1 in stages:
            order += [(f"s1.{it}.{n}", AT[f"s1.{n}"]) for it in range(3) for n in S1_TILES]
        if 2 in stages:
            order += [(n, AT[n]) for n in ["s2.out"] + [f"s2.ffn{1 if x[0] == 'a' else 2}_{x[1]}" for x in EXPERT]]
        if 3 in stages:
            order += [(n, AT[n]) for n in SMALL if n.startswith("s3.")] + [("s3.moe", None)]
        for st in (4, 5):
            if st in stages:
                order += [(n, AT[n]) for n in SMALL if n.startswith(f"s{st}.")]
        if 6 in stages:
            order += [("s6.moe", None)]
        slot, before, place = {}, {}, 0
        last = [None] * RING
        for name, tile in order:
            if tile is None:
                place = -(-place // RING) * RING
                before[name] = [x for x in last if x]
                tiles = EXPERT if name == "s3.moe" else [f"{k}.{x}" for k in (0, 1) for x in EXPERT]
                for k, x in enumerate(tiles):
                    slot[f"{name}.{x}"] = k % RING
                    last[k % RING] = f"{name}.{x}"
            else:
                slot[name] = place % RING
                before[name] = last[place % RING]
                last[place % RING] = name
                place += 1

        def wt(name):
            return ring[slot[name]]

        bank_reader = {}

        def linear_pe(pe, at, tag, terms, banks, outs, after=()):
            for due in at.last(*after):
                pe.wait_ge(*due)
            for n, oc in enumerate(outs):
                k = banks[n % len(banks)]
                if bank_reader.get(k):
                    pe.wait_ge(*at.done(bank_reader[k]))
                for a, (w, x) in enumerate(terms):
                    if n == 0:
                        pe.wait_ge(*at.done(w))
                    for c in range(KC):
                        mm = pe.matmul(bank(k), wt(w)[:, c, oc * P:(oc + 1) * P], x[:, c, :],
                                          start=(a == 0 and c == 0), stop=(a == len(terms) - 1 and c == KC - 1))
                mm.then_inc(*at.step(f"{tag}.{oc}"))
                bank_reader[k] = f"{tag}.{oc}.out"
            for w, _ in terms:
                at.same(w + ".used")

        def linear_out(act, at, tag, banks, outs, op):
            for n, oc in enumerate(outs):
                act.wait_ge(*at.done(f"{tag}.{oc}"))
                op(bank(banks[n % len(banks)]), oc).then_inc(*at.step(f"{tag}.{oc}.out"))

        def norm_pe(pe, at, tag, x, after, centred=True):
            if centred:
                for due in at.last(*after):
                    pe.wait_ge(*due)
                if bank_reader.get(7):
                    pe.wait_ge(*at.done(bank_reader[7]))
                for c in range(KC):
                    mm = pe.matmul(bank(7), C["ones_d"], x[:, c, :], start=(c == 0), stop=(c == KC - 1))
                mm.then_inc(*at.step(f"{tag}.mean"))
                bank_reader[7] = f"{tag}.centred"
            pe.wait_ge(*at.done(f"{tag}.square"))
            if bank_reader.get(6):
                pe.wait_ge(*at.done(bank_reader[6]))
            for c in range(KC):
                mm = pe.matmul(bank(6), C["ones_d"], TS[5][:, c, :], start=(c == 0), stop=(c == KC - 1))
            mm.then_inc(*at.step(f"{tag}.var"))
            bank_reader[6] = f"{tag}.eps"

        def norm_act(act, at, tag, x, after=(), centred=True, xc=None):
            xc = xc if centred else x
            for due in at.last(*([f"{tag}.centred"] if centred else after)):
                act.wait_ge(*due)
            act.activation(TS[5][:, :, :], xc[:, :, :], ACT.Square).then_inc(*at.step(f"{tag}.square"))
            act.wait_ge(*at.done(f"{tag}.eps"))
            act.activation(rstd[:, :], rstd[:, :], ACT.Sqrt).then_inc(*at.step(f"{tag}.root"))

        def norm_dve(dve, at, tag, x, y, eps, w=None, b=None, centred=True, xc=None):
            if centred:
                dve.wait_ge(*at.done(f"{tag}.mean"))
                dve.tensor_tensor(xc[:, :, :], x[:, :, :], bank(7).unsqueeze(1).broadcast_to([P, KC, T]),
                                      ALU.subtract).then_inc(*at.step(f"{tag}.centred"))
            else:
                xc = x
            dve.wait_ge(*at.done(f"{tag}.var"))
            dve.tensor_scalar(rstd[:, :], bank(6), eps, None, ALU.add).then_inc(*at.step(f"{tag}.eps"))
            dve.wait_ge(*at.done(f"{tag}.root"))
            dve.reciprocal(rstd[:, :], rstd[:, :]).then_inc(*at.step())
            dve.wait_ge(*at.own())
            for c in range(KC):
                if w:
                    op = dve.scalar_tensor_tensor(out=y[:, c, :], in0=xc[:, c, :], scalar=v(w, c), in1=rstd[:, :],
                                                    op0=ALU.mult, op1=ALU.mult)
                else:
                    op = dve.tensor_tensor(y[:, c, :], xc[:, c, :], rstd[:, :], ALU.mult)
                op.then_inc(*at.step(f"{tag}.scaled"))
            if b:
                dve.wait_ge(*at.own())
                for c in range(KC):
                    dve.tensor_scalar(y[:, c, :], y[:, c, :], v(b, c), None, ALU.add).then_inc(*at.step())
            at.same(f"{tag}.done")

        SL, SN, UP, RG, ZG = TS[0], TS[1], TS[2], TS[3], TS[4]
        ss = PR[0:S, 0:MP]
        st = PTs[:, 0:7, :].rearrange("p m k -> p (m k)")
        ST = [st[:, 0:7 * S].rearrange("p (m k) -> p m k", k=S), st[:, 448:448 + 6 * S].rearrange("p (m k) -> p m k", k=S)]
        AR = [RC[:, 0:7 * S].rearrange("p (m k) -> p m k", k=S), RC[:, 448:448 + 6 * S].rearrange("p (m k) -> p m k", k=S)]
        UN = RC[0:S, 1024:1536]
        stat = [misc[:, 0:8], misc[:, 8:16]]
        ssq = misc[:, 16:16 + MT]
        rden = misc[0:S, 32:33]
        sqs = TS[5][:, 0, :]
        qb = QB[:, :, 0:S]

        def s1_pool(pool, at):
            for it in range(3):
                L = f"s1.{it}.loop"
                with at.loop(pool, L, B) as b:
                    for h in (0, 1):
                        m0, mt = HALF[h]
                        pool.wait_ge(*at.done(f"{L}.S{h}", back=1))
                        pool.nop(nofuse=True)
                        pool.dma_start(CT[h][:, :, :], t["ctxT"][b, :, :, m0 * P:(m0 + mt) * P]).then_inc(*at.load(f"ctxT_loaded{h}", f"{L}.ct{h}"))
                    for h in (0, 1):
                        m0, mt = HALF[h]
                        pool.wait_ge(*at.done(f"{L}.U", back=1))
                        pool.nop(nofuse=True)
                        pool.dma_start(CN[h][:, :, :], t["ctxN"][b, :, m0:m0 + mt, :]).then_inc(*at.load(f"ctxN_loaded{h}", f"{L}.cn{h}"))

        def s1_pe(pe, at):
            norm_pe(pe, at, "s1.ln", X, ["x"])
            for it in range(3):
                p, L = f"s1.{it}", f"s1.{it}.loop"
                norm_pe(pe, at, f"{p}.rms", SL, [], centred=False)
                linear_pe(pe, at, f"{p}.q", [(f"{p}.wq", SN)], (0, 1, 2, 3), range(KC), [f"{p}.rms.done"])
                linear_pe(pe, at, f"{p}.qk", [(f"{p}.wk", UP)], (0, 1, 2, 3), range(KC), [f"{p}.q.{c}.out" for c in range(KC)])
                with at.loop(pe, L, B) as b:
                    for h in (0, 1):
                        m0, mt = HALF[h]
                        w = mt * S
                        if h == 0:
                            pe.wait_ge(*at.done(f"{L}.qb"))
                            pe.wait_ge(*at.done(f"{p}.qk.3.out"))
                        pe.wait_ge(*at.done(f"{L}.ct{h}"))
                        pe.wait_ge(*at.done(f"{L}.S{h}.out", back=1))
                        for j in (0, 1):
                            for c in range(KC):
                                mm = pe.matmul(PS[0:S, 2 * h + j, 0:w], qb[:, c, :], CT[h][:, c, j * w:(j + 1) * w],
                                                  start=(c == 0), stop=(c == KC - 1))
                        mm.then_inc(*at.step(f"{L}.S{h}"))
                    for h in (0, 1):
                        m0, mt = HALF[h]
                        pe.wait_ge(*at.done(f"{L}.S{h}.out"))
                        pe.wait_ge(*at.done(f"{L}.st{h}", back=1))
                        pe.nop(nofuse=True)
                        for j in range(mt):
                            mm = pe.transpose(PS[:, 4 + h, j * S:(j + 1) * S], ss[:, (m0 + j) * P:(m0 + j + 1) * P],
                                                 C["ident"][0:S, 0:S])
                        mm.then_inc(*at.step(f"{L}.T{h}"))
                    pe.wait_ge(*at.done(f"{L}.ut", back=1))
                    for h in (0, 1):
                        m0, mt = HALF[h]
                        pe.wait_ge(*at.done(f"{L}.ar{h}"))
                        pe.wait_ge(*at.done(f"{L}.cn{h}"))
                        for j in range(mt):
                            m = m0 + j
                            k = P if m < MT - 1 else MLAST
                            mm = pe.matmul(PS[0:S, 7, 0:1], ST[h][0:k, j, :], C["ones"][0:k, 0:1],
                                              start=(m == 0), stop=(m == MT - 1))
                        if h:
                            mm.then_inc(*at.step(f"{L}.den"))
                        else:
                            pe.wait_ge(*at.done(f"{L}.un", back=1))
                        for j in range(mt):
                            m = m0 + j
                            mm = pe.matmul(PS[0:S, 6, :], AR[h][:, j, :], CN[h][:, j, :],
                                              start=(m == 0), stop=(m == MT - 1))
                    mm.then_inc(*at.step(f"{L}.U"))
                    pe.wait_ge(*at.done(f"{L}.un"))
                    pe.nop(nofuse=True)
                    for c in range(KC):
                        mm = pe.transpose(PS[:, 7, 128 + c * S:128 + (c + 1) * S], UN[:, c * P:(c + 1) * P],
                                             C["ident"][0:S, 0:S])
                    mm.then_inc(*at.step(f"{L}.UT"))
                bank_reader.update({k: f"{L}.S{k // 2}.out" for k in range(4)})
                bank_reader.update({4: f"{L}.st0", 5: f"{L}.st1", 6: f"{L}.un", 7: f"{L}.ut"})
                linear_pe(pe, at, f"{p}.v", [(f"{p}.wv", UP)], (0, 1, 2, 3), range(KC), [f"{p}.utw"])
                vout = [f"{p}.v.{c}.out" for c in range(KC)]
                linear_pe(pe, at, f"{p}.r", [(f"{p}.wih0", SN), (f"{p}.whh0", SL)], (0, 1, 2, 3), range(KC), vout)
                linear_pe(pe, at, f"{p}.z", [(f"{p}.wih1", SN), (f"{p}.whh1", SL)], (0, 1, 2, 3), range(KC))
                linear_pe(pe, at, f"{p}.gx", [(f"{p}.wih2", SN)], (4, 5, 6, 7), range(KC))
                linear_pe(pe, at, f"{p}.gh", [(f"{p}.whh2", SL)], (0, 1, 2, 3), range(KC))
                if it < 2:
                    pe.wait_ge(*at.done(f"{p}.sl"))

        def s1_act(act, at):
            norm_act(act, at, "s1.ln", X, xc=SN)
            for it in range(3):
                p, L = f"s1.{it}", f"s1.{it}.loop"
                norm_act(act, at, f"{p}.rms", SL, ["s1.ln.done"] if it == 0 else [f"s1.{it - 1}.sl"], centred=False)
                linear_out(act, at, f"{p}.q", (0, 1, 2, 3), range(KC), lambda ps, c: act.activation(UP[:, c, :], ps, ACT.Copy))
                if it == 0:
                    act.wait_ge(*at.done("s1.inws"))
                linear_out(act, at, f"{p}.qk", (0, 1, 2, 3), range(KC), lambda ps, c: act.activation(SN[:, c, :], ps, ACT.Copy, scale=inws[:, c:c + 1]))
                with at.loop(act, L, B) as b:
                    if it == 0:

                        for h in (0, 1):
                            m0, mt = HALF[h]
                            act.wait_ge(*at.done(f"{L}.cn{h}"))
                            for j in range(mt):
                                act.wait_ge(*at.own())
                                act.activation(sqs, CN[h][:, j, :], ACT.Square, accum_out=ssq[:, m0 + j:m0 + j + 1]).then_inc(*at.step(f"{L}.ssq"))
                        act.wait_ge(*at.done(f"{L}.msq"))
                        act.activation(ssq, ssq, ACT.Sqrt).then_inc(*at.step(f"{L}.rms"))
                    for h in (0, 1):
                        m0, mt = HALF[h]
                        w = mt * S
                        act.wait_ge(*at.done(f"{L}.S{h}"))
                        act.wait_ge(*at.done(f"{L}.T{h}", back=1))
                        act.activation(ss[:, m0 * P:(m0 + mt) * P].rearrange("p (a m) -> p a m", a=2),
                                           PS[0:S, 2 * h:2 * h + 2, 0:w], ACT.Copy).then_inc(*at.step(f"{L}.S{h}.out"))
                    for h in (0, 1):
                        act.wait_ge(*at.done(f"{L}.sub{h}"))
                        act.activation(ST[h], ST[h], ACT.Exp).then_inc(*at.step(f"{L}.exp{h}"))
                    act.wait_ge(*at.done(f"{L}.UT"))
                    act.activation(UP[:, :, bass.ds(b * S, S)],
                                       PS[:, 7, 128:128 + KC * S].rearrange("p (c k) -> p c k", c=KC), ACT.Copy).then_inc(*at.step(f"{L}.ut"))
                linear_out(act, at, f"{p}.v", (0, 1, 2, 3), range(KC), lambda ps, c: act.activation(SN[:, c, :], ps, ACT.Copy))
                for c in range(KC):
                    for due in at.last(f"{p}.r.{c}", "s1.bsum"):
                        act.wait_ge(*due)
                    act.activation(RG[:, c, :], bank(c), ACT.Sigmoid, bias=bsum[:, c:c + 1]).then_inc(*at.step(f"{p}.r.{c}.out"))
                for c in range(KC):
                    act.wait_ge(*at.done(f"{p}.z.{c}"))
                    act.activation(ZG[:, c, :], bank(c), ACT.Sigmoid, bias=bsum[:, 4 + c:5 + c]).then_inc(*at.step(f"{p}.z.{c}.out"))
                for c in range(KC):
                    act.wait_ge(*at.done(f"{p}.pre.{c}"))
                    act.activation(UP[:, c, :], UP[:, c, :], ACT.Tanh, bias=v("bih", 8 + c)).then_inc(*at.step(f"{p}.n.{c}"))

        def s1_dve(dve, at):
            dve.wait_ge(*at.done("consts"))
            dve.tensor_tensor(bsum[:, :], vec[:, VAT["bih"]:VAT["bih"] + 12], vec[:, VAT["bhh"]:VAT["bhh"] + 12], ALU.add).then_inc(*at.step("s1.bsum"))
            dve.tensor_scalar(inws[:, :], vec[:, VAT["in_w"]:VAT["in_w"] + 4], D ** -0.5, None, ALU.mult).then_inc(*at.step("s1.inws"))
            norm_dve(dve, at, "s1.ln", X, SL, 1e-5, xc=SN)
            for it in range(3):
                p, L = f"s1.{it}", f"s1.{it}.loop"
                norm_dve(dve, at, f"{p}.rms", SL, SN, 1e-6, w="slot_w", centred=False)
                for c in range(KC):
                    dve.wait_ge(*at.done(f"{p}.qk.{c}.out"))
                with at.loop(dve, L, B) as b:
                    dve.wait_ge(*at.done(f"{L}.S1", back=1))
                    dve.tensor_copy(qb, SN[:, :, bass.ds(b * S, S)]).then_inc(*at.step(f"{L}.qb"))
                    rn = RN[:, b, :]
                    if it == 0:
                        dve.wait_ge(*at.done(f"{L}.ssq"))
                        dve.tensor_scalar(ssq, ssq, 1.0 / D, 1e-6, ALU.mult, ALU.add).then_inc(*at.step(f"{L}.msq"))
                        dve.wait_ge(*at.done(f"{L}.rms"))
                        dve.reciprocal(rn, ssq).then_inc(*at.step(f"{L}.rinv"))
                        dve.wait_ge(*at.own())
                    for h in (0, 1):
                        m0, mt = HALF[h]
                        r = rn[:, m0:m0 + mt].unsqueeze(2).broadcast_to([P, mt, S])
                        mx, sm = stat[h][:, 0:mt], misc[:, 40 + 8 * h:40 + 8 * h + mt]
                        bc = lambda a: a.unsqueeze(2).broadcast_to([P, mt, S])
                        dve.wait_ge(*at.done(f"{L}.T{h}"))
                        dve.wait_ge(*at.done(f"{L}.U", back=1))
                        dve.tensor_tensor(ST[h], PS[:, 4 + h, 0:mt * S].rearrange("p (m k) -> p m k", k=S), r, ALU.mult).then_inc(*at.step(f"{L}.st{h}"))
                        dve.wait_ge(*at.own())
                        dve.tensor_reduce(mx, ST[h], AX.X, ALU.max).then_inc(*at.step())
                        dve.wait_ge(*at.own())
                        dve.tensor_tensor(ST[h], ST[h], bc(mx), ALU.subtract).then_inc(*at.step(f"{L}.sub{h}"))
                    for h in (0, 1):
                        m0, mt = HALF[h]
                        r = rn[:, m0:m0 + mt].unsqueeze(2).broadcast_to([P, mt, S])
                        sm = misc[:, 40 + 8 * h:40 + 8 * h + mt]
                        bc = lambda a: a.unsqueeze(2).broadcast_to([P, mt, S])
                        dve.wait_ge(*at.done(f"{L}.exp{h}"))
                        dve.tensor_reduce(sm, ST[h], AX.X, ALU.add).then_inc(*at.step())
                        dve.wait_ge(*at.own())
                        dve.reciprocal(sm, sm).then_inc(*at.step())
                        dve.wait_ge(*at.own())
                        dve.tensor_tensor(ST[h], ST[h], bc(sm), ALU.mult).then_inc(*at.step())
                        dve.wait_ge(*at.own())
                        dve.tensor_tensor(AR[h], ST[h], r, ALU.mult).then_inc(*at.step(f"{L}.ar{h}"))
                    dve.wait_ge(*at.done(f"{L}.den"))
                    dve.tensor_scalar(rden, PS[0:S, 7, 0:1], 1e-6, None, ALU.add).then_inc(*at.step())
                    dve.wait_ge(*at.own())
                    dve.reciprocal(rden, rden).then_inc(*at.step())
                    dve.wait_ge(*at.own())
                    dve.wait_ge(*at.done(f"{L}.U"))
                    dve.wait_ge(*at.done(f"{L}.UT", back=1))
                    dve.tensor_scalar(UN, PS[0:S, 6, :], rden, None, ALU.mult).then_inc(*at.step(f"{L}.un"))
                dve.wait_ge(*at.done(f"{L}.ut"))
                for c in range(KC):
                    dve.tensor_scalar(UP[:, c, :], UP[:, c, :], v("in_w", c), None, ALU.mult).then_inc(*at.step(f"{p}.utw"))
                for c in range(KC):
                    for due in at.last(f"{p}.gh.{c}", f"{p}.r.{c}.out"):
                        dve.wait_ge(*due)
                    dve.scalar_tensor_tensor(out=UP[:, c, :], in0=bank(c), scalar=v("bhh", 8 + c), in1=RG[:, c, :],
                                                 op0=ALU.add, op1=ALU.mult).then_inc(*at.step(f"{p}.gh.{c}.out"))
                    dve.wait_ge(*at.own())
                    dve.wait_ge(*at.done(f"{p}.gx.{c}"))
                    dve.tensor_tensor(UP[:, c, :], UP[:, c, :], bank(4 + c), ALU.add).then_inc(*at.step(f"{p}.pre.{c}"))
                    at.same(f"{p}.gx.{c}.out", f"{p}.pre.{c}")
                for c in range(KC):
                    for due in at.last(f"{p}.n.{c}", f"{p}.z.{c}.out", f"{p}.gh.3"):
                        dve.wait_ge(*due)
                    dve.tensor_tensor(SL[:, c, :], SL[:, c, :], UP[:, c, :], ALU.subtract).then_inc(*at.step())
                    dve.wait_ge(*at.own())
                    dve.tensor_tensor(SL[:, c, :], SL[:, c, :], ZG[:, c, :], ALU.mult).then_inc(*at.step())
                    dve.wait_ge(*at.own())
                    dve.tensor_tensor(SL[:, c, :], SL[:, c, :], UP[:, c, :], ALU.add).then_inc(*at.step(f"{p}.sl"))
            dve.wait_ge(*at.own())
            dve.tensor_tensor(X[:, :, :], X[:, :, :], SL[:, :, :], ALU.add).then_inc(*at.step("x1"))

        HB = [RB4[0], RB4[1]]

        def expert_pe(pe, at, tag, w, x, inloop):
            def hidden(s):
                pe.wait_ge(*at.done(w("a", s)))
                for oc in range(KC):
                    if s:
                        pe.wait_ge(*at.done(f"{tag}.h{s - 1}.{oc}.out"))
                    elif inloop:
                        pe.wait_ge(*at.done(f"{tag}.h3.{oc}.out", back=1))
                    for c in range(KC):
                        mm = pe.matmul(bank(oc), wt(w("a", s))[:, c, oc * P:(oc + 1) * P], x[:, c, :],
                                          start=(c == 0), stop=(c == KC - 1))
                    mm.then_inc(*at.step(f"{tag}.h{s}.{oc}"))
                at.same(w("a", s) + ".used", f"{tag}.h{s}.3")

            def output(s):
                pe.wait_ge(*at.done(w("b", s)))
                for oc in range(KC):
                    if s == 0 and inloop:
                        pe.wait_ge(*at.done(f"{tag}.y{oc}.out", back=1))
                    for c in range(KC):
                        for due in at.last(*([f"{tag}.h{s}.{c}.out"] if oc == 0 else [])):
                            pe.wait_ge(*due)
                        mm = pe.matmul(bank(4 + oc), wt(w("b", s))[:, c, oc * P:(oc + 1) * P], HB[s % 2][:, c, :],
                                          start=(s == 0 and c == 0), stop=(s == FS - 1 and c == KC - 1))
                    if s == FS - 1:
                        mm.then_inc(*at.step(f"{tag}.y{oc}"))
                if s < FS - 1:
                    mm.then_inc(*at.step(f"{tag}.Y{s}"))
                else:
                    at.same(f"{tag}.Y{s}", f"{tag}.y3")
                at.same(w("b", s) + ".used", f"{tag}.Y{s}")

            hidden(0)
            for s in range(FS):
                if s + 1 < FS:
                    hidden(s + 1)
                output(s)

        def expert_act(act, at, tag, func, bias, inloop):
            for s in range(FS):
                if s >= 2:
                    act.wait_ge(*at.done(f"{tag}.Y{s - 2}"))
                elif inloop:
                    act.wait_ge(*at.done(f"{tag}.Y{s + 2}", back=1))
                for oc in range(KC):
                    act.wait_ge(*at.done(f"{tag}.h{s}.{oc}"))
                    act.activation(HB[s % 2][:, oc, :], bank(oc), func, bias=bias(4 * s + oc)).then_inc(*at.step(f"{tag}.h{s}.{oc}.out"))

        pw = RC[:, 2560:2560 + S * KC * N_STATE].rearrange("p (j c n) -> p j c n", j=S, c=KC)
        abc = RC[:, 1600:1792].rearrange("p (a c n) -> p a c n", a=3, c=KC)
        R2, N2, Y2 = TS[0], TS[1], TS[2]

        def s2_pool(pool, at):
            pool.wait_ge(*at.done("s2.decay"))
            pool.tensor_tensor(pw[:, 0], abc[:, 1], abc[:, 2], ALU.mult).then_inc(*at.step())
            for j in range(1, S):
                pool.wait_ge(*at.own())
                pool.tensor_tensor(pw[:, j], pw[:, j - 1], abc[:, 0], ALU.mult).then_inc(*at.step("s2.powers"))

        def s2_pe(pe, at):
            norm_pe(pe, at, "s2.ln", X, ["x1"] if 1 in stages else ["x"])
            norm_pe(pe, at, "s2.ln1", R2, ["s2.ln.done"])
            linear_pe(pe, at, "s2.out", [("s2.out", Y2)], (0, 1, 2, 3), range(KC), ["s2.silu"])
            norm_pe(pe, at, "s2.ln2", R2, ["s2.res"])
            for due in at.last("s2.ln2.done", *(f"s2.out.{c}.out" for c in range(KC))):
                pe.wait_ge(*due)
            expert_pe(pe, at, "s2.ffn", lambda ab, s: f"s2.ffn{1 if ab == 'a' else 2}_{s}", N2, False)
            bank_reader.update({k: f"s2.ffn.h3.{k}.out" for k in range(4)})
            bank_reader.update({4 + k: f"s2.ffn.y{k}.out" for k in range(4)})

        def s2_act(act, at):
            for due in at.last("abc", "s1.bsum" if 1 in stages else "consts"):
                act.wait_ge(*due)
            if 1 in stages:
                act.wait_ge(*at.done("x1"))
            act.activation(abc[:, 0], abc[:, 0], ACT.Sigmoid).then_inc(*at.step("s2.decay"))
            norm_act(act, at, "s2.ln", X, xc=N2)
            norm_act(act, at, "s2.ln1", R2, xc=N2)
            act.wait_ge(*at.done("s2.conv"))
            act.activation(Y2[:, :, :], Y2[:, :, :], ACT.Silu).then_inc(*at.step("s2.silu"))
            norm_act(act, at, "s2.ln2", R2, xc=N2)
            expert_act(act, at, "s2.ffn", ACT.Gelu, lambda k: v("ffn1_b", k), False)

        def s2_dve(dve, at):
            norm_dve(dve, at, "s2.ln", X, R2, 1e-5, xc=N2)
            dve.wait_ge(*at.own())
            norm_dve(dve, at, "s2.ln1", R2, N2, 1e-5, w="ln_w", b="ln_b", xc=N2)
            dve.wait_ge(*at.done("s2.powers"))
            dve.tensor_reduce(kconv[:, :, :].rearrange("p c j -> p j c"), pw, AX.X, ALU.add).then_inc(*at.step())
            dve.wait_ge(*at.own())
            dve.tensor_tensor(kconv[:, :, 0:1], kconv[:, :, 0:1], vec[:, VAT["D"]:VAT["D"] + 4].unsqueeze(2), ALU.add).then_inc(*at.step())
            dve.wait_ge(*at.own())
            xn, y = (a[:, :, :].rearrange("p c (b s) -> p c b s", b=B) for a in (N2, Y2))
            for c in range(KC):
                dve.tensor_scalar(Y2[:, c, :], N2[:, c, :], kconv[:, c, 0:1], None, ALU.mult).then_inc(*at.step("s2.conv"))
            for j in range(1, S):
                for c in range(KC):
                    dve.wait_ge(sems["vector_done"], at.count["vector_done"] - KC + 1)
                    dve.scalar_tensor_tensor(out=y[:, c, :, j:S], in0=xn[:, c, :, 0:S - j], scalar=kconv[:, c, j:j + 1],
                                                 in1=y[:, c, :, j:S], op0=ALU.mult, op1=ALU.add).then_inc(*at.step("s2.conv"))
            for c in range(KC):
                dve.wait_ge(*at.done(f"s2.out.{c}"))
                dve.scalar_tensor_tensor(out=R2[:, c, :], in0=bank(c), scalar=v("out_b", c), in1=R2[:, c, :],
                                             op0=ALU.add, op1=ALU.add).then_inc(*at.step(f"s2.out.{c}.out"))
            at.same("s2.res", "s2.out.3.out")
            dve.wait_ge(*at.own())
            norm_dve(dve, at, "s2.ln2", R2, N2, 1e-5, w="ln2_w", b="ln2_b", xc=N2)
            for c in range(KC):
                dve.tensor_tensor(X[:, c, :], X[:, c, :], R2[:, c, :], ALU.add).then_inc(*at.step())
            for c in range(KC):
                dve.wait_ge(*at.done(f"s2.ffn.y{c}"))
                dve.wait_ge(*at.own())
                dve.scalar_tensor_tensor(out=X[:, c, :], in0=bank(4 + c), scalar=v("ffn2_b", c), in1=X[:, c, :],
                                             op0=ALU.add, op1=ALU.add).then_inc(*at.step(f"s2.ffn.y{c}.out"))
            at.same("x2", "s2.ffn.y3.out")

        KBD = [RB4[0], RB4[1]]
        SC, PT = RC4[0], RC4[1]
        probs = SC.rearrange("p c (h k) -> p (c h) k", k=P)
        probsT = PT.rearrange("p c (h k) -> p (c h) k", k=P)
        NBP = T // P

        def attn_pool(pool, at, tag, K, ready):
            for x in KBD:
                pool.memset(x[:, :, :], 0.0).then_inc(*at.step(f"{tag}.zero"))
            pool.wait_ge(*at.own())
            for due in at.last(*ready):
                pool.wait_ge(*due)
            for bp in range(NBP):
                if bp >= 2:
                    pool.wait_ge(*at.done(f"{tag}.S{bp - 2}"))
                for a in range(G):
                    pool.tensor_copy(KBD[bp % 2][a * HD:(a + 1) * HD, :, a * P:(a + 1) * P],
                                        K[a * HD:(a + 1) * HD, :, bp * P:(bp + 1) * P]).then_inc(*at.step(f"{tag}.kb{bp}"))

        def attn_pe(pe, at, tag, Q, V, ready):
            def scores(bp):
                pe.wait_ge(*at.done(f"{tag}.kb{bp}"))
                for g in range(KC):
                    if bp:
                        pe.wait_ge(*at.done(f"{tag}.masked{bp - 1}"))
                    elif bank_reader.get(g):
                        pe.wait_ge(*at.done(bank_reader[g]))
                    mm = pe.matmul(bank(g), Q[:, g, bp * P:(bp + 1) * P], KBD[bp % 2][:, g, :], start=True, stop=True)
                mm.then_inc(*at.step(f"{tag}.S{bp}"))

            def values(bp):
                pe.wait_ge(*at.done(f"{tag}.p{bp}"))
                for g in range(KC):
                    k = 4 + g % 3
                    if bank_reader.get(k):
                        pe.wait_ge(*at.done(bank_reader[k]))
                    for a in range(G):
                        mm = pe.transpose(PS[:, k, a * P:(a + 1) * P], probs[:, G * g + a, :], C["ident"])
                    mm.then_inc(*at.step(f"{tag}.T{bp}.{g}"))
                    bank_reader[k] = f"{tag}.T{bp}.{g}.out"
                if bank_reader.get(7):
                    pe.wait_ge(*at.done(bank_reader[7]))
                for g in range(KC):
                    pe.wait_ge(*at.done(f"{tag}.T{bp}.{g}.out"))
                    for a in range(G):
                        h = G * g + a
                        mm = pe.matmul(PS[a * HD:(a + 1) * HD, 7, g * P:(g + 1) * P], V[:, bp, h * HD:(h + 1) * HD],
                                          probsT[:, h, :], start=True, stop=True)
                mm.then_inc(*at.step(f"{tag}.O{bp}"))
                bank_reader[7] = f"{tag}.O{bp}.out"

            for due in at.last(*ready):
                pe.wait_ge(*due)
            scores(0)
            for bp in range(NBP):
                if bp + 1 < NBP:
                    scores(bp + 1)
                values(bp)
            for g in range(KC):
                bank_reader[g] = f"{tag}.masked{NBP - 1}"

        def attn_act(act, at, tag):
            for bp in range(NBP):
                act.wait_ge(*at.done(f"{tag}.sub{bp}"))
                act.activation(SC[:, :, :], SC[:, :, :], ACT.Exp).then_inc(*at.step(f"{tag}.exp{bp}"))
                for g in range(KC):
                    act.wait_ge(*at.done(f"{tag}.T{bp}.{g}"))
                    if bp:
                        act.wait_ge(*at.done(f"{tag}.O{bp - 1}"))
                    act.activation(PT[:, g, :], bank(4 + g % 3), ACT.Copy).then_inc(*at.step(f"{tag}.T{bp}.{g}.out"))

        def attn_dve(dve, at, tag, O, mask):
            mx, sm = misc[:, 0:H], misc[:, 16:16 + H]
            for bp in range(NBP):
                dve.wait_ge(*at.done(f"{tag}.S{bp}"))
                if bp:
                    dve.wait_ge(*at.done(f"{tag}.T{bp - 1}.3"))
                dve.scalar_tensor_tensor(out=probs, in0=PS[:, 0:4, :].rearrange("p g (a k) -> p (g a) k", k=P),
                                             scalar=HD ** -0.5, in1=mask.unsqueeze(1).broadcast_to([P, H, P]),
                                             op0=ALU.mult, op1=ALU.add).then_inc(*at.step(f"{tag}.masked{bp}"))
                dve.wait_ge(*at.own())
                dve.tensor_reduce(mx, probs, AX.X, ALU.max).then_inc(*at.step())
                dve.wait_ge(*at.own())
                dve.tensor_tensor(probs, probs, mx.unsqueeze(2).broadcast_to([P, H, P]), ALU.subtract).then_inc(*at.step(f"{tag}.sub{bp}"))
                dve.wait_ge(*at.done(f"{tag}.exp{bp}"))
                dve.tensor_reduce(sm, probs, AX.X, ALU.add).then_inc(*at.step())
                dve.wait_ge(*at.own())
                dve.reciprocal(sm, sm).then_inc(*at.step())
                dve.wait_ge(*at.own())
                dve.tensor_tensor(probs, probs, sm.unsqueeze(2).broadcast_to([P, H, P]), ALU.mult).then_inc(*at.step(f"{tag}.p{bp}"))
                dve.wait_ge(*at.done(f"{tag}.O{bp}"))
                dve.tensor_copy(O[:, :, bp * P:(bp + 1) * P], PS[:, 7, :].rearrange("p (g k) -> p g k", k=P)).then_inc(*at.step(f"{tag}.O{bp}.out"))

        def values_pe(pe, at, tag, w, x, banks):
            for tt in range(T // P):
                k = banks[tt % len(banks)]
                if bank_reader.get(k):
                    pe.wait_ge(*at.done(bank_reader[k]))
                if tt == 0:
                    pe.wait_ge(*at.done(w))
                for c in range(KC):
                    mm = pe.matmul(bank(k), x[:, c, tt * P:(tt + 1) * P], wt(w)[:, c, :], start=(c == 0), stop=(c == KC - 1))
                mm.then_inc(*at.step(f"{tag}.{tt}"))
                bank_reader[k] = f"{tag}.{tt}.out"
            at.same(w + ".used", f"{tag}.3")

        def values_dve(dve, at, tag, V, bias, banks):
            for tt in range(T // P):
                dve.wait_ge(*at.done(f"{tag}.{tt}"))
                dve.tensor_tensor(V[:, tt, :], bank(banks[tt % len(banks)]), row(bias, D), ALU.add).then_inc(*at.step(f"{tag}.{tt}.out"))

        XPAD = RC[:, 4200:4200 + KC * B * (S + 2)].rearrange("p (c b s) -> p c b s", c=KC, b=B)
        X3, Q3, K3, V3, O3 = TS[1], TS[2], TS[3], TS[4], TS[0]
        PB = RA[:, 0:E_ * T].rearrange("p (e t) -> p e t", e=E_)
        gl = misc[:, 64:96].rearrange("p (a e) -> p a e", e=E_)
        gm, gs = misc[:, 96:100], misc[:, 100:104]
        gT = misc[0:E_, 0:0 + 512]
        ga = RC[:, 0:32].rearrange("p (a e) -> p a e", e=E_)
        gst = RC[:, 64:128]

        def gate_pe(pe, at, tag, x, w, after):
            for due in at.last(*after):
                pe.wait_ge(*due)
            if bank_reader.get(0):
                pe.wait_ge(*at.done(bank_reader[0]))
            for tt in range(T // P):
                for c in range(KC):
                    mm = pe.matmul(PS[:, 0, tt * E_:(tt + 1) * E_], x[:, c, tt * P:(tt + 1) * P], gw[:, w, c, :],
                                      start=(c == 0), stop=(c == KC - 1))
            mm.then_inc(*at.step(f"{tag}.logits"))
            bank_reader[0] = f"{tag}.logits.out"

        def gate_act(act, at, tag):
            act.wait_ge(*at.done(f"{tag}.sub"))
            act.activation(ga, ga, ACT.Exp).then_inc(*at.step(f"{tag}.exp"))

        def gate_dve(dve, at, tag, bias):
            ps = PS[:, 0, 0:32].rearrange("p (a e) -> p a e", e=E_)
            bc = lambda a: a.unsqueeze(2).broadcast_to([P, 4, E_])
            dve.wait_ge(*at.done(f"{tag}.logits"))
            if bias:
                dve.tensor_tensor(ga, ps, row("gate_b", E_).unsqueeze(1).broadcast_to([P, 4, E_]), ALU.add).then_inc(*at.step(f"{tag}.logits.out"))
            else:
                dve.tensor_copy(ga, ps).then_inc(*at.step(f"{tag}.logits.out"))
            dve.wait_ge(*at.own())
            dve.tensor_reduce(gst[:, 0:4], ga, AX.X, ALU.max).then_inc(*at.step())
            dve.wait_ge(*at.own())
            dve.tensor_tensor(ga, ga, bc(gst[:, 0:4]), ALU.subtract).then_inc(*at.step(f"{tag}.sub"))
            dve.wait_ge(*at.done(f"{tag}.exp"))
            dve.tensor_reduce(gst[:, 4:8], ga, AX.X, ALU.add).then_inc(*at.step())
            dve.wait_ge(*at.own())
            dve.reciprocal(gst[:, 4:8], gst[:, 4:8]).then_inc(*at.step())
            dve.wait_ge(*at.own())
            dve.tensor_tensor(ga, ga, bc(gst[:, 4:8]), ALU.mult).then_inc(*at.step(f"{tag}.probs"))

        def s3_pool(pool, at):
            if 2 in stages:
                pool.wait_ge(*at.done("s2.conv"))
            pool.memset(XPAD[:, :, :, 0:1], 0.0).then_inc(*at.step())
            pool.memset(XPAD[:, :, :, S + 1:S + 2], 0.0).then_inc(*at.step("s3.pad"))
            if 2 in stages:
                pool.wait_ge(*at.done("x2"))
            attn_pool(pool, at, "s3.at", K3, [f"s3.k.{c}.out" for c in range(KC)])

        def s3_pe(pe, at):
            norm_pe(pe, at, "s3.ln", X, ["x2"] if 2 in stages else ["x"])
            for due in at.last("s3.padded", "s3.pad"):
                pe.wait_ge(*due)
            for oc in range(KC):
                if bank_reader.get(oc):
                    pe.wait_ge(*at.done(bank_reader[oc]))
                for k in range(3):
                    if oc == 0:
                        pe.wait_ge(*at.done(f"s3.conv{k}"))
                    for c in range(KC):
                        mm = pe.matmul(bank(oc), wt(f"s3.conv{k}")[:, c, oc * P:(oc + 1) * P], XPAD[:, c, :, k:k + S],
                                          start=(k == 0 and c == 0), stop=(k == 2 and c == KC - 1))
                mm.then_inc(*at.step(f"s3.cv.{oc}"))
                bank_reader[oc] = f"s3.cv.{oc}.out"
            for k in range(3):
                at.same(f"s3.conv{k}.used", "s3.cv.3")
            cv = [f"s3.cv.{c}.out" for c in range(KC)]
            linear_pe(pe, at, "s3.q", [("s3.wq", X3)], (4, 5, 6, 7), range(KC), cv)
            linear_pe(pe, at, "s3.k", [("s3.wk", X3)], (0, 1, 2, 3), range(KC))
            values_pe(pe, at, "s3.v", "s3.wv", X3, (4, 5, 6, 7))
            attn_pe(pe, at, "s3.at", Q3, V3, [f"s3.q.{c}.out" for c in range(KC)] + [f"s3.v.{c}.out" for c in range(4)])
            linear_pe(pe, at, "s3.o", [("s3.wo", O3)], (0, 1, 2, 3), range(KC), ["s3.at.O3.out"])
            norm_pe(pe, at, "s3.ln1", X3, [f"s3.o.{c}.out" for c in range(KC)])
            gate_pe(pe, at, "s3.g", X3, 0, ["s3.ln1.done"])
            pe.wait_ge(*at.done("s3.g.probs"))
            for tt in range(4):
                mm = pe.transpose(PS[0:E_, 1, tt * P:(tt + 1) * P], ga[:, tt, :], C["ident"])
            mm.then_inc(*at.step("s3.gT"))
            pe.wait_ge(*at.done("s3.gT.out"))
            for x in range(E_):
                k = 2 + x % 2
                if x >= 2:
                    pe.wait_ge(*at.done(f"s3.pb.{x - 2}.out"))
                mm = pe.matmul(bank(k), C["ident"][0:E_, x:x + 1].broadcast_to([E_, P]), gT, start=True, stop=True)
                mm.then_inc(*at.step(f"s3.pb.{x}"))
            for due in at.last("s3.pb.6.out", "s3.pb.7.out", "s3.acc0"):
                pe.wait_ge(*due)
            with at.loop(pe, "s3.loop", E_) as i:
                expert_pe(pe, at, "s3.moe", lambda ab, s: f"s3.moe.{ab}{s}", X3, True)
            bank_reader.update({k: f"s3.moe.h3.{k}.out" for k in range(4)})
            bank_reader.update({4 + k: f"s3.moe.y{k}.out" for k in range(4)})
            norm_pe(pe, at, "s3.ln2", X3, ["s3.x5"])

        def s3_act(act, at):
            norm_act(act, at, "s3.ln", X, xc=TS[0])
            linear_out(act, at, "s3.cv", (0, 1, 2, 3), range(KC), lambda ps, c: act.activation(X3[:, c, :], ps, ACT.Identity, bias=v("conv_b", c)))
            linear_out(act, at, "s3.q", (4, 5, 6, 7), range(KC), lambda ps, c: act.activation(Q3[:, c, :], ps, ACT.Identity, bias=v("bqkv", c)))
            linear_out(act, at, "s3.k", (0, 1, 2, 3), range(KC), lambda ps, c: act.activation(K3[:, c, :], ps, ACT.Identity, bias=v("bqkv", 4 + c)))
            attn_act(act, at, "s3.at")
            norm_act(act, at, "s3.ln1", X3, xc=X3)
            gate_act(act, at, "s3.g")
            act.wait_ge(*at.done("s3.gT"))
            act.activation(gT, PS[0:E_, 1, :], ACT.Copy).then_inc(*at.step("s3.gT.out"))
            for x in range(E_):
                act.wait_ge(*at.done(f"s3.pb.{x}"))
                act.activation(PB[:, x, :], bank(2 + x % 2), ACT.Copy).then_inc(*at.step(f"s3.pb.{x}.out"))
            with at.loop(act, "s3.loop", E_) as i:
                expert_act(act, at, "s3.moe", ACT.Relu, lambda k: vec[:, bass.ds(i * 16 + (VAT["b1"] + k), 1)], True)
            norm_act(act, at, "s3.ln2", X3, xc=X3)

        def s3_dve(dve, at):
            norm_dve(dve, at, "s3.ln", X, TS[0], 1e-5, xc=TS[0])
            dve.wait_ge(*at.own())
            dve.tensor_copy(XPAD[:, :, :, 1:S + 1].rearrange("p c b s -> p (c b) s"),
                                TS[0][:, :, :].rearrange("p c (b s) -> p (c b) s", s=S)).then_inc(*at.step("s3.padded"))
            values_dve(dve, at, "s3.v", V3, "bv3", (4, 5, 6, 7))
            attn_dve(dve, at, "s3.at", O3, C["blockmask"])
            for c in range(KC):
                dve.wait_ge(*at.done(f"s3.o.{c}"))
                dve.scalar_tensor_tensor(out=X3[:, c, :], in0=bank(c), scalar=v("bo3", c), in1=X3[:, c, :],
                                             op0=ALU.add, op1=ALU.add).then_inc(*at.step(f"s3.o.{c}.out"))
            dve.wait_ge(*at.own())
            norm_dve(dve, at, "s3.ln1", X3, X3, 1e-5, w="ln1_g", b="ln1_b", xc=X3)
            gate_dve(dve, at, "s3.g", True)
            acc, tmp = TS[2], TS[3]
            dve.memset(acc[:, :, :], 0.0).then_inc(*at.step("s3.acc0"))
            dve.wait_ge(*at.done("s3.pb.7.out"))
            with at.loop(dve, "s3.loop", E_) as i:
                for c in range(KC):
                    dve.wait_ge(*at.done(f"s3.moe.y{c}"))
                    dve.wait_ge(*at.own())
                    dve.scalar_tensor_tensor(out=tmp[:, c, :], in0=bank(4 + c), scalar=vec[:, bass.ds(i * 4 + (VAT["b2"] + c), 1)],
                                                 in1=PB[:, i, :], op0=ALU.add, op1=ALU.mult).then_inc(*at.step(f"s3.moe.y{c}.out"))
                    dve.wait_ge(*at.own())
                    dve.tensor_tensor(acc[:, c, :], acc[:, c, :], tmp[:, c, :], ALU.add).then_inc(*at.step())
            dve.wait_ge(*at.own())
            dve.wait_ge(*at.done("s3.moe.y3"))
            dve.tensor_tensor(X3[:, :, :], X3[:, :, :], acc[:, :, :], ALU.add).then_inc(*at.step("s3.x5"))
            dve.wait_ge(*at.own())
            norm_dve(dve, at, "s3.ln2", X3, acc, 1e-5, w="ln2_g", b="ln2b3", xc=X3)
            dve.wait_ge(*at.own())
            dve.tensor_tensor(X[:, :, :], X[:, :, :], acc[:, :, :], ALU.add).then_inc(*at.step("x3"))

        KT = RC[:, 0:KC * MP].rearrange("p (g m) -> p g m", g=KC)
        VT = RB[:, 0:MT * D].rearrange("p (m d) -> p m d", d=D)
        N4, Q4, O4 = TS[0], TS[1], TS[3]
        qd = TS[2][:, 0:2, :].rearrange("p a b -> p (a b)").rearrange("p (g h q) -> p g h q", g=KC, h=G)
        QD = TS[2][:, 0:2, :].rearrange("p a b -> p (a b)").rearrange("p (g r) -> p g r", g=KC)
        keep, flag = PTs[:, :, :].rearrange("p m k -> p (m k)"), misc[:, 0:1]
        NP = H // 2
        TG = [(k, min(4, MT - k)) for k in range(0, MT, 4)]
        SCALE = HD ** -0.5

        def s4_pool(pool, at):
            if 3 in stages:
                pool.wait_ge(*at.done("s3.x5"))
            with at.loop(pool, "s4.loop", B) as b:
                for h in (0, 1):
                    m0, mt = HALF[h]
                    pool.wait_ge(*at.done(f"s4.V{h}", back=1))
                    pool.nop(nofuse=True)
                    pool.dma_start(CT[h][:, :, :], t["ctxT"][b, :, :, m0 * P:(m0 + mt) * P]).then_inc(*at.load(f"ctxT_loaded{h}", f"s4.ct{h}"))

        def s4_pe(pe, at):
            norm_pe(pe, at, "s4.ln", X, ["x3"] if 3 in stages else ["x"])
            linear_pe(pe, at, "s4.q", [("s4.wq", N4)], (0, 1, 2, 3), range(KC), ["s4.ln.done"])
            for due in at.last("s4.wk", "s4.wv", *(f"s4.q.{c}.out" for c in range(KC))):
                pe.wait_ge(*due)

            def keys_values(h):
                m0, mt = HALF[h]
                w = mt * S
                pe.wait_ge(*at.done(f"s4.ct{h}"))
                for oc in range(KC):
                    for j in (0, 1):
                        n = 2 * oc + j
                        if n >= 4:
                            pe.wait_ge(*at.done(f"s4.K{h}.{n - 4}.out"))
                        elif h:
                            pe.wait_ge(*at.done(f"s4.K0.{n + 4}.out"))
                        else:
                            pe.wait_ge(*at.done("s4.exp7", back=1))
                        for c in range(KC):
                            mm = pe.matmul(bank(n % 4, w), wt("s4.wk")[:, c, oc * P:(oc + 1) * P],
                                              CT[h][:, c, j * w:(j + 1) * w], start=(c == 0), stop=(c == KC - 1))
                        mm.then_inc(*at.step(f"s4.K{h}.{n}"))
                for j in range(mt):
                    if j >= 2:
                        pe.wait_ge(*at.done(f"s4.V{h}.{j - 2}.out"))
                    elif h:
                        pe.wait_ge(*at.done(f"s4.V0.{HALF[0][1] - 2 + j}.out"))
                    else:
                        for due in at.last("s4.pt7.2.out", "s4.pt7.3.out", back=1):
                            pe.wait_ge(*due)
                    for c in range(KC):
                        mm = pe.matmul(bank(4 + (m0 + j) % 2), CT[h][:, c, j * P:(j + 1) * P], wt("s4.wv")[:, c, :],
                                          start=(c == 0), stop=(c == KC - 1))
                    mm.then_inc(*at.step(f"s4.V{h}.{j}"))
                at.same(f"s4.V{h}", f"s4.V{h}.{mt - 1}")

            def scores(p):
                g, a = p // 2, p % 2
                if p:
                    pe.wait_ge(*at.done(f"s4.exp{p - 1}"))
                else:
                    for due in at.last(*(f"s4.K{h}.{n}.out" for n in range(8) for h in (0, 1))):
                        pe.wait_ge(*due)
                    pe.wait_ge(*at.done("s4.qd"))
                for j in range(4):
                    pe.matmul(bank(j, MB), QD[:, g, a * P:(a + 1) * P], KT[:, g, j * MB:(j + 1) * MB], start=True, stop=False)
                    mm = pe.matmul(bank(j, MB), idb[:, :], maskneg[:, j * MB:(j + 1) * MB], start=False, stop=True)
                mm.then_inc(*at.step(f"s4.S{p}"))

            def values(p):
                pe.wait_ge(*at.done(f"s4.p{p}"))
                for k, (m0, n) in enumerate(TG):
                    if k >= 2:
                        pe.wait_ge(*at.done(f"s4.pt{p}.{k - 2}.out"))
                    elif p:
                        pe.wait_ge(*at.done(f"s4.pt{p - 1}.{k + 2}.out"))
                    else:
                        for j in range(HALF[1][1] - 2, HALF[1][1]):
                            pe.wait_ge(*at.done(f"s4.V1.{j}.out"))
                    for j in range(n):
                        mm = pe.transpose(PS[:, 4 + k % 2, j * P:(j + 1) * P], PR[:, (m0 + j) * P:(m0 + j + 1) * P], C["ident"])
                    mm.then_inc(*at.step(f"s4.pt{p}.{k}"))
                a = p % 2
                if p >= 2:
                    pe.wait_ge(*at.done(f"s4.o{p - 2}.out"))
                else:
                    pe.wait_ge(*at.done(f"s4.o{p + 6}.out", back=1))
                for k, (m0, n) in enumerate(TG):
                    pe.wait_ge(*at.done(f"s4.pt{p}.{k}.out"))
                    for m in range(m0, m0 + n):
                        mm = pe.matmul(PS[a * 64:a * 64 + 64, 6 + a, 0:P], VT[:, m, p * 64:(p + 1) * 64], PTs[:, m, :],
                                          start=(m == 0), stop=(m == MT - 1))
                mm.then_inc(*at.step(f"s4.o{p}"))

            with at.loop(pe, "s4.loop", B) as b:
                keys_values(0)
                keys_values(1)
                scores(0)
                for p in range(NP):
                    if p + 1 < NP:
                        scores(p + 1)
                    values(p)
            at.same("s4.wk.used", "s4.o7"); at.same("s4.wv.used", "s4.o7")
            bank_reader.update({k: "s4.exp7" for k in range(4)})
            bank_reader.update({4: "s4.pt7.2.out", 5: "s4.pt7.3.out", 6: "s4.o6.out", 7: "s4.o7.out"})
            linear_pe(pe, at, "s4.wo_", [("s4.wo", O4)], (0, 1, 2, 3), range(KC), ["s4.o7.out"])

        def s4_act(act, at):
            norm_act(act, at, "s4.ln", X, xc=TS[0])
            linear_out(act, at, "s4.q", (0, 1, 2, 3), range(KC), lambda ps, c: act.activation(Q4[:, c, :], ps, ACT.Identity, bias=v("bq4", c)))
            act.wait_ge(*at.done("s4.flag"))
            with at.loop(act, "s4.loop", B) as b:
                for h in (0, 1):
                    m0, mt = HALF[h]
                    w = mt * S
                    act.wait_ge(*at.done("s4.S7", back=1))
                    for n in range(8):
                        act.wait_ge(*at.done(f"s4.K{h}.{n}"))
                        act.activation(KT[:, n // 2, m0 * P + (n % 2) * w:m0 * P + (n % 2 + 1) * w], bank(n % 4, w),
                                           ACT.Identity, bias=v("bk4", n // 2)).then_inc(*at.step(f"s4.K{h}.{n}.out"))
                for p in range(NP):
                    act.wait_ge(*at.done(f"s4.max{p}"))
                    if p:
                        act.wait_ge(*at.done(f"s4.pt{p - 1}.3"))
                    else:
                        act.wait_ge(*at.done("s4.pt7.3", back=1))
                    act.activation(PR[:, :].rearrange("p (a m) -> p a m", a=4), PS[:, 0:4, 0:MB], ACT.Exp,
                                       bias=misc[:, 4 + p % 2:5 + p % 2], scale=SCALE, accum_out=misc[:, 8 + p % 2:9 + p % 2]).then_inc(*at.step(f"s4.exp{p}"))
                    for k in (0, 2):
                        m0, n = TG[k]
                        act.wait_ge(*at.done(f"s4.pt{p}.{k}"))
                        if p:
                            act.wait_ge(*at.done(f"s4.o{p - 1}"))
                        act.activation(PTs[:, m0:m0 + n, :], PS[:, 4 + k % 2, 0:n * P].rearrange("p (m q) -> p m q", q=P),
                                           ACT.Copy).then_inc(*at.step(f"s4.pt{p}.{k}.out"))

        def s4_dve(dve, at):
            dve.wait_ge(*at.done("mask"))
            if 1 in stages:
                dve.wait_ge(*at.done("x1"))
            dve.tensor_scalar(keep, PR[:, :].bitcast(I32), 0, None, ALU.not_equal).then_inc(*at.step())
            dve.wait_ge(*at.own())
            dve.tensor_scalar(maskneg[:, :], keep, -NEG, NEG, ALU.mult, ALU.add).then_inc(*at.step())
            dve.tensor_reduce(flag, keep, AX.X, ALU.max).then_inc(*at.step())
            dve.memset(TS[2][:, 0:2, :], 0.0).then_inc(*at.step("s4.flag"))
            norm_dve(dve, at, "s4.ln", X, N4, 1e-5, xc=N4)
            for c in range(KC):
                dve.wait_ge(*at.done(f"s4.q.{c}.out"))
            with at.loop(dve, "s4.loop", B) as b:
                dve.wait_ge(*at.done("s4.S7", back=1))
                for a in range(G):
                    dve.tensor_copy(qd[a * HD:(a + 1) * HD, :, a, :], Q4[a * HD:(a + 1) * HD, :, bass.ds(b * S, S)]).then_inc(*at.step("s4.qd"))
                dve.wait_ge(*at.done("s4.o7", back=1))
                for h in (0, 1):
                    m0, mt = HALF[h]
                    for j in range(mt):
                        dve.wait_ge(*at.done(f"s4.V{h}.{j}"))
                        dve.tensor_tensor(VT[:, m0 + j, :], bank(4 + (m0 + j) % 2), row("bv4", D), ALU.add).then_inc(*at.step(f"s4.V{h}.{j}.out"))

                def out(p):
                    a = (p % 2) * 64
                    dve.wait_ge(*at.done(f"s4.o{p}"))
                    for r in (0, 1):
                        q = a + r * HD
                        dve.tensor_copy(O4[q:q + HD, p // 2, bass.ds(b * S, S)], PS[q:q + HD, 6 + p % 2, r * S:(r + 1) * S]).then_inc(*at.step(f"s4.o{p}.out"))

                for p in range(NP):
                    mx, nm, sm = (misc[:, k + p % 2:k + 1 + p % 2] for k in (2, 4, 8))
                    dve.wait_ge(*at.done(f"s4.S{p}"))
                    dve.tensor_reduce(mx, PS[:, 0:4, 0:MB], AX.XY, ALU.max).then_inc(*at.step())
                    dve.wait_ge(*at.own())
                    dve.tensor_scalar(nm, mx, -SCALE, None, ALU.mult).then_inc(*at.step(f"s4.max{p}"))
                    if p:
                        for k in (1, 3):
                            m0, n = TG[k]
                            dve.wait_ge(*at.done(f"s4.pt{p - 1}.{k}"))
                            if p > 1:
                                dve.wait_ge(*at.done(f"s4.o{p - 2}"))
                            dve.tensor_copy(PTs[:, m0:m0 + n, :], PS[:, 4 + k % 2, 0:n * P].rearrange("p (m q) -> p m q", q=P)).then_inc(*at.step(f"s4.pt{p - 1}.{k}.out"))
                    dve.wait_ge(*at.done(f"s4.exp{p}"))
                    dve.reciprocal(sm, sm).then_inc(*at.step())
                    dve.wait_ge(*at.own())
                    dve.tensor_tensor(sm, sm, flag, ALU.mult).then_inc(*at.step())
                    dve.wait_ge(*at.own())
                    dve.tensor_scalar(PR[:, :], PR[:, :], sm, None, ALU.mult).then_inc(*at.step(f"s4.p{p}"))
                    if p:
                        out(p - 1)
                for k in (1, 3):
                    m0, n = TG[k]
                    dve.wait_ge(*at.done(f"s4.pt7.{k}"))
                    dve.wait_ge(*at.done("s4.o6"))
                    dve.tensor_copy(PTs[:, m0:m0 + n, :], PS[:, 4 + k % 2, 0:n * P].rearrange("p (m q) -> p m q", q=P)).then_inc(*at.step(f"s4.pt7.{k}.out"))
                out(7)
            for c in range(KC):
                dve.wait_ge(*at.done(f"s4.wo_.{c}"))
                dve.scalar_tensor_tensor(out=X[:, c, :], in0=bank(c), scalar=v("bo4", c), in1=X[:, c, :],
                                             op0=ALU.add, op1=ALU.add).then_inc(*at.step(f"s4.wo_.{c}.out"))
            at.same("x4", "s4.wo_.3.out")

        N5, Q5, K5, V5, O5 = TS[0], TS[1], TS[2], TS[3], TS[4]
        trig = RC[:, 4200:4200 + 2 * T].rearrange("p (a s) -> p a s", a=2)

        def rotate_pe(pe, at, tag, x, outs, banks):
            for c in range(KC):
                pe.wait_ge(*at.done(outs[c]))
                if bank_reader.get(banks[c]):
                    pe.wait_ge(*at.done(bank_reader[banks[c]]))
                pe.matmul(bank(banks[c]), C["rot"], x[:, c, :], start=True, stop=True).then_inc(*at.step(f"{tag}.{c}"))
                bank_reader[banks[c]] = f"{tag}.{c}.out"

        def rotate_dve(dve, at, tag, x, tmp, banks):
            for c in range(KC):
                dve.wait_ge(*at.done(f"{tag}.{c}"))
                dve.tensor_tensor(tmp[:, c, :], bank(banks[c]), trig[:, 1, :], ALU.mult).then_inc(*at.step(f"{tag}.{c}.out"))
                dve.tensor_tensor(x[:, c, :], x[:, c, :], trig[:, 0, :], ALU.mult).then_inc(*at.step())
                dve.wait_ge(*at.own())
                dve.tensor_tensor(x[:, c, :], x[:, c, :], tmp[:, c, :], ALU.add).then_inc(*at.step(f"{tag}.done"))

        def s5_pool(pool, at):
            if 4 in stages:
                pool.wait_ge(*at.done("s4.S7"))
            pool.dma_start(trig, t["trig"]).then_inc(*at.load("mask_loaded", "trig"))
            if 4 in stages:
                pool.wait_ge(*at.done("s4.o7"))
            attn_pool(pool, at, "s5.at", K5, ["s5.kr.done"])

        def s5_pe(pe, at):
            norm_pe(pe, at, "s5.ln", X, ["x4"] if 4 in stages else ["x"])
            linear_pe(pe, at, "s5.q", [("s5.wq", N5)], (0, 1, 2, 3), range(KC), ["s5.ln.done"])
            linear_pe(pe, at, "s5.k", [("s5.wk", N5)], (4, 5, 6, 7), range(KC))
            rotate_pe(pe, at, "s5.qr", Q5, [f"s5.q.{c}.out" for c in range(KC)], (0, 1, 2, 3))
            rotate_pe(pe, at, "s5.kr", K5, [f"s5.k.{c}.out" for c in range(KC)], (4, 5, 6, 7))
            values_pe(pe, at, "s5.v", "s5.wv", N5, (0, 1, 2, 3))
            attn_pe(pe, at, "s5.at", Q5, V5, ["s5.qr.done"] + [f"s5.v.{c}.out" for c in range(4)])
            linear_pe(pe, at, "s5.o", [("s5.wo", O5)], (0, 1, 2, 3), range(KC), ["s5.at.O3.out"])

        def s5_act(act, at):
            norm_act(act, at, "s5.ln", X, xc=N5)
            linear_out(act, at, "s5.q", (0, 1, 2, 3), range(KC), lambda ps, c: act.activation(Q5[:, c, :], ps, ACT.Identity, bias=v("bq5", c)))
            linear_out(act, at, "s5.k", (4, 5, 6, 7), range(KC), lambda ps, c: act.activation(K5[:, c, :], ps, ACT.Identity, bias=v("bk5", c)))
            attn_act(act, at, "s5.at")

        def s5_dve(dve, at):
            norm_dve(dve, at, "s5.ln", X, N5, 1e-5, xc=N5)
            dve.wait_ge(*at.done("trig"))
            rotate_dve(dve, at, "s5.qr", Q5, TS[4], (0, 1, 2, 3))
            rotate_dve(dve, at, "s5.kr", K5, TS[5], (4, 5, 6, 7))
            values_dve(dve, at, "s5.v", V5, "bv5", (0, 1, 2, 3))
            attn_dve(dve, at, "s5.at", O5, C["causal"])
            for c in range(KC):
                dve.wait_ge(*at.done(f"s5.o.{c}"))
                dve.scalar_tensor_tensor(out=X[:, c, :], in0=bank(c), scalar=v("bo5", c), in1=X[:, c, :],
                                             op0=ALU.add, op1=ALU.add).then_inc(*at.step(f"s5.o.{c}.out"))
            at.same("x5", "s5.o.3.out")

        N6, XT, SEL, SELG, SELT, EIN = TS[0], TS[1], TS[2], TS[3], TS[4], TS[5]
        YS = TS[1]
        EB = [QB[:, :, 0:S], QB[:, :, S:2 * S]]
        HS = [RC[0:S, 2048:2560], RC[0:S, 2560:3072]]
        HT = [RC[:, 3072 + 256 * k:3328 + 256 * k].rearrange("p (c s) -> p c s", c=KC) for k in (0, 1)]
        oh = RC[:, 128:160].rearrange("p (a e) -> p a e", e=E_)
        val = RC[:, 160:192].rearrange("p (a e) -> p a e", e=E_)
        gate6, idx6, pos6, over6, slot6 = (RC[:, 192 + 4 * k:196 + 4 * k] for k in range(5))

        def s6_pe(pe, at):
            norm_pe(pe, at, "s6.ln", X, ["x5"] if 5 in stages else ["x"])
            gate_pe(pe, at, "s6.g", N6, 1, ["s6.ln.done"])
            for tt in range(4):
                k = 4 + tt
                if bank_reader.get(k):
                    pe.wait_ge(*at.done(bank_reader[k]))
                for c in range(KC):
                    mm = pe.transpose(PS[:, k, c * P:(c + 1) * P], N6[:, c, tt * P:(tt + 1) * P], C["ident"])
                mm.then_inc(*at.step(f"s6.xt{tt}"))
            pe.wait_ge(*at.done("s6.onehot"))
            if bank_reader.get(1):
                pe.wait_ge(*at.done(bank_reader[1]))
            for tt in range(4):
                for u in range(tt + 1):
                    mm = pe.matmul(PS[:, 1, tt * E_:(tt + 1) * E_], C["earlier"] if u == tt else C["ones"], oh[:, u, :],
                                      start=(u == 0), stop=(u == tt))
            mm.then_inc(*at.step("s6.pos"))
            for due in at.last("s6.sel", "s6.pos.out", *(f"s6.xt{k}.out" for k in range(4))):
                pe.wait_ge(*due)
            for dc in range(KC):
                if bank_reader.get(dc) and dc > 1:
                    pe.wait_ge(*at.done(bank_reader[dc]))
                for tt in range(4):
                    mm = pe.matmul(bank(dc), XT[:, tt, dc * P:(dc + 1) * P], SEL[:, tt, :], start=(tt == 0), stop=(tt == 3))
                mm.then_inc(*at.step(f"s6.ein{dc}"))
            for j in range(4):
                for tt in range(4):
                    mm = pe.transpose(PS[:, 4 + j, tt * P:(tt + 1) * P], SELG[:, tt, j * P:(j + 1) * P], C["ident"])
                mm.then_inc(*at.step(f"s6.selt{j}"))
            for due in at.last(*(f"s6.ein{k}.out" for k in range(4)), *(f"s6.selt{k}.out" for k in range(4))):
                pe.wait_ge(*due)
            with at.loop(pe, "s6.loop", E_ // 2) as j:
                for k in (0, 1):
                    q = f"s6.{k}"

                    def hidden(s):
                        w = f"s6.moe.{k}.a{s}"
                        pe.wait_ge(*at.done(w))
                        if s >= 2:
                            pe.wait_ge(*at.done(f"{q}.h{s - 2}.out"))
                        elif k:
                            pe.wait_ge(*at.done(f"s6.0.h{s + 2}.out"))
                        else:
                            pe.wait_ge(*at.done(f"s6.1.h{s + 2}.out", back=1))
                        for c in range(KC):
                            mm = pe.matmul(PS[0:S, s % 2, :], EB[k][:, c, :], wt(w)[:, c, :], start=(c == 0), stop=(c == KC - 1))
                        mm.then_inc(*at.step(f"{q}.h{s}"))
                        at.same(w + ".used", f"{q}.h{s}")

                    def output(s):
                        w = f"s6.moe.{k}.b{s}"
                        pe.wait_ge(*at.done(f"{q}.h{s}.out"))
                        if s >= 2:
                            pe.wait_ge(*at.done(f"{q}.ht{s - 2}.out"))
                        elif k:
                            pe.wait_ge(*at.done(f"s6.0.ht{s + 2}.out"))
                        else:
                            pe.wait_ge(*at.done(f"s6.1.ht{s + 2}.out", back=1))
                        pe.nop(nofuse=True)
                        for c in range(KC):
                            mm = pe.transpose(PS[:, 2 + s % 2, c * S:(c + 1) * S], HS[s % 2][:, c * P:(c + 1) * P],
                                                 C["ident"][0:S, 0:S])
                        mm.then_inc(*at.step(f"{q}.ht{s}"))
                        for due in at.last(w, f"{q}.ht{s}.out"):
                            pe.wait_ge(*due)
                        if s == 0:
                            pe.wait_ge(*at.done(f"{q}.y.out", back=1))
                        for c in range(KC):
                            mm = pe.matmul(PS[k * S:(k + 1) * S, 4 + k, :], HT[s % 2][:, c, :], wt(w)[:, c, :],
                                              start=(s == 0 and c == 0), stop=(s == FS - 1 and c == KC - 1))
                        mm.then_inc(*at.step(f"{q}.y{s}"))
                        at.same(w + ".used", f"{q}.y{s}")

                    pe.wait_ge(*at.done(f"{q}.eb"))
                    hidden(0)
                    for s in range(FS):
                        if s + 1 < FS:
                            hidden(s + 1)
                        output(s)
            for due in at.last("s6.0.y.out", "s6.1.y.out"):
                pe.wait_ge(*due)
            rd = {0: "s6.1.h2.out", 1: "s6.1.h3.out", 2: "s6.1.ht2.out", 3: "s6.1.ht3.out"}
            for dc in range(KC):
                pe.wait_ge(*at.done(rd[dc]))
                for j in range(4):
                    mm = pe.matmul(bank(dc), YS[:, j, dc * P:(dc + 1) * P], SELT[:, j, :], start=(j == 0), stop=(j == 3))
                mm.then_inc(*at.step(f"s6.out{dc}"))

        def s6_act(act, at):
            norm_act(act, at, "s6.ln", X, xc=N6)
            gate_act(act, at, "s6.g")
            for dc in range(KC):
                act.wait_ge(*at.done(f"s6.ein{dc}"))
                act.activation(EIN[:, dc, :], bank(dc), ACT.Copy).then_inc(*at.step(f"s6.ein{dc}.out"))
            for j in range(4):
                act.wait_ge(*at.done(f"s6.selt{j}"))
                act.activation(SELT[:, j, :], bank(4 + j), ACT.Copy).then_inc(*at.step(f"s6.selt{j}.out"))
            with at.loop(act, "s6.loop", E_ // 2) as j:
                for k in (0, 1):
                    q = f"s6.{k}"
                    for s in range(FS):
                        act.wait_ge(*at.done(f"{q}.h{s}"))
                        if s >= 2:
                            act.wait_ge(*at.done(f"{q}.ht{s - 2}"))
                        elif k:
                            act.wait_ge(*at.done(f"s6.0.ht{s + 2}"))
                        else:
                            act.wait_ge(*at.done(f"s6.1.ht{s + 2}", back=1))
                        act.activation(HS[s % 2], PS[0:S, s % 2, :], ACT.Gelu_apprx_tanh).then_inc(*at.step(f"{q}.h{s}.out"))

        def s6_dve(dve, at):
            norm_dve(dve, at, "s6.ln", X, N6, 1e-5, xc=N6)
            gate_dve(dve, at, "s6.g", False)
            for tt in range(4):
                dve.wait_ge(*at.done(f"s6.xt{tt}"))
                dve.tensor_copy(XT[:, tt, :], bank(4 + tt)).then_inc(*at.step(f"s6.xt{tt}.out"))
            bc = lambda a: a.unsqueeze(2).broadcast_to([P, 4, E_])
            iota_e = row("iota_e", 32).rearrange("p (a e) -> p a e", e=E_)
            dve.wait_ge(*at.own())
            dve.tensor_reduce(gate6, ga, AX.X, ALU.max).then_inc(*at.step())
            dve.wait_ge(*at.own())
            dve.tensor_tensor(val, ga, bc(gate6), ALU.is_equal).then_inc(*at.step())
            dve.wait_ge(*at.own())
            dve.scalar_tensor_tensor(out=val, in0=val, scalar=-128.0, in1=iota_e, op0=ALU.mult, op1=ALU.add).then_inc(*at.step())
            dve.wait_ge(*at.own())
            dve.tensor_reduce(idx6, val, AX.X, ALU.min).then_inc(*at.step())
            dve.wait_ge(*at.own())
            dve.tensor_tensor(oh, val, bc(idx6), ALU.is_equal).then_inc(*at.step("s6.onehot"))
            dve.wait_ge(*at.done("s6.pos"))
            dve.tensor_tensor(val, PS[:, 1, 0:32].rearrange("p (a e) -> p a e", e=E_), oh, ALU.mult).then_inc(*at.step("s6.pos.out"))
            dve.wait_ge(*at.own())
            dve.tensor_reduce(pos6, val, AX.X, ALU.add).then_inc(*at.step())
            dve.wait_ge(*at.own())
            dve.tensor_scalar(over6, pos6, float(CAP), 16384.0, ALU.is_ge, ALU.mult).then_inc(*at.step())
            dve.tensor_scalar(slot6, idx6, float(CAP), 128.0 * CAP, ALU.mult, ALU.add).then_inc(*at.step())
            dve.wait_ge(*at.own())
            dve.tensor_tensor(slot6, slot6, pos6, ALU.add).then_inc(*at.step())
            dve.wait_ge(*at.own())
            dve.tensor_tensor(slot6, slot6, over6, ALU.add).then_inc(*at.step())
            dve.wait_ge(*at.own())
            for tt in range(4):
                dve.tensor_scalar(SEL[:, tt, :], row("iota_slot", D), slot6[:, tt:tt + 1], None, ALU.is_equal).then_inc(*at.step())
            dve.wait_ge(*at.own())
            for tt in range(4):
                dve.tensor_scalar(SELG[:, tt, :], SEL[:, tt, :], gate6[:, tt:tt + 1], None, ALU.mult).then_inc(*at.step("s6.sel"))
            for due in at.last(*(f"s6.ein{k}.out" for k in range(4))):
                dve.wait_ge(*due)
            with at.loop(dve, "s6.loop", E_ // 2) as j:
                for k in (0, 1):
                    q = f"s6.{k}"
                    dve.wait_ge(*at.done(f"{q}.h3", back=1))
                    dve.tensor_copy(EB[k], EIN[:, :, bass.ds(j * (2 * S) + k * S, S)]).then_inc(*at.step(f"{q}.eb"))
                for k in (0, 1):
                    q = f"s6.{k}"
                    for s in range(FS):
                        dve.wait_ge(*at.done(f"{q}.ht{s}"))
                        if s >= 2:
                            dve.wait_ge(*at.done(f"{q}.y{s - 2}"))
                        elif k:
                            dve.wait_ge(*at.done(f"s6.0.y{s + 2}"))
                        else:
                            dve.wait_ge(*at.done(f"s6.1.y{s + 2}", back=1))
                        dve.tensor_copy(HT[s % 2], PS[:, 2 + s % 2, 0:KC * S].rearrange("p (c s) -> p c s", c=KC)).then_inc(*at.step(f"{q}.ht{s}.out"))
                    dve.wait_ge(*at.done(f"{q}.y3"))
                    dve.tensor_copy(YS[k * S:(k + 1) * S, j, :], PS[k * S:(k + 1) * S, 4 + k, :]).then_inc(*at.step(f"{q}.y.out"))
            for dc in range(KC):
                dve.wait_ge(*at.done(f"s6.out{dc}"))
                dve.tensor_tensor(X[:, dc, :], X[:, dc, :], bank(dc), ALU.add).then_inc(*at.step("x6"))

        @block.sync
        def _(sync):
            at = Steps(sems, "out_stored", marks, new)
            for dst, src, name in ((X[:, :, :], t["x"], "x"), (sq[:, :, :], t["squares"], "x"), (vec[:, :], t["vecs"], "consts"),
                                   (rows[:, :], t["rows"], "consts"), (gw[:, :, :, :], t["gates"], "consts"), (RC[:, 1600:1792].rearrange("p (a b) -> p a b", a=3), t["abc"], "consts")):
                sync.dma_start(dst, src).then_inc(*at.load("consts_loaded", name))
            at.same("abc", "consts"); at.same("x", "consts")
            for name, tile in order:
                if tile is not None:
                    if before[name]:
                        sync.wait_ge(*at.done(before[name] + ".used"))
                    sync.dma_start(ring[slot[name]][:, :, :], t["tiles"][tile]).then_inc(*at.load(f"weights_loaded{slot[name]}", name))
                    continue
                for x in before[name]:
                    sync.wait_ge(*at.done(x + ".used"))
                if name == "s3.moe":
                    with at.loop(sync, "s3.loop", E_) as i:
                        for k, x in enumerate(EXPERT):
                            prev = EXPERT[(k - RING) % 8]
                            sync.wait_ge(*at.done(f"{name}.{prev}.used", back=0 if k >= RING else 1))
                            sync.dma_start(ring[k % RING][:, :, :], t["experts3"][i, k]).then_inc(*at.load(f"weights_loaded{k % RING}", f"{name}.{x}"))
                else:
                    with at.loop(sync, "s6.loop", E_ // 2) as i:
                        for n in range(16):
                            prev = (n - RING) % 16
                            sync.wait_ge(*at.done(f"{name}.{prev // 8}.{EXPERT[prev % 8]}.used", back=0 if n >= RING else 1))
                            sync.dma_start(ring[n % RING][:, :, :], t["experts6"][i, n]).then_inc(*at.load(f"weights_loaded{n % RING}", f"{name}.{n // 8}.{EXPERT[n % 8]}"))
            sync.wait_ge(*at.done(f"x{max(stages)}"))
            sync.dma_start(t["out"], X[:, :, :]).then_inc(*at.load("out_stored", "stored"))
            sync.wait_ge(sems["out_stored"], 16)

        @block.gpsimd
        def _(pool):
            at = Steps(sems, "pool_done", marks, new)
            if 1 in stages:
                s1_pool(pool, at)
                pool.wait_ge(*at.done("x1"))
            pool.dma_start(PR[:, :].bitcast(I32), t["mask"]).then_inc(*at.load("mask_loaded", "mask"))
            for s, part in ((2, s2_pool), (3, s3_pool), (4, s4_pool), (5, s5_pool)):
                if s in stages:
                    part(pool, at)

        @block.scalar
        def _(act):
            at = Steps(sems, "scalar_done", marks, new)
            for s, part in ((1, s1_act), (2, s2_act), (3, s3_act), (4, s4_act), (5, s5_act), (6, s6_act)):
                if s in stages:
                    part(act, at)

        @block.tensor
        def _(pe):
            at = Steps(sems, "tensor_done", marks, new)
            bank_reader.clear()
            for s, part in ((1, s1_pe), (2, s2_pe), (3, s3_pe), (4, s4_pe), (5, s5_pe), (6, s6_pe)):
                if s in stages:
                    part(pe, at)

        @block.vector
        def _(dve):
            at = Steps(sems, "vector_done", marks, new)
            dve.wait_ge(*at.done("x"))
            dve.tensor_copy(idb[:, :], C["ident"]).then_inc(*at.step("idb"))
            for s, part in ((1, s1_dve), (2, s2_dve), (3, s3_dve), (4, s4_dve), (5, s5_dve), (6, s6_dve)):
                if s in stages:
                    part(dve, at)


def _tiles(w, n=None):
    a, b = w.shape[0] // D, w.shape[1] // D
    return w.reshape(a, KC, P, b, D).transpose(0, 3, 2, 1, 4).reshape(a * b, P, KC, D)


def layout(i):
    f = lambda n: np.asarray(i[n])
    feat = lambda a: a.reshape(T, D).T.reshape(KC, P, T).transpose(1, 0, 2)
    ctx = np.zeros((B, MP, D), np.float32)
    ctx[:, :M] = f("ctx_1024")
    g, a0, f0 = "L0_xattn_", "L0_attn_", "L0_ffn_"
    tiles = [f(g + "Wq").T, f(g + "Wk"), f(g + "Wv").T]
    for k in range(3):
        tiles += [f(g + "gru_wih")[k * D:(k + 1) * D].T, f(g + "gru_whh")[k * D:(k + 1) * D].T]
    tiles += [f(a0 + "out_w").T]
    for j in range(FS):
        tiles += [f(a0 + "ffn1_w")[j * D:(j + 1) * D].T, f(a0 + "ffn2_w")[:, j * D:(j + 1) * D].T]
    tiles += [f(f0 + "conv_w")[:, :, k].T for k in range(3)]
    tiles += [f(f0 + "wqkv")[k * D:(k + 1) * D].T for k in range(3)] + [f(f0 + "wo").T]
    tiles += [f("L1_xattn_" + n) for n in ("Wq", "Wk", "Wv", "Wo")] + [f("L1_attn_" + n).T for n in ("Wq", "Wk", "Wv", "Wo")]
    experts = lambda w1, w2: np.stack([np.concatenate([(_tiles(w1[x]) if ab == "a" else _tiles(w2[x]))[int(s):int(s) + 1]
                                       for ab, s in ("a0", "a1", "b0", "a2", "b1", "a3", "b2", "b3")]) for x in range(E_)])
    src = dict(slot_w=g + "slot_norm_w", in_w=g + "input_norm_w", bih=g + "gru_bih", bhh=g + "gru_bhh", ln_w=a0 + "ln_w",
               ln_b=a0 + "ln_b", D=a0 + "D_vec", out_b=a0 + "out_b", ln2_w=a0 + "ln2_w", ln2_b=a0 + "ln2_b",
               ffn1_b=a0 + "ffn1_b", ffn2_b=a0 + "ffn2_b", conv_b=f0 + "conv_b", bqkv=f0 + "bqkv", bo3=f0 + "bo",
               ln1_g=f0 + "ln1_g", ln1_b=f0 + "ln1_b", ln2_g=f0 + "ln2_g", ln2b3=f0 + "ln2_b", b1=f0 + "b1", b2=f0 + "b2",
               bq4="L1_xattn_bq", bk4="L1_xattn_bk", bo4="L1_xattn_bo", bq5="L1_attn_bq", bk5="L1_attn_bk", bo5="L1_attn_bo")
    vecs = np.concatenate([f(src[n]).reshape(-1, P).T for n, _ in VECS], axis=1)
    rep = lambda a: np.broadcast_to(a, (P, a.shape[-1]))
    rows = np.concatenate([rep(f(f0 + "gate_b")), rep(f(f0 + "bqkv")[2 * D:]), rep(f("L1_xattn_bv")), rep(f("L1_attn_bv")),
                           rep(np.arange(D, dtype=np.float32)), rep(np.tile(np.arange(E_, dtype=np.float32), 4))], axis=1)
    gates = np.stack([f(f0 + "gate_w").reshape(KC, P, E_), f("L1_ffn_router_w").reshape(KC, P, E_)]).transpose(2, 0, 1, 3)
    abc = np.stack([f(a0 + n).reshape(KC, P, N_STATE) for n in ("A_log", "B_mat", "C_mat")]).transpose(2, 0, 1, 3).reshape(P, 3, -1)
    r = np.arange(P)
    same = (r[:, None] // S) == (r[None] // S)
    rot = np.zeros((P, P), np.float32)
    rot[r[1::2], r[::2]] = -1
    rot[r[::2], r[1::2]] = 1
    squares = np.stack([np.eye(P), np.full((P, P), 1 / D), np.ones((P, P)), np.where(same, 0, NEG),
                        np.where(same & (r[None] <= r[:, None]), 0, NEG), r[:, None] < r[None], rot]).astype(np.float32)
    ang = np.outer(np.arange(S, dtype=np.float32), (1.0 / np.float32(10000.0) ** (np.arange(0, HD, 2, dtype=np.float32) / HD)))
    ang = np.tile(ang[:, (r % HD) // 2].T, (1, B)).astype(np.float32)
    mask = np.zeros((P, MP), np.int32)
    mask[:, :M] = np.concatenate([f("mask_SxS2_ik0")] * 2)
    return {
        "x": feat(f("x")), "ctxN": ctx.reshape(B, MT, P, D).transpose(0, 2, 1, 3),
        "ctxT": ctx.reshape(B, MP, KC, P).transpose(0, 3, 2, 1), "mask": mask,
        "tiles": np.stack([_tiles(w)[0] for w in tiles]),
        "experts3": experts(f(f0 + "w1"), f(f0 + "w2")),
        "experts6": experts(f("L1_ffn_w1"), f("L1_ffn_w2")).reshape(E_ // 2, 16, P, KC, D),
        "vecs": vecs, "rows": rows, "gates": gates, "abc": abc,
        "squares": squares.transpose(1, 0, 2), "trig": np.stack([np.cos(ang), np.sin(ang)], axis=1),
    }


def kernel(**inputs):
    import concourse.bacc as bacc
    from concourse.bass_utils import run_bass_kernel_spmd

    arrays = {n: np.ascontiguousarray(a) for n, a in layout(inputs).items()}

    def program(marks):
        nc = bacc.Bacc("TRN2", target_bir_lowering=False, num_devices=1)
        t = {n: nc.dram_tensor(f"in_{n}", a.shape, mybir.dt.from_np(a.dtype), kind="ExternalInput").ap() for n, a in arrays.items()}
        t["out"] = nc.dram_tensor("out_x", (P, KC, T), FP32, kind="ExternalOutput").ap()
        new = Marks()
        build(nc, marks, new, t)
        return nc, new

    _, counted = program(Marks())
    nc, _ = program(counted)
    r = run_bass_kernel_spmd(nc, [{f"in_{n}": a for n, a in arrays.items()}], core_ids=[0])
    y = r.results[0]["out_x"]
    return np.ascontiguousarray(y.transpose(1, 0, 2).reshape(D, T).T).reshape(B, S, D)
```

```python
import numpy as np
import concourse.bass as bass
from concourse import mybir
from contextlib import ExitStack, contextmanager

FP32, BF16, I32 = mybir.dt.float32, mybir.dt.bfloat16, mybir.dt.int32
FP32R = mybir.dt.float32r
ALU, ACT, AX = mybir.AluOpType, mybir.ActivationFunctionType, mybir.AxisListType

B, S, D = 8, 64, 512
T = B * S
P = 128
KC = D // P
M = 1601
MT = -(-M // P)
MP = MT * P
MLAST = M - (MT - 1) * P
HALF = [(0, 7), (7, MT - 7)]
H, HD = 16, 32
G = H // KC
E_, F = 8, 2048
FS = F // D
CAP = T // E_
N_STATE = 16
RING = 4
MB = MP // 4
NEG = -1e30
AHEAD = 100

S1_TILES = ["wq", "wk", "wv"] + [f"{w}{g}" for g in range(3) for w in ("wih", "whh")]
SMALL = [f"s1.{n}" for n in S1_TILES]
SMALL += ["s2.out"] + [f"s2.{w}{j}" for j in range(FS) for w in ("ffn1_", "ffn2_")]
SMALL += [f"s3.conv{k}" for k in range(3)] + ["s3.wq", "s3.wk", "s3.wv", "s3.wo"]
SMALL += ["s4.wq", "s4.wk", "s4.wv", "s4.wo", "s5.wq", "s5.wk", "s5.wv", "s5.wo"]
AT = {n: i for i, n in enumerate(SMALL)}

VECS = [("slot_w", 4), ("in_w", 4), ("bih", 12), ("bhh", 12), ("ln_w", 4), ("ln_b", 4), ("D", 4), ("out_b", 4),
        ("ln2_w", 4), ("ln2_b", 4), ("ffn1_b", 16), ("ffn2_b", 4), ("conv_b", 4), ("bqkv", 12), ("bo3", 4),
        ("ln1_g", 4), ("ln1_b", 4), ("ln2_g", 4), ("ln2b3", 4), ("b1", 16 * E_), ("b2", 4 * E_),
        ("bq4", 4), ("bk4", 4), ("bo4", 4), ("bq5", 4), ("bk5", 4), ("bo5", 4)]
VAT, _n = {}, 0
for _k, _w in VECS:
    VAT[_k] = _n
    _n += _w
NVEC = _n
ROWS = [("gate_b", 8), ("bv3", D), ("bv4", D), ("bv5", D), ("iota_slot", D), ("iota_e", 4 * E_), ("in_last", 1)]
RAT, _n = {}, 0
for _k, _w in ROWS:
    RAT[_k] = _n
    _n += _w
NROW = _n
SQ = ["ident", "ones_d", "ones", "blockmask", "causal", "earlier", "rot"]


class Marks:

    def __init__(self):
        self.at, self.per = {}, {}


class Steps:

    def __init__(self, sems, own_key, marks, new):
        self.sems, self.own_key, self.marks, self.new = sems, own_key, marks, new
        self.count, self.i, self.inside = {}, None, None

    def load(self, key, name=None, by=16):
        self.count[key] = self.count.get(key, 0) + by
        if name:
            self.new.at[name] = (key, self.count[key], self.inside)
        return self.sems[key], by

    def step(self, name=None, by=1):
        return self.load(self.own_key, name, by)

    def same(self, name, other=None):
        self.new.at[name] = self.new.at[other] if other else (self.own_key, self.count[self.own_key], self.inside)

    def done(self, name, back=0):
        key, n, loop = self.marks.at.get(name, (self.own_key, 1, None))
        per, reps = self.marks.per.get((loop, key), (0, 1))
        if loop is None:
            return self.sems[key], n
        if loop == self.inside:
            assert n - per * back >= 0, (name, n, per)
            return self.sems[key], n - per * back + self.i * per
        return self.sems[key], n + per * (reps - 1)

    def last(self, *names, back=0):
        last = {}
        for name in names:
            key, n, _ = self.marks.at.get(name, (self.own_key, 1, None))
            if n >= last.get(key, (0, None))[0]:
                last[key] = n, name
        return [self.done(name, back) for _, name in last.values()]

    def own(self):
        n = self.count.get(self.own_key, 0)
        if self.inside is not None:
            n = n + self.i * self.marks.per.get((self.inside, self.own_key), (0, 1))[0]
        return self.sems[self.own_key], n

    @contextmanager
    def loop(self, eng, name, reps):
        before = dict(self.count)
        with eng.Fori(0, reps) as i:
            self.i, self.inside = i, name
            yield i
        self.i, self.inside = None, None
        for key, n in list(self.count.items()):
            per = n - before.get(key, 0)
            if per:
                self.new.per[name, key] = (per, reps)
                self.count[key] = n + per * (reps - 1)


def sem_names():
    return (["tensor_done", "scalar_done", "vector_done", "pool_done", "consts_loaded", "mask_loaded", "out_stored"]
            + [f"weights_loaded{s}" for s in range(RING)]
            + [f"{c}_loaded{h}" for c in ("ctxT", "ctxN") for h in (0, 1)])


def build(nc, marks, new, t, stages=(1, 2, 3, 4, 5, 6)):
    ctx = ExitStack()
    with ctx:
        address = {}

        def sb(name, shape, dt=FP32):
            address[name] = nc.sbuf_base
            return ctx.enter_context(nc.sbuf_tensor(name, shape, dt))

        def part(name, of, k=0, n=D):
            return nc.alloc_sbuf_tensor_at(name, [P, KC, n], FP32R, offset=address[of] + round(4 * k * KC * D))

        X = sb("X", [P, KC, T])
        TS = [sb(f"T{k}", [P, KC, T]) for k in range(6)]
        ring = [sb(f"ring{s}", [P, KC, D]) for s in range(RING)]
        RA, RB, RC = (sb(n, [P, MT * D]) for n in ("RA", "RB", "RC"))
        n0 = HALF[0][1]
        CT = [RA[:, 0:KC * n0 * P].rearrange("p (c m) -> p c m", c=KC),
              RA[:, KC * n0 * P:KC * MP].rearrange("p (c m) -> p c m", c=KC)]
        CN = [RB[:, 0:n0 * D].rearrange("p (m d) -> p m d", d=D),
              RB[:, n0 * D:MT * D].rearrange("p (m d) -> p m d", d=D)]
        RA4 = [RA[:, k * 2048:(k + 1) * 2048].rearrange("p (c m) -> p c m", c=KC) for k in range(3)]
        RB4 = [RB[:, k * 2048:(k + 1) * 2048].rearrange("p (c m) -> p c m", c=KC) for k in range(3)]
        RC4 = [RC[:, k * 2048:(k + 1) * 2048].rearrange("p (c m) -> p c m", c=KC) for k in range(3)]
        ring_part = [part(f"W_part{s}", f"ring{s}") for s in range(RING)]
        WH = [part("W_high0", "RB", 2), part("W_high1", "RC", 2), part("W_high2", "RA", 2)]
        XH, XL = part("X_high", "T4"), part("X_low", "T5")
        HH = [part("H_high0", "RB", 0), part("H_high1", "RB", 1)]
        HL = [part("H_low0", "RC", 0), part("H_low1", "RC", 1)]
        CL = [part("C_low0", "RA", 0, n0 * P), part("C_low1", "RA", n0 * P / D, HALF[1][1] * P)]
        CH = [part("C_high0", "T4", 0, n0 * P), part("C_high1", "T0", 0, HALF[1][1] * P)]
        assert address["T5"] == address["T4"] + 4 * KC * T and address["T1"] == address["T0"] + 4 * KC * T
        sq = sb("sq", [P, len(SQ), P])
        C = {n: sq[:, k, :] for k, n in enumerate(SQ)}
        vec = sb("vec", [P, NVEC])
        rows = sb("rows", [P, NROW])
        gw = sb("gw", [P, 2, KC, E_])
        kconv = sb("kconv", [P, KC, S])
        RN = sb("RN", [P, B, MT])
        bsum = sb("bsum", [P, 12])
        inws = sb("inws", [P, 4])
        rstd = sb("rstd", [P, T])
        misc = sb("misc", [P, 512])
        idb = sb("idb", [P, P], BF16)
        PR = sb("PR", [P, 2, MP])
        PTs = sb("PTs", [P, MT, P])
        maskneg = sb("maskneg", [P, MP], BF16)
        QB = PR[:, 1, 0:KC * P].rearrange("p (c k) -> p c k", c=KC)
        PS = ctx.enter_context(nc.psum_tensor("PS", [P, 8, 512], FP32))

        def v(name, c=0):
            k = VAT[name] + c
            return vec[:, k:k + 1]

        def row(name, n):
            return rows[:, RAT[name]:RAT[name] + n]

        sems = {n: ctx.enter_context(nc.semaphore(n)) for n in sem_names()}
        block = ctx.enter_context(nc.Block())

        def bank(k, n=512):
            return PS[:, k, 0:n]

        EXPERT = ["a0", "a1", "b0", "a2", "b1", "a3", "b2", "b3"]
        order = []
        if 1 in stages:
            order += [(f"s1.{it}.{n}", AT[f"s1.{n}"]) for it in range(3) for n in S1_TILES]
        if 2 in stages:
            order += [(n, AT[n]) for n in ["s2.out"] + [f"s2.ffn{1 if x[0] == 'a' else 2}_{x[1]}" for x in EXPERT]]
        if 3 in stages:
            order += [(n, AT[n]) for n in SMALL if n.startswith("s3.")] + [("s3.moe", None)]
        for st in (4, 5):
            if st in stages:
                order += [(n, AT[n]) for n in SMALL if n.startswith(f"s{st}.")]
        if 6 in stages:
            order += [("s6.moe", None)]
        slot, before, place = {}, {}, 0
        last = [None] * RING
        for name, tile in order:
            if tile is None:
                place = -(-place // RING) * RING
                before[name] = [x for x in last if x]
                tiles = EXPERT if name == "s3.moe" else [f"{k}.{x}" for k in (0, 1) for x in EXPERT]
                for k, x in enumerate(tiles):
                    slot[f"{name}.{x}"] = k % RING
                    last[k % RING] = f"{name}.{x}"
            else:
                slot[name] = place % RING
                before[name] = last[place % RING]
                last[place % RING] = name
                place += 1

        before_wk_high = before.get("s4.wo")
        if 4 in stages:
            before["s4.wo"] = "s4.wk"
            if 5 in stages:
                before["s5.wq"] = "s4.wk"

        def wt(name):
            return ring[slot[name]]

        bank_reader = {}

        def linear_pe(pe, at, tag, terms, banks, outs, after=()):
            for due in at.last(*after):
                pe.wait_ge(*due)
            for n, oc in enumerate(outs):
                k = banks[n % len(banks)]
                if bank_reader.get(k):
                    pe.wait_ge(*at.done(bank_reader[k]))
                for a, (w, x) in enumerate(terms):
                    if n == 0:
                        pe.wait_ge(*at.done(w))
                    for c in range(KC):
                        mm = pe.matmul(bank(k), wt(w)[:, c, oc * P:(oc + 1) * P], x[:, c, :],
                                          start=(a == 0 and c == 0), stop=(a == len(terms) - 1 and c == KC - 1))
                mm.then_inc(*at.step(f"{tag}.{oc}"))
                bank_reader[k] = f"{tag}.{oc}.out"
            for w, _ in terms:
                at.same(w + ".used")

        def linear_out(act, at, tag, banks, outs, op):
            for n, oc in enumerate(outs):
                act.wait_ge(*at.done(f"{tag}.{oc}"))
                op(bank(banks[n % len(banks)]), oc).then_inc(*at.step(f"{tag}.{oc}.out"))

        def norm_pe(pe, at, tag, x, after, centred=True):
            if centred:
                for due in at.last(*after):
                    pe.wait_ge(*due)
                if bank_reader.get(7):
                    pe.wait_ge(*at.done(bank_reader[7]))
                for c in range(KC):
                    mm = pe.matmul(bank(7), C["ones_d"], x[:, c, :], start=(c == 0), stop=(c == KC - 1))
                mm.then_inc(*at.step(f"{tag}.mean"))
                bank_reader[7] = f"{tag}.centred"
            pe.wait_ge(*at.done(f"{tag}.square"))
            if bank_reader.get(6):
                pe.wait_ge(*at.done(bank_reader[6]))
            for c in range(KC):
                mm = pe.matmul(bank(6), C["ones_d"], TS[5][:, c, :], start=(c == 0), stop=(c == KC - 1))
            mm.then_inc(*at.step(f"{tag}.var"))
            bank_reader[6] = f"{tag}.eps"

        def norm_act(act, at, tag, x, after=(), centred=True, xc=None):
            xc = xc if centred else x
            for due in at.last(*([f"{tag}.centred"] if centred else after)):
                act.wait_ge(*due)
            act.activation(TS[5][:, :, :], xc[:, :, :], ACT.Square).then_inc(*at.step(f"{tag}.square"))
            act.wait_ge(*at.done(f"{tag}.eps"))
            act.activation(rstd[:, :], rstd[:, :], ACT.Sqrt).then_inc(*at.step(f"{tag}.root"))

        def norm_dve(dve, at, tag, x, y, eps, w=None, b=None, centred=True, xc=None):
            if centred:
                dve.wait_ge(*at.done(f"{tag}.mean"))
                dve.tensor_tensor(xc[:, :, :], x[:, :, :], bank(7).unsqueeze(1).broadcast_to([P, KC, T]),
                                      ALU.subtract).then_inc(*at.step(f"{tag}.centred"))
            else:
                xc = x
            dve.wait_ge(*at.done(f"{tag}.var"))
            dve.tensor_scalar(rstd[:, :], bank(6), eps, None, ALU.add).then_inc(*at.step(f"{tag}.eps"))
            dve.wait_ge(*at.done(f"{tag}.root"))
            dve.reciprocal(rstd[:, :], rstd[:, :]).then_inc(*at.step())
            dve.wait_ge(*at.own())
            for c in range(KC):
                if w:
                    op = dve.scalar_tensor_tensor(out=y[:, c, :], in0=xc[:, c, :], scalar=v(w, c), in1=rstd[:, :],
                                                    op0=ALU.mult, op1=ALU.mult)
                else:
                    op = dve.tensor_tensor(y[:, c, :], xc[:, c, :], rstd[:, :], ALU.mult)
                op.then_inc(*at.step(f"{tag}.scaled"))
            if b:
                dve.wait_ge(*at.own())
                for c in range(KC):
                    dve.tensor_scalar(y[:, c, :], y[:, c, :], v(b, c), None, ALU.add).then_inc(*at.step())
            at.same(f"{tag}.done")

        SL, SN, UP, RG, ZG = TS[0], TS[1], TS[2], TS[3], TS[4]
        ss = PR[0:S, 0, :]
        W1 = MT * S
        ptf = PTs[:, :, :].rearrange("p m k -> p (m k)")
        rgf = RG[:, :, :].rearrange("p c t -> p (c t)")
        A_ = [ptf[:, u * W1:(u + 1) * W1].rearrange("p (m k) -> p m k", k=S) for u in (0, 1)]
        AR = [rgf[:, u * W1:(u + 1) * W1].rearrange("p (m k) -> p m k", k=S) for u in (0, 1)]
        UN = [RC[0:S, u * D:(u + 1) * D] for u in (0, 1)]
        asum = [RC[:, 1024 + u * S:1088 + u * S] for u in (0, 1)]
        stat = [[misc[:, 64 * u + 8 * k:64 * u + 8 * k + 8] for k in range(4)] for u in (0, 1)]
        ssq = [misc[:, 128 + 16 * u:128 + 16 * u + MT] for u in (0, 1)]
        rden = [misc[0:S, 160 + u:161 + u] for u in (0, 1)]
        sqs = TS[5][:, 0, :]
        qb = [QB[:, :, u * S:(u + 1) * S] for u in (0, 1)]
        SPLIT = MT - 4
        CNB = RC[:, 1792:1792 + SPLIT * D].rearrange("p (m d) -> p m d", d=D)
        cn_all = RB[:, 0:MT * D].rearrange("p (m d) -> p m d", d=D)

        def cn(u, m):
            if u == 0:
                return cn_all[:, m, :]
            return CNB[:, m, :] if m < SPLIT else ZG[:, m - SPLIT, :]

        def s1_pool(pool, at):
            for it in range(3):
                L = f"s1.{it}.loop"
                if it:
                    for due in at.last(*(f"s1.{it - 1}.z.{c}.out" for c in range(KC)), f"s1.{it - 1}.sl"):
                        pool.wait_ge(*due)
                with at.loop(pool, L, B // 2) as b:
                    for u in (0, 1):
                        for h in (0, 1):
                            m0, mt = HALF[h]
                            pool.wait_ge(*at.done(f"{L}.S{h}.{1 - u}", back=1 - u))
                            pool.nop(nofuse=True)
                            pool.dma_start(CT[h][:, :, :], t["ctxT"][b * 2 + u, :, :, m0 * P:(m0 + mt) * P])\
                                .then_inc(*at.load(f"ctxT_loaded{h}", f"{L}.ct{h}.{u}"))
                        pool.wait_ge(*at.done(f"{L}.U.{u}", back=1))
                        pool.nop(nofuse=True)
                        if u == 0:
                            pool.dma_start(cn_all, t["ctxN"][b * 2]).then_inc(*at.load("ctxN_loaded0", f"{L}.cn.0"))
                        else:
                            pool.dma_start(CNB, t["ctxN"][b * 2 + 1, :, 0:SPLIT, :]).then_inc(*at.load("ctxN_loaded1"))
                            pool.dma_start(ZG[:, :, :], t["ctxN"][b * 2 + 1, :, SPLIT:MT, :])\
                                .then_inc(*at.load("ctxN_loaded1", f"{L}.cn.1"))

        def s1_pe(pe, at):
            norm_pe(pe, at, "s1.ln", X, ["x"])
            for it in range(3):
                p, L = f"s1.{it}", f"s1.{it}.loop"
                norm_pe(pe, at, f"{p}.rms", SL, [], centred=False)
                linear_pe(pe, at, f"{p}.q", [(f"{p}.wq", SN)], (0, 1, 2, 3), range(KC), [f"{p}.rms.done"])
                linear_pe(pe, at, f"{p}.qk", [(f"{p}.wk", UP)], (0, 1, 2, 3), range(KC), [f"{p}.q.{c}.out" for c in range(KC)])

                def scores(u, h):
                    m0, mt = HALF[h]
                    w = mt * S
                    if h == 0:
                        pe.wait_ge(*at.done(f"{L}.qb.{u}"))
                    pe.wait_ge(*at.done(f"{L}.ct{h}.{u}"))
                    if u == 0:
                        pe.wait_ge(*at.done(f"{p}.qk.3.out"))
                    pe.wait_ge(*at.done(f"{L}.S{h}.{1 - u}.out", back=1 - u))
                    for j in (0, 1):
                        for c in range(KC):
                            mm = pe.matmul(PS[0:S, 2 * h + j, 0:w], qb[u][:, c, :], CT[h][:, c, j * w:(j + 1) * w],
                                           start=(c == 0), stop=(c == KC - 1))
                    mm.then_inc(*at.step(f"{L}.S{h}.{u}"))

                def transposes(u, h):
                    m0, mt = HALF[h]
                    pe.wait_ge(*at.done(f"{L}.S{h}.{u}.out"))
                    if u:
                        pe.wait_ge(*at.done(f"{L}.st{h}.0"))
                    else:
                        pe.wait_ge(*at.done(f"{L}.ut.{h}", back=1))
                    pe.nop(nofuse=True)
                    for j in range(mt):
                        mm = pe.transpose(PS[:, 4 + h, j * S:(j + 1) * S], ss[:, (m0 + j) * P:(m0 + j + 1) * P],
                                          C["ident"][0:S, 0:S])
                    mm.then_inc(*at.step(f"{L}.T{h}.{u}"))

                def updates(u, h):
                    m0, mt = HALF[h]
                    pe.wait_ge(*at.done(f"{L}.ar{h}.{u}"))
                    if h == 0:
                        pe.wait_ge(*at.done(f"{L}.cn.{u}"))
                        pe.wait_ge(*at.done(f"{L}.un.{u}", back=1))
                    for m in range(m0, m0 + mt):
                        mm = pe.matmul(PS[0:S, 6 + u, :], AR[u][:, m, :], cn(u, m), start=(m == 0), stop=(m == MT - 1))
                    if h:
                        mm.then_inc(*at.step(f"{L}.U.{u}"))

                def totals(u):
                    pe.wait_ge(*at.done(f"{L}.asum.{u}"))
                    pe.wait_ge(*at.done(f"{L}.st{u}.1"))
                    pe.matmul(PS[0:S, 4 + u, 448:449], asum[u], C["ones"][:, 0:1], start=True, stop=True)\
                        .then_inc(*at.step(f"{L}.den.{u}"))

                def turn(u):
                    pe.wait_ge(*at.done(f"{L}.un.{u}"))
                    pe.nop(nofuse=True)
                    for c in range(KC):
                        mm = pe.transpose(PS[:, 4 + u, c * S:(c + 1) * S], UN[u][:, c * P:(c + 1) * P], C["ident"][0:S, 0:S])
                    mm.then_inc(*at.step(f"{L}.UT.{u}"))

                with at.loop(pe, L, B // 2) as b:
                    scores(0, 0)
                    scores(0, 1)
                    transposes(0, 0)
                    scores(1, 0)
                    transposes(0, 1)
                    scores(1, 1)
                    transposes(1, 0)
                    updates(0, 0)
                    transposes(1, 1)
                    updates(0, 1)
                    totals(0)
                    updates(1, 0)
                    turn(0)
                    totals(1)
                    updates(1, 1)
                    turn(1)
                bank_reader.update({k: f"{L}.S{k // 2}.1.out" for k in range(4)})
                bank_reader.update({4: f"{L}.ut.0", 5: f"{L}.ut.1", 6: f"{L}.un.0", 7: f"{L}.un.1"})
                linear_pe(pe, at, f"{p}.v", [(f"{p}.wv", UP)], (0, 1, 2, 3), range(KC), [f"{p}.utw"])
                vout = [f"{p}.v.{c}.out" for c in range(KC)]
                linear_pe(pe, at, f"{p}.r", [(f"{p}.wih0", SN), (f"{p}.whh0", SL)], (0, 1, 2, 3), range(KC), vout)
                linear_pe(pe, at, f"{p}.z", [(f"{p}.wih1", SN), (f"{p}.whh1", SL)], (0, 1, 2, 3), range(KC))
                linear_pe(pe, at, f"{p}.gx", [(f"{p}.wih2", SN)], (4, 5, 6, 7), range(KC))
                linear_pe(pe, at, f"{p}.gh", [(f"{p}.whh2", SL)], (0, 1, 2, 3), range(KC))
                if it < 2:
                    pe.wait_ge(*at.done(f"{p}.sl"))

        def s1_act(act, at):
            norm_act(act, at, "s1.ln", X, xc=SN)
            for it in range(3):
                p, L = f"s1.{it}", f"s1.{it}.loop"
                norm_act(act, at, f"{p}.rms", SL, ["s1.ln.done"] if it == 0 else [f"s1.{it - 1}.sl"], centred=False)
                linear_out(act, at, f"{p}.q", (0, 1, 2, 3), range(KC),
                           lambda ps, c: act.activation(UP[:, c, :], ps, ACT.Copy))
                if it == 0:
                    act.wait_ge(*at.done("s1.inws"))
                linear_out(act, at, f"{p}.qk", (0, 1, 2, 3), range(KC),
                           lambda ps, c: act.activation(SN[:, c, :], ps, ACT.Copy, scale=inws[:, c:c + 1]))

                def squares(u):
                    act.wait_ge(*at.done(f"{L}.cn.{u}"))
                    for m in range(MT):
                        act.wait_ge(*at.own())
                        act.activation(sqs, cn(u, m), ACT.Square, accum_out=ssq[u][:, m:m + 1]).then_inc(*at.step(f"{L}.ssq.{u}"))
                    act.wait_ge(*at.done(f"{L}.msq.{u}"))
                    act.activation(ssq[u], ssq[u], ACT.Sqrt).then_inc(*at.step(f"{L}.rms.{u}"))

                def scores_out(u, h):
                    m0, mt = HALF[h]
                    w = mt * S
                    act.wait_ge(*at.done(f"{L}.S{h}.{u}"))
                    act.wait_ge(*at.done(f"{L}.T{h}.{1 - u}", back=1 - u))
                    act.activation(ss[:, m0 * P:(m0 + mt) * P].rearrange("p (a m) -> p a m", a=2),
                                   PS[0:S, 2 * h:2 * h + 2, 0:w], ACT.Copy).then_inc(*at.step(f"{L}.S{h}.{u}.out"))

                def exps(u, h):
                    m0, mt = HALF[h]
                    x = A_[u][:, m0:m0 + mt, :]
                    act.wait_ge(*at.done(f"{L}.sub{h}.{u}"))
                    act.activation(x, x, ACT.Exp).then_inc(*at.step(f"{L}.exp{h}.{u}"))

                def updates_out(b, u):
                    act.wait_ge(*at.done(f"{L}.UT.{u}"))
                    act.activation(UP[:, :, bass.ds(b * (2 * S) + u * S, S)],
                                   PS[:, 4 + u, 0:KC * S].rearrange("p (c k) -> p c k", c=KC), ACT.Copy)\
                        .then_inc(*at.step(f"{L}.ut.{u}"))

                with at.loop(act, L, B // 2) as b:
                    if it == 0:
                        squares(0)
                    scores_out(0, 0)
                    scores_out(0, 1)
                    exps(0, 0)
                    scores_out(1, 0)
                    exps(0, 1)
                    scores_out(1, 1)
                    if it == 0:
                        squares(1)
                    exps(1, 0)
                    exps(1, 1)
                    updates_out(b, 0)
                    updates_out(b, 1)
                linear_out(act, at, f"{p}.v", (0, 1, 2, 3), range(KC),
                           lambda ps, c: act.activation(SN[:, c, :], ps, ACT.Copy))
                for c in range(KC):
                    act.wait_ge(*at.done(f"{p}.r.{c}"))
                    act.wait_ge(*at.done("s1.bsum"))
                    act.activation(RG[:, c, :], bank(c), ACT.Sigmoid, bias=bsum[:, c:c + 1]).then_inc(*at.step(f"{p}.r.{c}.out"))
                for c in range(KC):
                    act.wait_ge(*at.done(f"{p}.z.{c}"))
                    act.activation(ZG[:, c, :], bank(c), ACT.Sigmoid, bias=bsum[:, 4 + c:5 + c]).then_inc(*at.step(f"{p}.z.{c}.out"))
                for c in range(KC):
                    act.wait_ge(*at.done(f"{p}.pre.{c}"))
                    act.activation(UP[:, c, :], UP[:, c, :], ACT.Tanh, bias=v("bih", 8 + c)).then_inc(*at.step(f"{p}.n.{c}"))

        def s1_dve(dve, at):
            dve.wait_ge(*at.done("consts"))
            dve.tensor_tensor(bsum[:, :], vec[:, VAT["bih"]:VAT["bih"] + 12], vec[:, VAT["bhh"]:VAT["bhh"] + 12], ALU.add)\
                .then_inc(*at.step("s1.bsum"))
            dve.tensor_scalar(inws[:, :], vec[:, VAT["in_w"]:VAT["in_w"] + 4], D ** -0.5, None, ALU.mult)\
                .then_inc(*at.step("s1.inws"))
            norm_dve(dve, at, "s1.ln", X, SL, 1e-5, xc=SN)
            for it in range(3):
                p, L = f"s1.{it}", f"s1.{it}.loop"
                norm_dve(dve, at, f"{p}.rms", SL, SN, 1e-6, w="slot_w", centred=False)
                for c in range(KC):
                    dve.wait_ge(*at.done(f"{p}.qk.{c}.out"))

                def slots(b, u):
                    dve.wait_ge(*at.done(f"{L}.S1.{u}", back=1))
                    dve.tensor_copy(qb[u], SN[:, :, bass.ds(b * (2 * S) + u * S, S)]).then_inc(*at.step(f"{L}.qb.{u}"))

                def inverse_rms(b, u):
                    dve.wait_ge(*at.done(f"{L}.ssq.{u}"))
                    dve.tensor_scalar(ssq[u], ssq[u], 1.0 / D, 1e-6, ALU.mult, ALU.add).then_inc(*at.step(f"{L}.msq.{u}"))
                    dve.wait_ge(*at.done(f"{L}.rms.{u}"))
                    dve.reciprocal(RN[:, b * 2 + u, :], ssq[u]).then_inc(*at.step(f"{L}.rinv.{u}"))
                    dve.wait_ge(*at.own())

                def spread(a, mt):
                    return a.unsqueeze(2).broadcast_to([P, mt, S])

                def shifted(b, u, h):
                    m0, mt = HALF[h]
                    x, mx = A_[u][:, m0:m0 + mt, :], stat[u][h][:, 0:mt]
                    dve.wait_ge(*at.done(f"{L}.T{h}.{u}"))
                    dve.wait_ge(*at.done(f"{L}.den.{u}", back=1))
                    dve.tensor_tensor(x, PS[:, 4 + h, 0:mt * S].rearrange("p (m k) -> p m k", k=S),
                                      spread(RN[:, b * 2 + u, m0:m0 + mt], mt), ALU.mult).then_inc(*at.step(f"{L}.st{h}.{u}"))
                    dve.wait_ge(*at.own())
                    dve.tensor_reduce(mx, x, AX.X, ALU.max).then_inc(*at.step())
                    dve.wait_ge(*at.own())
                    dve.tensor_tensor(x, x, spread(mx, mt), ALU.subtract).then_inc(*at.step(f"{L}.sub{h}.{u}"))

                def weights(b, u, h):
                    m0, mt = HALF[h]
                    x, sm = A_[u][:, m0:m0 + mt, :], stat[u][2 + h][:, 0:mt]
                    dve.wait_ge(*at.done(f"{L}.exp{h}.{u}"))
                    dve.tensor_reduce(sm, x, AX.X, ALU.add).then_inc(*at.step())
                    dve.wait_ge(*at.own())
                    dve.reciprocal(sm, sm).then_inc(*at.step())
                    dve.wait_ge(*at.own())
                    if h:
                        dve.tensor_tensor(sm[:, mt - 1:mt], sm[:, mt - 1:mt], row("in_last", 1), ALU.mult).then_inc(*at.step())
                        dve.wait_ge(*at.own())
                    dve.tensor_tensor(x, x, spread(sm, mt), ALU.mult).then_inc(*at.step())
                    dve.wait_ge(*at.own())
                    dve.wait_ge(*at.done(f"{L}.U.{u}", back=1))
                    dve.tensor_tensor(AR[u][:, m0:m0 + mt, :], x, spread(RN[:, b * 2 + u, m0:m0 + mt], mt), ALU.mult)\
                        .then_inc(*at.step(f"{L}.ar{h}.{u}"))
                    if h:
                        dve.tensor_reduce(asum[u], A_[u].rearrange("p m k -> p k m"), AX.X, ALU.add)\
                            .then_inc(*at.step(f"{L}.asum.{u}"))

                def normalise(u):
                    dve.wait_ge(*at.done(f"{L}.den.{u}"))
                    dve.tensor_scalar(rden[u], PS[0:S, 4 + u, 448:449], 1e-6, None, ALU.add).then_inc(*at.step())
                    dve.wait_ge(*at.own())
                    dve.reciprocal(rden[u], rden[u]).then_inc(*at.step())
                    dve.wait_ge(*at.own())
                    dve.wait_ge(*at.done(f"{L}.U.{u}"))
                    dve.wait_ge(*at.done(f"{L}.UT.{u}", back=1))
                    dve.tensor_scalar(UN[u], PS[0:S, 6 + u, :], rden[u], None, ALU.mult).then_inc(*at.step(f"{L}.un.{u}"))

                with at.loop(dve, L, B // 2) as b:
                    slots(b, 0)
                    slots(b, 1)
                    if it == 0:
                        inverse_rms(b, 0)
                    shifted(b, 0, 0)
                    shifted(b, 0, 1)
                    weights(b, 0, 0)
                    weights(b, 0, 1)
                    if it == 0:
                        inverse_rms(b, 1)
                    shifted(b, 1, 0)
                    shifted(b, 1, 1)
                    weights(b, 1, 0)
                    normalise(0)
                    weights(b, 1, 1)
                    normalise(1)
                dve.wait_ge(*at.done(f"{L}.ut.1"))
                for c in range(KC):
                    dve.tensor_scalar(UP[:, c, :], UP[:, c, :], v("in_w", c), None, ALU.mult).then_inc(*at.step(f"{p}.utw"))
                for c in range(KC):
                    dve.wait_ge(*at.done(f"{p}.gh.{c}"))
                    dve.wait_ge(*at.done(f"{p}.r.{c}.out"))
                    dve.scalar_tensor_tensor(out=UP[:, c, :], in0=bank(c), scalar=v("bhh", 8 + c), in1=RG[:, c, :],
                                             op0=ALU.add, op1=ALU.mult).then_inc(*at.step(f"{p}.gh.{c}.out"))
                    dve.wait_ge(*at.own())
                    dve.wait_ge(*at.done(f"{p}.gx.{c}"))
                    dve.tensor_tensor(UP[:, c, :], UP[:, c, :], bank(4 + c), ALU.add).then_inc(*at.step(f"{p}.pre.{c}"))
                    at.same(f"{p}.gx.{c}.out", f"{p}.pre.{c}")
                for c in range(KC):
                    dve.wait_ge(*at.done(f"{p}.n.{c}"))
                    dve.wait_ge(*at.done(f"{p}.z.{c}.out"))
                    dve.wait_ge(*at.done(f"{p}.gh.3"))
                    dve.tensor_tensor(SL[:, c, :], SL[:, c, :], UP[:, c, :], ALU.subtract).then_inc(*at.step())
                    dve.wait_ge(*at.own())
                    dve.tensor_tensor(SL[:, c, :], SL[:, c, :], ZG[:, c, :], ALU.mult).then_inc(*at.step())
                    dve.wait_ge(*at.own())
                    dve.tensor_tensor(SL[:, c, :], SL[:, c, :], UP[:, c, :], ALU.add).then_inc(*at.step(f"{p}.sl"))
            dve.wait_ge(*at.own())
            dve.tensor_tensor(X[:, :, :], X[:, :, :], SL[:, :, :], ALU.add).then_inc(*at.step("x1"))

        def high_at(k):
            return WH[2] if k == 0 else WH[k % 2]

        def triple(pe, ps, w, k, c, oc, xh, xl, start, stop):
            a, b = high_at(k)[:, c, oc * P:(oc + 1) * P], ring_part[slot[w]][:, c, oc * P:(oc + 1) * P]
            pe.matmul(ps, a, xh, start=start, stop=False)
            pe.matmul(ps, a, xl, start=False, stop=False)
            return pe.matmul(ps, b, xh, start=False, stop=stop)

        def expert_pe(pe, at, tag, w, inloop):
            def hidden(s, k):
                pe.wait_ge(*at.done(w(k) + ".low"))
                for oc in range(KC):
                    if s:
                        pe.wait_ge(*at.done(f"{tag}.h{s - 1}.{oc}.out"))
                    elif inloop:
                        pe.wait_ge(*at.done(f"{tag}.h3.{oc}.out", back=1))
                    for c in range(KC):
                        mm = triple(pe, bank(oc), w(k), k, c, oc, XH[:, c, :], XL[:, c, :], c == 0, c == KC - 1)
                    mm.then_inc(*at.step(f"{tag}.h{s}.{oc}"))
                at.same(w(k) + ".used", f"{tag}.h{s}.3")

            def output(s, k):
                pe.wait_ge(*at.done(w(k) + ".low"))
                for oc in range(KC):
                    if s == 0 and inloop:
                        pe.wait_ge(*at.done(f"{tag}.y{oc}.out", back=1))
                    for c in range(KC):
                        if oc == 0:
                            pe.wait_ge(*at.done(f"{tag}.h{s}.{c}.low"))
                        mm = triple(pe, bank(4 + oc), w(k), k, c, oc, HH[s % 2][:, c, :], HL[s % 2][:, c, :],
                                    s == 0 and c == 0, s == FS - 1 and c == KC - 1)
                    if s == FS - 1:
                        mm.then_inc(*at.step(f"{tag}.y{oc}"))
                if s < FS - 1:
                    mm.then_inc(*at.step(f"{tag}.Y{s}"))
                else:
                    at.same(f"{tag}.Y{s}", f"{tag}.y3")
                at.same(w(k) + ".used", f"{tag}.Y{s}")

            for k, x in enumerate(EXPERT):
                (hidden if x[0] == "a" else output)(int(x[1]), k)

        def expert_act(act, at, tag, w, func, bias, raw, inloop):
            def high(k):
                act.wait_ge(*at.done(w(k)))
                if k >= 3:
                    act.wait_ge(*at.done(w(k - 2) + ".used"))
                elif inloop:
                    act.wait_ge(*at.done(w((0, 7, 6)[k]) + ".used", back=1))
                act.activation(high_at(k)[:, :, :], wt(w(k))[:, :, :], ACT.Copy).then_inc(*at.step(w(k) + ".high"))

            high(0)
            for k, x in enumerate(EXPERT):
                if k + 1 < len(EXPERT):
                    high(k + 1)
                if x[0] != "a":
                    continue
                s = int(x[1])
                if s >= 2:
                    act.wait_ge(*at.done(f"{tag}.Y{s - 2}"))
                elif inloop:
                    act.wait_ge(*at.done(f"{tag}.Y{s + 2}", back=1))
                for oc in range(KC):
                    act.wait_ge(*at.done(f"{tag}.h{s}.{oc}"))
                    if s:
                        act.wait_ge(*at.done(f"{tag}.h{s - 1}.{oc}.low"))
                    elif inloop:
                        act.wait_ge(*at.done(f"{tag}.h3.{oc}.low", back=1))
                    act.activation(raw[:, oc, :], bank(oc), func, bias=bias(4 * s + oc)).then_inc(*at.step())
                    act.activation(HH[s % 2][:, oc, :], bank(oc), func, bias=bias(4 * s + oc)).then_inc(*at.step(f"{tag}.h{s}.{oc}.out"))

        def first_low_pool(pool, at, w):
            pool.wait_ge(*at.done(w(0) + ".high"))
            pool.tensor_tensor(ring_part[slot[w(0)]][:, :, :], wt(w(0))[:, :, :], high_at(0)[:, :, :].bitcast(FP32),
                               ALU.subtract).then_inc(*at.step(w(0) + ".low"))

        def expert_dve(dve, at, tag, w, raw):
            for k, x in enumerate(EXPERT):
                if k + 1 < len(EXPERT):
                    dve.wait_ge(*at.done(w(k + 1) + ".high"))
                    dve.tensor_tensor(ring_part[slot[w(k + 1)]][:, :, :], wt(w(k + 1))[:, :, :], high_at(k + 1)[:, :, :].bitcast(FP32),
                                      ALU.subtract).then_inc(*at.step(w(k + 1) + ".low"))
                if x[0] == "a":
                    s = int(x[1])
                    for oc in range(KC):
                        dve.wait_ge(*at.done(f"{tag}.h{s}.{oc}.out"))
                        dve.tensor_tensor(HL[s % 2][:, oc, :], raw[:, oc, :], HH[s % 2][:, oc, :].bitcast(FP32),
                                          ALU.subtract).then_inc(*at.step(f"{tag}.h{s}.{oc}.low"))

        def split_act(act, at, tag, x):
            for c in range(KC):
                act.activation(XH[:, c, :], x[:, c, :], ACT.Copy).then_inc(*at.step(f"{tag}.high{c}"))

        def split_dve(dve, at, tag, x):
            for c in range(KC):
                dve.wait_ge(*at.done(f"{tag}.high{c}"))
                dve.tensor_tensor(XL[:, c, :], x[:, c, :], XH[:, c, :].bitcast(FP32), ALU.subtract).then_inc(*at.step(f"{tag}.split"))

        pw = RC[:, 2560:2560 + S * KC * N_STATE].rearrange("p (j c n) -> p j c n", j=S, c=KC)
        abc = RC[:, 1600:1792].rearrange("p (a c n) -> p a c n", a=3, c=KC)
        R2, N2, Y2 = TS[0], TS[1], TS[2]

        CONV_DVE = 2
        CONV_PE = range(CONV_DVE, KC)
        LAGS = 8
        xn, y = (a[:, :, :].rearrange("p c (b s) -> p c b s", b=B) for a in (N2, Y2))

        def diag(c, j):
            k = ((c - CONV_DVE) * S + j) % (3 * LAGS)
            return RB[:, k * P:(k + 1) * P]

        def FFN(k):
            return f"s2.ffn{1 if EXPERT[k][0] == 'a' else 2}_{EXPERT[k][1]}"

        def s2_pool(pool, at):
            pool.wait_ge(*at.done("s2.decay"))
            pool.tensor_tensor(pw[:, 0], abc[:, 1], abc[:, 2], ALU.mult).then_inc(*at.step())
            for j in range(1, S):
                pool.wait_ge(*at.own())
                pool.tensor_tensor(pw[:, j], pw[:, j - 1], abc[:, 0], ALU.mult).then_inc(*at.step("s2.powers"))
            first_low_pool(pool, at, FFN)

        def s2_pe(pe, at):
            norm_pe(pe, at, "s2.ln", X, ["x1"] if 1 in stages else ["x"])
            norm_pe(pe, at, "s2.ln1", R2, ["s2.ln.done"])
            pe.wait_ge(*at.done("s2.ln1.done"))
            for c in CONV_PE:
                if bank_reader.get(c):
                    pe.wait_ge(*at.done(bank_reader[c]))
                y = bank(c).rearrange("p (b s) -> p b s", b=B)
                for j in range(S):
                    if j % LAGS == 0:
                        pe.wait_ge(*at.done(f"s2.diag.{c}.{j // LAGS}"))
                    mm = pe.matmul(y[:, :, j:S], diag(c, j), xn[:, c, :, 0:S - j], start=(j == 0), stop=(j == S - 1))
                    if j % LAGS == LAGS - 1:
                        mm.then_inc(*at.step(f"s2.lags.{c}.{j // LAGS}"))
                bank_reader[c] = "s2.silu"
            linear_pe(pe, at, "s2.out", [("s2.out", Y2)], (0, 1, 2, 3), range(KC), ["s2.silu"])
            norm_pe(pe, at, "s2.ln2", R2, ["s2.res"])
            for due in at.last("s2.split", *(f"s2.out.{c}.out" for c in range(KC))):
                pe.wait_ge(*due)
            expert_pe(pe, at, "s2.ffn", FFN, False)
            bank_reader.update({k: f"s2.ffn.h3.{k}.out" for k in range(4)})
            bank_reader.update({4 + k: f"s2.ffn.y{k}.out" for k in range(4)})

        def s2_act(act, at):
            for due in at.last("abc", "s1.bsum" if 1 in stages else "consts"):
                act.wait_ge(*due)
            if 1 in stages:
                act.wait_ge(*at.done("x1"))
            act.activation(abc[:, 0], abc[:, 0], ACT.Sigmoid).then_inc(*at.step("s2.decay"))
            norm_act(act, at, "s2.ln", X, xc=N2)
            norm_act(act, at, "s2.ln1", R2, xc=N2)
            act.wait_ge(*at.done("s2.response"))
            groups = [(c, g) for c in CONV_PE for g in range(S // LAGS)]
            for n, (c, g) in enumerate(groups):
                if n >= 3:
                    act.wait_ge(*at.done("s2.lags.{}.{}".format(*groups[n - 3])))
                for j in range(g * LAGS, (g + 1) * LAGS):
                    act.activation(diag(c, j), C["ident"], ACT.Copy, scale=kconv[:, c, j:j + 1]).then_inc(*at.step(f"s2.diag.{c}.{g}"))
            for c in CONV_PE:
                act.wait_ge(*at.done(f"s2.lags.{c}.{S // LAGS - 1}"))
                act.activation(Y2[:, c, :], bank(c), ACT.Silu).then_inc(*at.step())
            act.wait_ge(*at.done("s2.conv"))
            act.activation(Y2[:, 0:CONV_DVE, :], Y2[:, 0:CONV_DVE, :], ACT.Silu).then_inc(*at.step("s2.silu"))
            norm_act(act, at, "s2.ln2", R2, xc=N2)
            act.wait_ge(*at.done("s2.ln2.done"))
            split_act(act, at, "s2", N2)
            expert_act(act, at, "s2.ffn", FFN, ACT.Gelu, lambda k: v("ffn1_b", k), TS[3], False)

        def s2_dve(dve, at):
            norm_dve(dve, at, "s2.ln", X, R2, 1e-5, xc=N2)
            dve.wait_ge(*at.own())
            norm_dve(dve, at, "s2.ln1", R2, N2, 1e-5, w="ln_w", b="ln_b", xc=N2)
            dve.wait_ge(*at.done("s2.powers"))
            dve.tensor_reduce(kconv[:, :, :].rearrange("p c j -> p j c"), pw, AX.X, ALU.add).then_inc(*at.step())
            dve.wait_ge(*at.own())
            dve.tensor_tensor(kconv[:, :, 0:1], kconv[:, :, 0:1], vec[:, VAT["D"]:VAT["D"] + 4].unsqueeze(2), ALU.add).then_inc(*at.step("s2.response"))
            dve.wait_ge(*at.own())
            for c in range(CONV_DVE):
                dve.tensor_scalar(Y2[:, c, :], N2[:, c, :], kconv[:, c, 0:1], None, ALU.mult).then_inc(*at.step("s2.conv"))
            for j in range(1, S):
                for c in range(CONV_DVE):
                    dve.wait_ge(sems["vector_done"], at.count["vector_done"] - CONV_DVE + 1)
                    dve.scalar_tensor_tensor(out=y[:, c, :, j:S], in0=xn[:, c, :, 0:S - j], scalar=kconv[:, c, j:j + 1],
                                                 in1=y[:, c, :, j:S], op0=ALU.mult, op1=ALU.add).then_inc(*at.step("s2.conv"))
            for c in range(KC):
                dve.wait_ge(*at.done(f"s2.out.{c}"))
                dve.scalar_tensor_tensor(out=R2[:, c, :], in0=bank(c), scalar=v("out_b", c), in1=R2[:, c, :],
                                             op0=ALU.add, op1=ALU.add).then_inc(*at.step(f"s2.out.{c}.out"))
            at.same("s2.res", "s2.out.3.out")
            dve.wait_ge(*at.own())
            norm_dve(dve, at, "s2.ln2", R2, N2, 1e-5, w="ln2_w", b="ln2_b", xc=N2)
            split_dve(dve, at, "s2", N2)
            for c in range(KC):
                dve.tensor_tensor(X[:, c, :], X[:, c, :], R2[:, c, :], ALU.add).then_inc(*at.step())
            expert_dve(dve, at, "s2.ffn", FFN, TS[3])
            for c in range(KC):
                dve.wait_ge(*at.done(f"s2.ffn.y{c}"))
                dve.wait_ge(*at.own())
                dve.scalar_tensor_tensor(out=X[:, c, :], in0=bank(4 + c), scalar=v("ffn2_b", c), in1=X[:, c, :],
                                             op0=ALU.add, op1=ALU.add).then_inc(*at.step(f"s2.ffn.y{c}.out"))
            at.same("x2", "s2.ffn.y3.out")

        KBD = [RB4[0], RB4[1]]
        SC, PT = RC4[0], RC4[1]
        probs = SC.rearrange("p c (h k) -> p (c h) k", k=P)
        probsT = PT.rearrange("p c (h k) -> p (c h) k", k=P)
        NBP = T // P

        def attn_pool(pool, at, tag, K, ready):
            for x in KBD:
                pool.memset(x[:, :, :], 0.0).then_inc(*at.step(f"{tag}.zero"))
            pool.wait_ge(*at.own())
            for due in at.last(*ready):
                pool.wait_ge(*due)
            for bp in range(NBP):
                if bp >= 2:
                    pool.wait_ge(*at.done(f"{tag}.S{bp - 2}"))
                for a in range(G):
                    pool.tensor_copy(KBD[bp % 2][a * HD:(a + 1) * HD, :, a * P:(a + 1) * P],
                                        K[a * HD:(a + 1) * HD, :, bp * P:(bp + 1) * P]).then_inc(*at.step(f"{tag}.kb{bp}"))

        def attn_pe(pe, at, tag, Q, V, ready):
            def scores(bp):
                pe.wait_ge(*at.done(f"{tag}.kb{bp}"))
                for g in range(KC):
                    if bp:
                        pe.wait_ge(*at.done(f"{tag}.masked{bp - 1}"))
                    elif bank_reader.get(g):
                        pe.wait_ge(*at.done(bank_reader[g]))
                    mm = pe.matmul(bank(g), Q[:, g, bp * P:(bp + 1) * P], KBD[bp % 2][:, g, :], start=True, stop=True)
                mm.then_inc(*at.step(f"{tag}.S{bp}"))

            def values(bp):
                pe.wait_ge(*at.done(f"{tag}.p{bp}"))
                for g in range(KC):
                    k = 4 + g % 3
                    if bank_reader.get(k):
                        pe.wait_ge(*at.done(bank_reader[k]))
                    for a in range(G):
                        mm = pe.transpose(PS[:, k, a * P:(a + 1) * P], probs[:, G * g + a, :], C["ident"])
                    mm.then_inc(*at.step(f"{tag}.T{bp}.{g}"))
                    bank_reader[k] = f"{tag}.T{bp}.{g}.out"
                if bank_reader.get(7):
                    pe.wait_ge(*at.done(bank_reader[7]))
                for g in range(KC):
                    pe.wait_ge(*at.done(f"{tag}.T{bp}.{g}.out"))
                    for a in range(G):
                        h = G * g + a
                        mm = pe.matmul(PS[a * HD:(a + 1) * HD, 7, g * P:(g + 1) * P], V[:, bp, h * HD:(h + 1) * HD],
                                          probsT[:, h, :], start=True, stop=True)
                mm.then_inc(*at.step(f"{tag}.O{bp}"))
                bank_reader[7] = f"{tag}.O{bp}.out"

            for due in at.last(*ready):
                pe.wait_ge(*due)
            scores(0)
            for bp in range(NBP):
                if bp + 1 < NBP:
                    scores(bp + 1)
                values(bp)
            for g in range(KC):
                bank_reader[g] = f"{tag}.masked{NBP - 1}"

        def attn_act(act, at, tag):
            for bp in range(NBP):
                act.wait_ge(*at.done(f"{tag}.sub{bp}"))
                act.activation(SC[:, :, :], SC[:, :, :], ACT.Exp).then_inc(*at.step(f"{tag}.exp{bp}"))
                for g in range(KC):
                    act.wait_ge(*at.done(f"{tag}.T{bp}.{g}"))
                    if bp:
                        act.wait_ge(*at.done(f"{tag}.O{bp - 1}"))
                    act.activation(PT[:, g, :], bank(4 + g % 3), ACT.Copy).then_inc(*at.step(f"{tag}.T{bp}.{g}.out"))

        def attn_dve(dve, at, tag, O, mask):
            mx, sm = misc[:, 0:H], misc[:, 16:16 + H]
            for bp in range(NBP):
                dve.wait_ge(*at.done(f"{tag}.S{bp}"))
                if bp:
                    dve.wait_ge(*at.done(f"{tag}.T{bp - 1}.3"))
                dve.scalar_tensor_tensor(out=probs, in0=PS[:, 0:4, :].rearrange("p g (a k) -> p (g a) k", k=P),
                                             scalar=HD ** -0.5, in1=mask.unsqueeze(1).broadcast_to([P, H, P]),
                                             op0=ALU.mult, op1=ALU.add).then_inc(*at.step(f"{tag}.masked{bp}"))
                dve.wait_ge(*at.own())
                dve.tensor_reduce(mx, probs, AX.X, ALU.max).then_inc(*at.step())
                dve.wait_ge(*at.own())
                dve.tensor_tensor(probs, probs, mx.unsqueeze(2).broadcast_to([P, H, P]), ALU.subtract).then_inc(*at.step(f"{tag}.sub{bp}"))
                dve.wait_ge(*at.done(f"{tag}.exp{bp}"))
                dve.tensor_reduce(sm, probs, AX.X, ALU.add).then_inc(*at.step())
                dve.wait_ge(*at.own())
                dve.reciprocal(sm, sm).then_inc(*at.step())
                dve.wait_ge(*at.own())
                dve.tensor_tensor(probs, probs, sm.unsqueeze(2).broadcast_to([P, H, P]), ALU.mult).then_inc(*at.step(f"{tag}.p{bp}"))
                dve.wait_ge(*at.done(f"{tag}.O{bp}"))
                dve.tensor_copy(O[:, :, bp * P:(bp + 1) * P], PS[:, 7, :].rearrange("p (g k) -> p g k", k=P)).then_inc(*at.step(f"{tag}.O{bp}.out"))

        def values_pe(pe, at, tag, w, x, banks):
            for tt in range(T // P):
                k = banks[tt % len(banks)]
                if bank_reader.get(k):
                    pe.wait_ge(*at.done(bank_reader[k]))
                if tt == 0:
                    pe.wait_ge(*at.done(w))
                for c in range(KC):
                    mm = pe.matmul(bank(k), x[:, c, tt * P:(tt + 1) * P], wt(w)[:, c, :], start=(c == 0), stop=(c == KC - 1))
                mm.then_inc(*at.step(f"{tag}.{tt}"))
                bank_reader[k] = f"{tag}.{tt}.out"
            at.same(w + ".used", f"{tag}.3")

        def values_dve(dve, at, tag, V, bias, banks):
            for tt in range(T // P):
                dve.wait_ge(*at.done(f"{tag}.{tt}"))
                dve.tensor_tensor(V[:, tt, :], bank(banks[tt % len(banks)]), row(bias, D), ALU.add).then_inc(*at.step(f"{tag}.{tt}.out"))

        XPAD = RC[:, 4200:4200 + KC * B * (S + 2)].rearrange("p (c b s) -> p c b s", c=KC, b=B)
        X3, Q3, K3, V3, O3 = TS[1], TS[2], TS[3], TS[4], TS[0]

        def MOE(k):
            return f"s3.moe.{EXPERT[k]}"

        PB = RA[:, 0:E_ * T].rearrange("p (e t) -> p e t", e=E_)
        gl = misc[:, 64:96].rearrange("p (a e) -> p a e", e=E_)
        gm, gs = misc[:, 96:100], misc[:, 100:104]
        gT = misc[0:E_, 0:0 + 512]
        ga = RC[:, 0:32].rearrange("p (a e) -> p a e", e=E_)
        gst = RC[:, 64:128]

        def gate_pe(pe, at, tag, x, w, after):
            for due in at.last(*after):
                pe.wait_ge(*due)
            if bank_reader.get(0):
                pe.wait_ge(*at.done(bank_reader[0]))
            for tt in range(T // P):
                for c in range(KC):
                    mm = pe.matmul(PS[:, 0, tt * E_:(tt + 1) * E_], x[:, c, tt * P:(tt + 1) * P], gw[:, w, c, :],
                                      start=(c == 0), stop=(c == KC - 1))
            mm.then_inc(*at.step(f"{tag}.logits"))
            bank_reader[0] = f"{tag}.logits.out"

        def gate_act(act, at, tag):
            act.wait_ge(*at.done(f"{tag}.sub"))
            act.activation(ga, ga, ACT.Exp).then_inc(*at.step(f"{tag}.exp"))

        def gate_dve(dve, at, tag, bias):
            ps = PS[:, 0, 0:32].rearrange("p (a e) -> p a e", e=E_)
            bc = lambda a: a.unsqueeze(2).broadcast_to([P, 4, E_])
            dve.wait_ge(*at.done(f"{tag}.logits"))
            if bias:
                dve.tensor_tensor(ga, ps, row("gate_b", E_).unsqueeze(1).broadcast_to([P, 4, E_]), ALU.add).then_inc(*at.step(f"{tag}.logits.out"))
            else:
                dve.tensor_copy(ga, ps).then_inc(*at.step(f"{tag}.logits.out"))
            dve.wait_ge(*at.own())
            dve.tensor_reduce(gst[:, 0:4], ga, AX.X, ALU.max).then_inc(*at.step())
            dve.wait_ge(*at.own())
            dve.tensor_tensor(ga, ga, bc(gst[:, 0:4]), ALU.subtract).then_inc(*at.step(f"{tag}.sub"))
            dve.wait_ge(*at.done(f"{tag}.exp"))
            dve.tensor_reduce(gst[:, 4:8], ga, AX.X, ALU.add).then_inc(*at.step())
            dve.wait_ge(*at.own())
            dve.reciprocal(gst[:, 4:8], gst[:, 4:8]).then_inc(*at.step())
            dve.wait_ge(*at.own())
            dve.tensor_tensor(ga, ga, bc(gst[:, 4:8]), ALU.mult).then_inc(*at.step(f"{tag}.probs"))

        def s3_pool(pool, at):
            if 2 in stages:
                pool.wait_ge(*at.done("x2"))
            pool.memset(XPAD[:, :, :, 0:1], 0.0).then_inc(*at.step())
            pool.memset(XPAD[:, :, :, S + 1:S + 2], 0.0).then_inc(*at.step("s3.pad"))
            attn_pool(pool, at, "s3.at", K3, [f"s3.k.{c}.out" for c in range(KC)])
            with at.loop(pool, "s3.loop", E_) as i:
                first_low_pool(pool, at, MOE)

        def s3_pe(pe, at):
            norm_pe(pe, at, "s3.ln", X, ["x2"] if 2 in stages else ["x"])
            for due in at.last("s3.padded", "s3.pad"):
                pe.wait_ge(*due)
            for oc in range(KC):
                if bank_reader.get(oc):
                    pe.wait_ge(*at.done(bank_reader[oc]))
                for k in range(3):
                    if oc == 0:
                        pe.wait_ge(*at.done(f"s3.conv{k}"))
                    for c in range(KC):
                        mm = pe.matmul(bank(oc), wt(f"s3.conv{k}")[:, c, oc * P:(oc + 1) * P], XPAD[:, c, :, k:k + S],
                                          start=(k == 0 and c == 0), stop=(k == 2 and c == KC - 1))
                mm.then_inc(*at.step(f"s3.cv.{oc}"))
                bank_reader[oc] = f"s3.cv.{oc}.out"
            for k in range(3):
                at.same(f"s3.conv{k}.used", "s3.cv.3")
            cv = [f"s3.cv.{c}.out" for c in range(KC)]
            linear_pe(pe, at, "s3.q", [("s3.wq", X3)], (4, 5, 6, 7), range(KC), cv)
            linear_pe(pe, at, "s3.k", [("s3.wk", X3)], (0, 1, 2, 3), range(KC))
            values_pe(pe, at, "s3.v", "s3.wv", X3, (4, 5, 6, 7))
            attn_pe(pe, at, "s3.at", Q3, V3, [f"s3.q.{c}.out" for c in range(KC)] + [f"s3.v.{c}.out" for c in range(4)])
            linear_pe(pe, at, "s3.o", [("s3.wo", O3)], (0, 1, 2, 3), range(KC), ["s3.at.O3.out"])
            norm_pe(pe, at, "s3.ln1", X3, [f"s3.o.{c}.out" for c in range(KC)])
            gate_pe(pe, at, "s3.g", X3, 0, ["s3.ln1.done"])
            pe.wait_ge(*at.done("s3.g.probs"))
            for tt in range(4):
                mm = pe.transpose(PS[0:E_, 1, tt * P:(tt + 1) * P], ga[:, tt, :], C["ident"])
            mm.then_inc(*at.step("s3.gT"))
            pe.wait_ge(*at.done("s3.gT.out"))
            for x in range(E_):
                k = 2 + x % 2
                if x >= 2:
                    pe.wait_ge(*at.done(f"s3.pb.{x - 2}.out"))
                mm = pe.matmul(bank(k), C["ident"][0:E_, x:x + 1].broadcast_to([E_, P]), gT, start=True, stop=True)
                mm.then_inc(*at.step(f"s3.pb.{x}"))
            for due in at.last("s3.pb.6.out", "s3.pb.7.out", "s3.split"):
                pe.wait_ge(*due)
            with at.loop(pe, "s3.loop", E_) as i:
                expert_pe(pe, at, "s3.moe", MOE, True)
            bank_reader.update({k: f"s3.moe.h3.{k}.out" for k in range(4)})
            bank_reader.update({4 + k: f"s3.moe.y{k}.out" for k in range(4)})
            norm_pe(pe, at, "s3.ln2", X3, ["s3.x5"])

        def s3_act(act, at):
            norm_act(act, at, "s3.ln", X, xc=TS[0])
            linear_out(act, at, "s3.cv", (0, 1, 2, 3), range(KC), lambda ps, c: act.activation(X3[:, c, :], ps, ACT.Identity, bias=v("conv_b", c)))
            linear_out(act, at, "s3.q", (4, 5, 6, 7), range(KC), lambda ps, c: act.activation(Q3[:, c, :], ps, ACT.Identity, bias=v("bqkv", c)))
            linear_out(act, at, "s3.k", (0, 1, 2, 3), range(KC), lambda ps, c: act.activation(K3[:, c, :], ps, ACT.Identity, bias=v("bqkv", 4 + c)))
            attn_act(act, at, "s3.at")
            norm_act(act, at, "s3.ln1", X3, xc=X3)
            act.wait_ge(*at.done("s3.ln1.done"))
            split_act(act, at, "s3", X3)
            gate_act(act, at, "s3.g")
            act.wait_ge(*at.done("s3.gT"))
            act.activation(gT, PS[0:E_, 1, :], ACT.Copy).then_inc(*at.step("s3.gT.out"))
            for x in range(E_):
                act.wait_ge(*at.done(f"s3.pb.{x}"))
                act.activation(PB[:, x, :], bank(2 + x % 2), ACT.Copy).then_inc(*at.step(f"s3.pb.{x}.out"))
            with at.loop(act, "s3.loop", E_) as i:
                expert_act(act, at, "s3.moe", MOE, ACT.Relu, lambda k: vec[:, bass.ds(i * 16 + (VAT["b1"] + k), 1)], TS[0], True)
            norm_act(act, at, "s3.ln2", X3, xc=X3)

        def s3_dve(dve, at):
            norm_dve(dve, at, "s3.ln", X, TS[0], 1e-5, xc=TS[0])
            dve.wait_ge(*at.own())
            dve.tensor_copy(XPAD[:, :, :, 1:S + 1].rearrange("p c b s -> p (c b) s"),
                                TS[0][:, :, :].rearrange("p c (b s) -> p (c b) s", s=S)).then_inc(*at.step("s3.padded"))
            values_dve(dve, at, "s3.v", V3, "bv3", (4, 5, 6, 7))
            attn_dve(dve, at, "s3.at", O3, C["blockmask"])
            for c in range(KC):
                dve.wait_ge(*at.done(f"s3.o.{c}"))
                dve.scalar_tensor_tensor(out=X3[:, c, :], in0=bank(c), scalar=v("bo3", c), in1=X3[:, c, :],
                                             op0=ALU.add, op1=ALU.add).then_inc(*at.step(f"s3.o.{c}.out"))
            dve.wait_ge(*at.own())
            norm_dve(dve, at, "s3.ln1", X3, X3, 1e-5, w="ln1_g", b="ln1_b", xc=X3)
            gate_dve(dve, at, "s3.g", True)
            split_dve(dve, at, "s3", X3)
            acc, tmp = TS[2], TS[3]
            dve.memset(acc[:, :, :], 0.0).then_inc(*at.step("s3.acc0"))
            dve.wait_ge(*at.done("s3.pb.7.out"))
            with at.loop(dve, "s3.loop", E_) as i:
                expert_dve(dve, at, "s3.moe", MOE, TS[0])
                for c in range(KC):
                    dve.wait_ge(*at.done(f"s3.moe.y{c}"))
                    dve.wait_ge(*at.own())
                    dve.scalar_tensor_tensor(out=tmp[:, c, :], in0=bank(4 + c), scalar=vec[:, bass.ds(i * 4 + (VAT["b2"] + c), 1)],
                                                 in1=PB[:, i, :], op0=ALU.add, op1=ALU.mult).then_inc(*at.step(f"s3.moe.y{c}.out"))
                    dve.wait_ge(*at.own())
                    dve.tensor_tensor(acc[:, c, :], acc[:, c, :], tmp[:, c, :], ALU.add).then_inc(*at.step())
            dve.wait_ge(*at.own())
            dve.wait_ge(*at.done("s3.moe.y3"))
            dve.tensor_tensor(X3[:, :, :], X3[:, :, :], acc[:, :, :], ALU.add).then_inc(*at.step("s3.x5"))
            dve.wait_ge(*at.own())
            norm_dve(dve, at, "s3.ln2", X3, acc, 1e-5, w="ln2_g", b="ln2b3", xc=X3)
            dve.wait_ge(*at.own())
            dve.tensor_tensor(X[:, :, :], X[:, :, :], acc[:, :, :], ALU.add).then_inc(*at.step("x3"))

        KT = RC[:, 0:KC * MP].rearrange("p (g m) -> p g m", g=KC)
        VT = RB[:, 0:MT * D].rearrange("p (m d) -> p m d", d=D)
        N4, Q4, O4 = TS[0], TS[2], TS[3]
        qd = TS[1][:, 2:4, :].rearrange("p a b -> p (a b)").rearrange("p (g h q) -> p g h q", g=KC, h=G)
        QD = TS[1][:, 2:4, :].rearrange("p a b -> p (a b)").rearrange("p (g r) -> p g r", g=KC)
        keep, flag = PTs[:, :, :].rearrange("p m k -> p (m k)"), misc[:, 0:1]
        NP = H // 2
        minus_max = [misc[:, 4:5], misc[:, 5:6]]
        top = [[misc[:, 8 + 2 * a + h:9 + 2 * a + h] for h in (0, 1)] for a in (0, 1)]
        total = [[misc[:, 12 + 2 * a + h:13 + 2 * a + h] for h in (0, 1)] for a in (0, 1)]
        TG = [(k, min(4, MT - k)) for k in range(0, MT, 4)]
        SCALE = HD ** -0.5
        W4 = {}
        if 4 in stages:
            W4 = {"wk": (ring_part[slot["s4.wo"]], ring_part[slot["s4.wk"]]), "wv": (ring_part[slot["s4.wq"]], ring_part[slot["s4.wv"]])}

        def s4_pool(pool, at):
            if 3 in stages:
                pool.wait_ge(*at.done("s3.x5"))
            with at.loop(pool, "s4.loop", B) as b:
                for h in (0, 1):
                    m0, mt = HALF[h]
                    pool.wait_ge(*at.done(f"s4.V{h}", back=1))
                    pool.nop(nofuse=True)
                    pool.dma_start(CT[h][:, :, :], t["ctxT"][b, :, :, m0 * P:(m0 + mt) * P]).then_inc(*at.load(f"ctxT_loaded{h}", f"s4.ct{h}"))
                pool.wait_ge(*at.done("s4.ct0"))
                pool.wait_ge(*at.done("s4.ln.done"))
                pool.wait_ge(*at.done("s4.V0", back=1))
                pool.nop(nofuse=True)
                pool.tensor_copy(CH[0][:, :, :], CT[0][:, :, :]).then_inc(*at.step("s4.high0"))
                pool.wait_ge(*at.own())
                pool.tensor_tensor(CL[0][:, :, :], CT[0][:, :, :], CH[0][:, :, :].bitcast(FP32), ALU.subtract).then_inc(*at.step("s4.low0"))

        def s4_pe(pe, at):
            norm_pe(pe, at, "s4.ln", X, ["x3"] if 3 in stages else ["x"])
            linear_pe(pe, at, "s4.q", [("s4.wq", N4)], (0, 1, 2, 3), range(KC), ["s4.ln.done"])
            for due in at.last("s4.wk.low", "s4.wv.low", *(f"s4.q.{c}.out" for c in range(KC))):
                pe.wait_ge(*due)
            (wkh, wkl), (wvh, wvl) = W4["wk"], W4["wv"]

            def keys_values(h):
                m0, mt = HALF[h]
                w = mt * S
                pe.wait_ge(*at.done(f"s4.low{h}"))
                for oc in range(KC):
                    for j in (0, 1):
                        n = 2 * oc + j
                        if n >= 4:
                            pe.wait_ge(*at.done(f"s4.K{h}.{n - 4}.out"))
                        elif h:
                            pe.wait_ge(*at.done(f"s4.K0.{n + 4}.out"))
                        else:
                            pe.wait_ge(*at.done("s4.exp7.1", back=1))
                        for c in range(KC):
                            f, m = slice(oc * P, (oc + 1) * P), slice(j * w, (j + 1) * w)
                            pe.matmul(bank(n % 4, w), wkh[:, c, f], CH[h][:, c, m], start=(c == 0), stop=False)
                            pe.matmul(bank(n % 4, w), wkh[:, c, f], CL[h][:, c, m], start=False, stop=False)
                            mm = pe.matmul(bank(n % 4, w), wkl[:, c, f], CH[h][:, c, m], start=False, stop=(c == KC - 1))
                        mm.then_inc(*at.step(f"s4.K{h}.{n}"))
                for j in range(mt):
                    if j >= 2:
                        pe.wait_ge(*at.done(f"s4.V{h}.{j - 2}.out"))
                    elif h:
                        pe.wait_ge(*at.done(f"s4.V0.{HALF[0][1] - 2 + j}.out"))
                    else:
                        for due in at.last("s4.pt7.2.out", "s4.pt7.3.out", back=1):
                            pe.wait_ge(*due)
                    for c in range(KC):
                        k, m = 4 + (m0 + j) % 2, slice(j * P, (j + 1) * P)
                        pe.matmul(bank(k), CH[h][:, c, m], wvh[:, c, :], start=(c == 0), stop=False)
                        pe.matmul(bank(k), CH[h][:, c, m], wvl[:, c, :], start=False, stop=False)
                        mm = pe.matmul(bank(k), CL[h][:, c, m], wvh[:, c, :], start=False, stop=(c == KC - 1))
                    mm.then_inc(*at.step(f"s4.V{h}.{j}"))
                at.same(f"s4.V{h}", f"s4.V{h}.{mt - 1}")

            def scores(p):
                g, a = p // 2, p % 2
                if not p:
                    for due in at.last(*(f"s4.K{h}.{n}.out" for n in range(8) for h in (0, 1))):
                        pe.wait_ge(*due)
                    pe.wait_ge(*at.done("s4.qd"))
                for j in range(4):
                    if p and j % 2 == 0:
                        pe.wait_ge(*at.done(f"s4.exp{p - 1}.{j // 2}"))
                    pe.matmul(bank(j, MB), QD[:, g, a * P:(a + 1) * P], KT[:, g, j * MB:(j + 1) * MB], start=True, stop=False)
                    mm = pe.matmul(bank(j, MB), idb[:, :], maskneg[:, j * MB:(j + 1) * MB], start=False, stop=True)
                    if j % 2:
                        mm.then_inc(*at.step(f"s4.S{p}.{j // 2}"))
                at.same(f"s4.S{p}")

            def values(p):
                pe.wait_ge(*at.done(f"s4.p{p}"))
                a = p % 2

                def transposes(k):
                    m0, n = TG[k]
                    if k >= 2:
                        pe.wait_ge(*at.done(f"s4.pt{p}.{k - 2}.out"))
                    elif p:
                        pe.wait_ge(*at.done(f"s4.pt{p - 1}.{k + 2}.out"))
                    else:
                        for j in range(HALF[1][1] - 2, HALF[1][1]):
                            pe.wait_ge(*at.done(f"s4.V1.{j}.out"))
                    for j in range(n):
                        mm = pe.transpose(PS[:, 4 + k % 2, j * P:(j + 1) * P], PR[:, a, (m0 + j) * P:(m0 + j + 1) * P], C["ident"])
                    mm.then_inc(*at.step(f"s4.pt{p}.{k}"))

                transposes(0)
                transposes(1)
                if p >= 2:
                    pe.wait_ge(*at.done(f"s4.o{p - 2}.out"))
                else:
                    pe.wait_ge(*at.done(f"s4.o{p + 6}.out", back=1))
                for k, (m0, n) in enumerate(TG):
                    pe.wait_ge(*at.done(f"s4.pt{p}.{k}.out"))
                    for m in range(m0, m0 + n):
                        mm = pe.matmul(PS[a * 64:a * 64 + 64, 6 + a, 0:P], VT[:, m, p * 64:(p + 1) * 64], PTs[:, m, :],
                                          start=(m == 0), stop=(m == MT - 1))
                    if k + 2 < len(TG):
                        transposes(k + 2)
                mm.then_inc(*at.step(f"s4.o{p}"))

            with at.loop(pe, "s4.loop", B) as b:
                keys_values(0)
                keys_values(1)
                scores(0)
                for p in range(NP):
                    if p + 1 < NP:
                        scores(p + 1)
                    values(p)
            at.same("s4.wk.used", "s4.o7"); at.same("s4.wv.used", "s4.o7")
            bank_reader.update({k: "s4.exp7.1" for k in range(4)})
            bank_reader.update({4: "s4.pt7.2.out", 5: "s4.pt7.3.out", 6: "s4.o6.out", 7: "s4.o7.out"})
            linear_pe(pe, at, "s4.wo_", [("s4.wo", O4)], (0, 1, 2, 3), range(KC), ["s4.o7.out"])

        def s4_act(act, at):
            norm_act(act, at, "s4.ln", X, xc=TS[0])
            act.wait_ge(*at.done("s4.wk"))
            if before_wk_high:
                act.wait_ge(*at.done(before_wk_high + ".used"))
            act.activation(W4["wk"][0][:, :, :], wt("s4.wk")[:, :, :], ACT.Copy).then_inc(*at.step("s4.wk.high"))
            linear_out(act, at, "s4.q", (0, 1, 2, 3), range(KC), lambda ps, c: act.activation(Q4[:, c, :], ps, ACT.Identity, bias=v("bq4", c)))
            act.wait_ge(*at.done("s4.wv"))
            act.activation(W4["wv"][0][:, :, :], wt("s4.wv")[:, :, :], ACT.Copy).then_inc(*at.step("s4.wv.high"))
            act.wait_ge(*at.done("s4.flag"))
            with at.loop(act, "s4.loop", B) as b:
                for h in (0, 1):
                    m0, mt = HALF[h]
                    w = mt * S
                    act.wait_ge(*at.done("s4.S7", back=1))
                    for n in range(8):
                        act.wait_ge(*at.done(f"s4.K{h}.{n}"))
                        act.activation(KT[:, n // 2, m0 * P + (n % 2) * w:m0 * P + (n % 2 + 1) * w], bank(n % 4, w),
                                           ACT.Identity, bias=v("bk4", n // 2)).then_inc(*at.step(f"s4.K{h}.{n}.out"))
                        if h == 0 and n < KC:
                            act.wait_ge(*at.done("s4.ct1"))
                            act.wait_ge(*at.done("s4.V1", back=1))
                            act.activation(CH[1][:, n, :], CT[1][:, n, :], ACT.Copy).then_inc(*at.step(f"s4.high1.{n}"))
                for p in range(NP):
                    act.wait_ge(*at.done(f"s4.max{p}"))
                    if p >= 2:
                        act.wait_ge(*at.done(f"s4.pt{p - 2}.3"))
                    else:
                        act.wait_ge(*at.done(f"s4.pt{p + 6}.3", back=1))
                    for h in (0, 1):
                        act.activation(PR[:, p % 2, 2 * h * MB:2 * (h + 1) * MB].rearrange("p (a m) -> p a m", a=2), PS[:, 2 * h:2 * h + 2, 0:MB],
                                       ACT.Exp, bias=minus_max[p % 2], scale=SCALE, accum_out=total[p % 2][h]).then_inc(*at.step(f"s4.exp{p}.{h}"))
                    for k, (m0, n) in enumerate(TG[:2]):
                        act.wait_ge(*at.done(f"s4.pt{p}.{k}"))
                        if p:
                            act.wait_ge(*at.done(f"s4.o{p - 1}"))
                        act.activation(PTs[:, m0:m0 + n, :], PS[:, 4 + k % 2, 0:n * P].rearrange("p (m q) -> p m q", q=P),
                                           ACT.Copy).then_inc(*at.step(f"s4.pt{p}.{k}.out"))

        def s4_dve(dve, at):
            dve.wait_ge(*at.done("mask"))
            if 1 in stages:
                dve.wait_ge(*at.done("x1"))
            dve.tensor_scalar(keep, PR[:, 0, :].bitcast(I32), 0, None, ALU.not_equal).then_inc(*at.step())
            dve.wait_ge(*at.own())
            dve.tensor_scalar(maskneg[:, :], keep, -NEG, NEG, ALU.mult, ALU.add).then_inc(*at.step())
            dve.tensor_reduce(flag, keep, AX.X, ALU.max).then_inc(*at.step())
            dve.memset(TS[1][:, 2:4, :], 0.0).then_inc(*at.step("s4.flag"))
            norm_dve(dve, at, "s4.ln", X, N4, 1e-5, xc=N4)
            for w in ("wk", "wv"):
                dve.wait_ge(*at.done(f"s4.{w}.high"))
                dve.tensor_tensor(W4[w][1][:, :, :], wt(f"s4.{w}")[:, :, :], W4[w][0][:, :, :].bitcast(FP32), ALU.subtract).then_inc(*at.step(f"s4.{w}.low"))
            for c in range(KC):
                dve.wait_ge(*at.done(f"s4.q.{c}.out"))
            with at.loop(dve, "s4.loop", B) as b:
                dve.wait_ge(*at.done("s4.S7", back=1))
                for a in range(G):
                    dve.tensor_copy(qd[a * HD:(a + 1) * HD, :, a, :], Q4[a * HD:(a + 1) * HD, :, bass.ds(b * S, S)]).then_inc(*at.step("s4.qd"))
                dve.wait_ge(*at.done("s4.o7", back=1))
                for h in (0, 1):
                    m0, mt = HALF[h]
                    for j in range(mt):
                        dve.wait_ge(*at.done(f"s4.V{h}.{j}"))
                        dve.tensor_tensor(VT[:, m0 + j, :], bank(4 + (m0 + j) % 2), row("bv4", D), ALU.add).then_inc(*at.step(f"s4.V{h}.{j}.out"))
                        if h == 0 and j < KC:
                            dve.wait_ge(*at.done(f"s4.high1.{j}"))
                            dve.tensor_tensor(CL[1][:, j, :], CT[1][:, j, :], CH[1][:, j, :].bitcast(FP32), ALU.subtract).then_inc(*at.step("s4.low1"))

                def out(p):
                    a = (p % 2) * 64
                    dve.wait_ge(*at.done(f"s4.o{p}"))
                    for r in (0, 1):
                        q = a + r * HD
                        dve.tensor_copy(O4[q:q + HD, p // 2, bass.ds(b * S, S)], PS[q:q + HD, 6 + p % 2, r * S:(r + 1) * S]).then_inc(*at.step(f"s4.o{p}.out"))

                def transposed(p):
                    for k, (m0, n) in list(enumerate(TG))[2:]:
                        dve.wait_ge(*at.done(f"s4.pt{p}.{k}"))
                        if p:
                            dve.wait_ge(*at.done(f"s4.o{p - 1}"))
                        dve.tensor_copy(PTs[:, m0:m0 + n, :], PS[:, 4 + k % 2, 0:n * P].rearrange("p (m q) -> p m q", q=P)).then_inc(*at.step(f"s4.pt{p}.{k}.out"))

                for p in range(NP):
                    a = p % 2
                    for h in (0, 1):
                        dve.wait_ge(*at.done(f"s4.S{p}.{h}"))
                        dve.tensor_reduce(top[a][h], PS[:, 2 * h:2 * h + 2, 0:MB], AX.XY, ALU.max).then_inc(*at.step())
                    dve.wait_ge(*at.own())
                    dve.tensor_scalar(minus_max[a], top[a][0], top[a][1], -SCALE, ALU.max, ALU.mult).then_inc(*at.step(f"s4.max{p}"))
                    if p:
                        transposed(p - 1)
                    sm = total[a][0]
                    dve.wait_ge(*at.done(f"s4.exp{p}.1"))
                    dve.tensor_tensor(sm, sm, total[a][1], ALU.add).then_inc(*at.step())
                    dve.wait_ge(*at.own())
                    dve.reciprocal(sm, sm).then_inc(*at.step())
                    dve.wait_ge(*at.own())
                    dve.tensor_tensor(sm, sm, flag, ALU.mult).then_inc(*at.step())
                    dve.wait_ge(*at.own())
                    dve.tensor_scalar(PR[:, p % 2, :], PR[:, p % 2, :], sm, None, ALU.mult).then_inc(*at.step(f"s4.p{p}"))
                    if p:
                        out(p - 1)
                transposed(NP - 1)
                out(7)
            for c in range(KC):
                dve.wait_ge(*at.done(f"s4.wo_.{c}"))
                dve.scalar_tensor_tensor(out=X[:, c, :], in0=bank(c), scalar=v("bo4", c), in1=X[:, c, :],
                                             op0=ALU.add, op1=ALU.add).then_inc(*at.step(f"s4.wo_.{c}.out"))
            at.same("x4", "s4.wo_.3.out")

        N5, Q5, K5, V5, O5 = TS[0], TS[1], TS[2], TS[3], TS[4]
        trig = RC[:, 4200:4200 + 2 * T].rearrange("p (a s) -> p a s", a=2)

        def rotate_pe(pe, at, tag, x, outs, banks):
            for c in range(KC):
                pe.wait_ge(*at.done(outs[c]))
                if bank_reader.get(banks[c]):
                    pe.wait_ge(*at.done(bank_reader[banks[c]]))
                pe.matmul(bank(banks[c]), C["rot"], x[:, c, :], start=True, stop=True).then_inc(*at.step(f"{tag}.{c}"))
                bank_reader[banks[c]] = f"{tag}.{c}.out"

        def rotate_dve(dve, at, tag, x, tmp, banks):
            for c in range(KC):
                dve.wait_ge(*at.done(f"{tag}.{c}"))
                dve.tensor_tensor(tmp[:, c, :], bank(banks[c]), trig[:, 1, :], ALU.mult).then_inc(*at.step(f"{tag}.{c}.out"))
                dve.tensor_tensor(x[:, c, :], x[:, c, :], trig[:, 0, :], ALU.mult).then_inc(*at.step())
                dve.wait_ge(*at.own())
                dve.tensor_tensor(x[:, c, :], x[:, c, :], tmp[:, c, :], ALU.add).then_inc(*at.step(f"{tag}.done"))

        def s5_pool(pool, at):
            if 4 in stages:
                pool.wait_ge(*at.done("s4.S7"))
            pool.dma_start(trig, t["trig"]).then_inc(*at.load("mask_loaded", "trig"))
            if 4 in stages:
                pool.wait_ge(*at.done("s4.o7"))
            attn_pool(pool, at, "s5.at", K5, ["s5.kr.done"])

        def s5_pe(pe, at):
            norm_pe(pe, at, "s5.ln", X, ["x4"] if 4 in stages else ["x"])
            linear_pe(pe, at, "s5.q", [("s5.wq", N5)], (0, 1, 2, 3), range(KC), ["s5.ln.done"])
            linear_pe(pe, at, "s5.k", [("s5.wk", N5)], (4, 5, 6, 7), range(KC))
            rotate_pe(pe, at, "s5.qr", Q5, [f"s5.q.{c}.out" for c in range(KC)], (0, 1, 2, 3))
            rotate_pe(pe, at, "s5.kr", K5, [f"s5.k.{c}.out" for c in range(KC)], (4, 5, 6, 7))
            values_pe(pe, at, "s5.v", "s5.wv", N5, (0, 1, 2, 3))
            attn_pe(pe, at, "s5.at", Q5, V5, ["s5.qr.done"] + [f"s5.v.{c}.out" for c in range(4)])
            linear_pe(pe, at, "s5.o", [("s5.wo", O5)], (0, 1, 2, 3), range(KC), ["s5.at.O3.out"])

        def s5_act(act, at):
            norm_act(act, at, "s5.ln", X, xc=N5)
            linear_out(act, at, "s5.q", (0, 1, 2, 3), range(KC), lambda ps, c: act.activation(Q5[:, c, :], ps, ACT.Identity, bias=v("bq5", c)))
            linear_out(act, at, "s5.k", (4, 5, 6, 7), range(KC), lambda ps, c: act.activation(K5[:, c, :], ps, ACT.Identity, bias=v("bk5", c)))
            attn_act(act, at, "s5.at")

        def s5_dve(dve, at):
            norm_dve(dve, at, "s5.ln", X, N5, 1e-5, xc=N5)
            dve.wait_ge(*at.done("trig"))
            rotate_dve(dve, at, "s5.qr", Q5, TS[4], (0, 1, 2, 3))
            rotate_dve(dve, at, "s5.kr", K5, TS[5], (4, 5, 6, 7))
            values_dve(dve, at, "s5.v", V5, "bv5", (0, 1, 2, 3))
            attn_dve(dve, at, "s5.at", O5, C["causal"])
            for c in range(KC):
                dve.wait_ge(*at.done(f"s5.o.{c}"))
                dve.scalar_tensor_tensor(out=X[:, c, :], in0=bank(c), scalar=v("bo5", c), in1=X[:, c, :],
                                             op0=ALU.add, op1=ALU.add).then_inc(*at.step(f"s5.o.{c}.out"))
            at.same("x5", "s5.o.3.out")

        N6, XT, SEL, SELG, SELT, EIN = TS[0], TS[1], TS[2], TS[3], TS[4], TS[5]
        YS = TS[1]
        EB = [QB[:, :, 0:S], QB[:, :, S:2 * S]]
        HS = [RC[0:S, 2048:2560], RC[0:S, 2560:3072]]
        HT = [RC[:, 3072 + 256 * k:3328 + 256 * k].rearrange("p (c s) -> p c s", c=KC) for k in (0, 1)]
        oh = RC[:, 128:160].rearrange("p (a e) -> p a e", e=E_)
        val = RC[:, 160:192].rearrange("p (a e) -> p a e", e=E_)
        gate6, idx6, pos6, over6, slot6 = (RC[:, 192 + 4 * k:196 + 4 * k] for k in range(5))

        def s6_pe(pe, at):
            norm_pe(pe, at, "s6.ln", X, ["x5"] if 5 in stages else ["x"])
            gate_pe(pe, at, "s6.g", N6, 1, ["s6.ln.done"])
            for tt in range(4):
                k = 4 + tt
                if bank_reader.get(k):
                    pe.wait_ge(*at.done(bank_reader[k]))
                for c in range(KC):
                    mm = pe.transpose(PS[:, k, c * P:(c + 1) * P], N6[:, c, tt * P:(tt + 1) * P], C["ident"])
                mm.then_inc(*at.step(f"s6.xt{tt}"))
            pe.wait_ge(*at.done("s6.onehot"))
            if bank_reader.get(1):
                pe.wait_ge(*at.done(bank_reader[1]))
            for tt in range(4):
                for u in range(tt + 1):
                    mm = pe.matmul(PS[:, 1, tt * E_:(tt + 1) * E_], C["earlier"] if u == tt else C["ones"], oh[:, u, :],
                                      start=(u == 0), stop=(u == tt))
            mm.then_inc(*at.step("s6.pos"))
            for due in at.last("s6.sel", "s6.pos.out", *(f"s6.xt{k}.out" for k in range(4))):
                pe.wait_ge(*due)
            for dc in range(KC):
                if bank_reader.get(dc) and dc > 1:
                    pe.wait_ge(*at.done(bank_reader[dc]))
                for tt in range(4):
                    mm = pe.matmul(bank(dc), XT[:, tt, dc * P:(dc + 1) * P], SEL[:, tt, :], start=(tt == 0), stop=(tt == 3))
                mm.then_inc(*at.step(f"s6.ein{dc}"))
            for j in range(4):
                for tt in range(4):
                    mm = pe.transpose(PS[:, 4 + j, tt * P:(tt + 1) * P], SELG[:, tt, j * P:(j + 1) * P], C["ident"])
                mm.then_inc(*at.step(f"s6.selt{j}"))
            for due in at.last(*(f"s6.ein{k}.out" for k in range(4)), *(f"s6.selt{k}.out" for k in range(4))):
                pe.wait_ge(*due)
            with at.loop(pe, "s6.loop", E_ // 2) as j:
                for k in (0, 1):
                    q = f"s6.{k}"

                    def hidden(s):
                        w = f"s6.moe.{k}.a{s}"
                        pe.wait_ge(*at.done(w))
                        if s >= 2:
                            pe.wait_ge(*at.done(f"{q}.h{s - 2}.out"))
                        elif k:
                            pe.wait_ge(*at.done(f"s6.0.h{s + 2}.out"))
                        else:
                            pe.wait_ge(*at.done(f"s6.1.h{s + 2}.out", back=1))
                        for c in range(KC):
                            mm = pe.matmul(PS[0:S, s % 2, :], EB[k][:, c, :], wt(w)[:, c, :], start=(c == 0), stop=(c == KC - 1))
                        mm.then_inc(*at.step(f"{q}.h{s}"))
                        at.same(w + ".used", f"{q}.h{s}")

                    def output(s):
                        w = f"s6.moe.{k}.b{s}"
                        pe.wait_ge(*at.done(f"{q}.h{s}.out"))
                        if s >= 2:
                            pe.wait_ge(*at.done(f"{q}.ht{s - 2}.out"))
                        elif k:
                            pe.wait_ge(*at.done(f"s6.0.ht{s + 2}.out"))
                        else:
                            pe.wait_ge(*at.done(f"s6.1.ht{s + 2}.out", back=1))
                        pe.nop(nofuse=True)
                        for c in range(KC):
                            mm = pe.transpose(PS[:, 2 + s % 2, c * S:(c + 1) * S], HS[s % 2][:, c * P:(c + 1) * P],
                                                 C["ident"][0:S, 0:S])
                        mm.then_inc(*at.step(f"{q}.ht{s}"))
                        for due in at.last(w, f"{q}.ht{s}.out"):
                            pe.wait_ge(*due)
                        if s == 0:
                            pe.wait_ge(*at.done(f"{q}.y.out", back=1))
                        for c in range(KC):
                            mm = pe.matmul(PS[k * S:(k + 1) * S, 4 + k, :], HT[s % 2][:, c, :], wt(w)[:, c, :],
                                              start=(s == 0 and c == 0), stop=(s == FS - 1 and c == KC - 1))
                        mm.then_inc(*at.step(f"{q}.y{s}"))
                        at.same(w + ".used", f"{q}.y{s}")

                    pe.wait_ge(*at.done(f"{q}.eb"))
                    hidden(0)
                    for s in range(FS):
                        if s + 1 < FS:
                            hidden(s + 1)
                        output(s)
            for due in at.last("s6.0.y.out", "s6.1.y.out"):
                pe.wait_ge(*due)
            rd = {0: "s6.1.h2.out", 1: "s6.1.h3.out", 2: "s6.1.ht2.out", 3: "s6.1.ht3.out"}
            for dc in range(KC):
                pe.wait_ge(*at.done(rd[dc]))
                for j in range(4):
                    mm = pe.matmul(bank(dc), YS[:, j, dc * P:(dc + 1) * P], SELT[:, j, :], start=(j == 0), stop=(j == 3))
                mm.then_inc(*at.step(f"s6.out{dc}"))

        def s6_act(act, at):
            norm_act(act, at, "s6.ln", X, xc=N6)
            gate_act(act, at, "s6.g")
            for dc in range(KC):
                act.wait_ge(*at.done(f"s6.ein{dc}"))
                act.activation(EIN[:, dc, :], bank(dc), ACT.Copy).then_inc(*at.step(f"s6.ein{dc}.out"))
            for j in range(4):
                act.wait_ge(*at.done(f"s6.selt{j}"))
                act.activation(SELT[:, j, :], bank(4 + j), ACT.Copy).then_inc(*at.step(f"s6.selt{j}.out"))
            with at.loop(act, "s6.loop", E_ // 2) as j:
                for k in (0, 1):
                    q = f"s6.{k}"
                    for s in range(FS):
                        act.wait_ge(*at.done(f"{q}.h{s}"))
                        if s >= 2:
                            act.wait_ge(*at.done(f"{q}.ht{s - 2}"))
                        elif k:
                            act.wait_ge(*at.done(f"s6.0.ht{s + 2}"))
                        else:
                            act.wait_ge(*at.done(f"s6.1.ht{s + 2}", back=1))
                        act.activation(HS[s % 2], PS[0:S, s % 2, :], ACT.Gelu_apprx_tanh).then_inc(*at.step(f"{q}.h{s}.out"))

        def s6_dve(dve, at):
            norm_dve(dve, at, "s6.ln", X, N6, 1e-5, xc=N6)
            gate_dve(dve, at, "s6.g", False)
            for tt in range(4):
                dve.wait_ge(*at.done(f"s6.xt{tt}"))
                dve.tensor_copy(XT[:, tt, :], bank(4 + tt)).then_inc(*at.step(f"s6.xt{tt}.out"))
            bc = lambda a: a.unsqueeze(2).broadcast_to([P, 4, E_])
            iota_e = row("iota_e", 32).rearrange("p (a e) -> p a e", e=E_)
            dve.wait_ge(*at.own())
            dve.tensor_reduce(gate6, ga, AX.X, ALU.max).then_inc(*at.step())
            dve.wait_ge(*at.own())
            dve.tensor_tensor(val, ga, bc(gate6), ALU.is_equal).then_inc(*at.step())
            dve.wait_ge(*at.own())
            dve.scalar_tensor_tensor(out=val, in0=val, scalar=-128.0, in1=iota_e, op0=ALU.mult, op1=ALU.add).then_inc(*at.step())
            dve.wait_ge(*at.own())
            dve.tensor_reduce(idx6, val, AX.X, ALU.min).then_inc(*at.step())
            dve.wait_ge(*at.own())
            dve.tensor_tensor(oh, val, bc(idx6), ALU.is_equal).then_inc(*at.step("s6.onehot"))
            dve.wait_ge(*at.done("s6.pos"))
            dve.tensor_tensor(val, PS[:, 1, 0:32].rearrange("p (a e) -> p a e", e=E_), oh, ALU.mult).then_inc(*at.step("s6.pos.out"))
            dve.wait_ge(*at.own())
            dve.tensor_reduce(pos6, val, AX.X, ALU.add).then_inc(*at.step())
            dve.wait_ge(*at.own())
            dve.tensor_scalar(over6, pos6, float(CAP), 16384.0, ALU.is_ge, ALU.mult).then_inc(*at.step())
            dve.tensor_scalar(slot6, idx6, float(CAP), 128.0 * CAP, ALU.mult, ALU.add).then_inc(*at.step())
            dve.wait_ge(*at.own())
            dve.tensor_tensor(slot6, slot6, pos6, ALU.add).then_inc(*at.step())
            dve.wait_ge(*at.own())
            dve.tensor_tensor(slot6, slot6, over6, ALU.add).then_inc(*at.step())
            dve.wait_ge(*at.own())
            for tt in range(4):
                dve.tensor_scalar(SEL[:, tt, :], row("iota_slot", D), slot6[:, tt:tt + 1], None, ALU.is_equal).then_inc(*at.step())
            dve.wait_ge(*at.own())
            for tt in range(4):
                dve.tensor_scalar(SELG[:, tt, :], SEL[:, tt, :], gate6[:, tt:tt + 1], None, ALU.mult).then_inc(*at.step("s6.sel"))
            for due in at.last(*(f"s6.ein{k}.out" for k in range(4))):
                dve.wait_ge(*due)
            with at.loop(dve, "s6.loop", E_ // 2) as j:
                for k in (0, 1):
                    q = f"s6.{k}"
                    dve.wait_ge(*at.done(f"{q}.h3", back=1))
                    dve.tensor_copy(EB[k], EIN[:, :, bass.ds(j * (2 * S) + k * S, S)]).then_inc(*at.step(f"{q}.eb"))
                for k in (0, 1):
                    q = f"s6.{k}"
                    for s in range(FS):
                        dve.wait_ge(*at.done(f"{q}.ht{s}"))
                        if s >= 2:
                            dve.wait_ge(*at.done(f"{q}.y{s - 2}"))
                        elif k:
                            dve.wait_ge(*at.done(f"s6.0.y{s + 2}"))
                        else:
                            dve.wait_ge(*at.done(f"s6.1.y{s + 2}", back=1))
                        dve.tensor_copy(HT[s % 2], PS[:, 2 + s % 2, 0:KC * S].rearrange("p (c s) -> p c s", c=KC)).then_inc(*at.step(f"{q}.ht{s}.out"))
                    dve.wait_ge(*at.done(f"{q}.y3"))
                    dve.tensor_copy(YS[k * S:(k + 1) * S, j, :], PS[k * S:(k + 1) * S, 4 + k, :]).then_inc(*at.step(f"{q}.y.out"))
            for dc in range(KC):
                dve.wait_ge(*at.done(f"s6.out{dc}"))
                dve.tensor_tensor(X[:, dc, :], X[:, dc, :], bank(dc), ALU.add).then_inc(*at.step("x6"))

        @block.sync
        def _(sync):
            at = Steps(sems, "out_stored", marks, new)
            for dst, src, name in ((X[:, :, :], t["x"], "x"), (sq[:, :, :], t["squares"], "x"), (vec[:, :], t["vecs"], "consts"),
                                   (rows[:, :], t["rows"], "consts"), (gw[:, :, :, :], t["gates"], "consts"), (RC[:, 1600:1792].rearrange("p (a b) -> p a b", a=3), t["abc"], "consts")):
                sync.dma_start(dst, src).then_inc(*at.load("consts_loaded", name))
            at.same("abc", "consts"); at.same("x", "consts")
            for name, tile in order:
                if tile is not None:
                    if before[name]:
                        sync.wait_ge(*at.done(before[name] + ".used"))
                    sync.dma_start(ring[slot[name]][:, :, :], t["tiles"][tile]).then_inc(*at.load(f"weights_loaded{slot[name]}", name))
                    continue
                for x in before[name]:
                    sync.wait_ge(*at.done(x + ".used"))
                if name == "s3.moe":
                    with at.loop(sync, "s3.loop", E_) as i:
                        for k, x in enumerate(EXPERT):
                            prev = EXPERT[(k - RING) % 8]
                            sync.wait_ge(*at.done(f"{name}.{prev}.used", back=0 if k >= RING else 1))
                            sync.dma_start(ring[k % RING][:, :, :], t["experts3"][i, k]).then_inc(*at.load(f"weights_loaded{k % RING}", f"{name}.{x}"))
                else:
                    with at.loop(sync, "s6.loop", E_ // 2) as i:
                        for n in range(16):
                            prev = (n - RING) % 16
                            sync.wait_ge(*at.done(f"{name}.{prev // 8}.{EXPERT[prev % 8]}.used", back=0 if n >= RING else 1))
                            sync.dma_start(ring[n % RING][:, :, :], t["experts6"][i, n]).then_inc(*at.load(f"weights_loaded{n % RING}", f"{name}.{n // 8}.{EXPERT[n % 8]}"))
            sync.wait_ge(*at.done(f"x{max(stages)}"))
            sync.dma_start(t["out"], X[:, :, :]).then_inc(*at.load("out_stored", "stored"))
            sync.wait_ge(sems["out_stored"], 16)

        @block.gpsimd
        def _(pool):
            at = Steps(sems, "pool_done", marks, new)
            if 1 in stages:
                s1_pool(pool, at)
                pool.wait_ge(*at.done("x1"))
            pool.dma_start(PR[:, 0, :].bitcast(I32), t["mask"]).then_inc(*at.load("mask_loaded", "mask"))
            for s, part in ((2, s2_pool), (3, s3_pool), (4, s4_pool), (5, s5_pool)):
                if s in stages:
                    part(pool, at)

        @block.scalar
        def _(act):
            at = Steps(sems, "scalar_done", marks, new)
            act.wait_ge(*at.done("x"))
            act.activation(rstd[:, 0:1], C["ident"][:, 0:1], ACT.Copy).then_inc(*at.step(by=AHEAD))
            for s, part in ((1, s1_act), (2, s2_act), (3, s3_act), (4, s4_act), (5, s5_act), (6, s6_act)):
                if s in stages:
                    part(act, at)

        @block.tensor
        def _(pe):
            at = Steps(sems, "tensor_done", marks, new)
            bank_reader.clear()
            pe.wait_ge(*at.done("x"))
            pe.matmul(bank(7, 1), C["ident"], C["ident"][:, 0:1], start=True, stop=True).then_inc(*at.step(by=AHEAD))
            for s, part in ((1, s1_pe), (2, s2_pe), (3, s3_pe), (4, s4_pe), (5, s5_pe), (6, s6_pe)):
                if s in stages:
                    part(pe, at)

        @block.vector
        def _(dve):
            at = Steps(sems, "vector_done", marks, new)
            dve.wait_ge(*at.done("x"))
            dve.tensor_copy(idb[:, :], C["ident"]).then_inc(*at.step("idb", AHEAD))
            for s, part in ((1, s1_dve), (2, s2_dve), (3, s3_dve), (4, s4_dve), (5, s5_dve), (6, s6_dve)):
                if s in stages:
                    part(dve, at)


def _tiles(w, n=None):
    a, b = w.shape[0] // D, w.shape[1] // D
    return w.reshape(a, KC, P, b, D).transpose(0, 3, 2, 1, 4).reshape(a * b, P, KC, D)


def layout(i):
    f = lambda n: np.asarray(i[n])
    feat = lambda a: a.reshape(T, D).T.reshape(KC, P, T).transpose(1, 0, 2)
    ctx = np.zeros((B, MP, D), np.float32)
    ctx[:, :M] = f("ctx_1024")
    g, a0, f0 = "L0_xattn_", "L0_attn_", "L0_ffn_"
    tiles = [f(g + "Wq").T, f(g + "Wk"), f(g + "Wv").T]
    for k in range(3):
        tiles += [f(g + "gru_wih")[k * D:(k + 1) * D].T, f(g + "gru_whh")[k * D:(k + 1) * D].T]
    tiles += [f(a0 + "out_w").T]
    for j in range(FS):
        tiles += [f(a0 + "ffn1_w")[j * D:(j + 1) * D].T, f(a0 + "ffn2_w")[:, j * D:(j + 1) * D].T]
    tiles += [f(f0 + "conv_w")[:, :, k].T for k in range(3)]
    tiles += [f(f0 + "wqkv")[k * D:(k + 1) * D].T for k in range(3)] + [f(f0 + "wo").T]
    tiles += [f("L1_xattn_" + n) for n in ("Wq", "Wk", "Wv", "Wo")] + [f("L1_attn_" + n).T for n in ("Wq", "Wk", "Wv", "Wo")]
    experts = lambda w1, w2: np.stack([np.concatenate([(_tiles(w1[x]) if ab == "a" else _tiles(w2[x]))[int(s):int(s) + 1]
                                       for ab, s in ("a0", "a1", "b0", "a2", "b1", "a3", "b2", "b3")]) for x in range(E_)])
    src = dict(slot_w=g + "slot_norm_w", in_w=g + "input_norm_w", bih=g + "gru_bih", bhh=g + "gru_bhh", ln_w=a0 + "ln_w",
               ln_b=a0 + "ln_b", D=a0 + "D_vec", out_b=a0 + "out_b", ln2_w=a0 + "ln2_w", ln2_b=a0 + "ln2_b",
               ffn1_b=a0 + "ffn1_b", ffn2_b=a0 + "ffn2_b", conv_b=f0 + "conv_b", bqkv=f0 + "bqkv", bo3=f0 + "bo",
               ln1_g=f0 + "ln1_g", ln1_b=f0 + "ln1_b", ln2_g=f0 + "ln2_g", ln2b3=f0 + "ln2_b", b1=f0 + "b1", b2=f0 + "b2",
               bq4="L1_xattn_bq", bk4="L1_xattn_bk", bo4="L1_xattn_bo", bq5="L1_attn_bq", bk5="L1_attn_bk", bo5="L1_attn_bo")
    vecs = np.concatenate([f(src[n]).reshape(-1, P).T for n, _ in VECS], axis=1)
    rep = lambda a: np.broadcast_to(a, (P, a.shape[-1]))
    rows = np.concatenate([rep(f(f0 + "gate_b")), rep(f(f0 + "bqkv")[2 * D:]), rep(f("L1_xattn_bv")), rep(f("L1_attn_bv")),
                           rep(np.arange(D, dtype=np.float32)), rep(np.tile(np.arange(E_, dtype=np.float32), 4)),
                           (np.arange(P)[:, None] < MLAST).astype(np.float32)], axis=1)
    gates = np.stack([f(f0 + "gate_w").reshape(KC, P, E_), f("L1_ffn_router_w").reshape(KC, P, E_)]).transpose(2, 0, 1, 3)
    abc = np.stack([f(a0 + n).reshape(KC, P, N_STATE) for n in ("A_log", "B_mat", "C_mat")]).transpose(2, 0, 1, 3).reshape(P, 3, -1)
    r = np.arange(P)
    same = (r[:, None] // S) == (r[None] // S)
    rot = np.zeros((P, P), np.float32)
    rot[r[1::2], r[::2]] = -1
    rot[r[::2], r[1::2]] = 1
    squares = np.stack([np.eye(P), np.full((P, P), 1 / D), np.ones((P, P)), np.where(same, 0, NEG),
                        np.where(same & (r[None] <= r[:, None]), 0, NEG), r[:, None] < r[None], rot]).astype(np.float32)
    ang = np.outer(np.arange(S, dtype=np.float32), (1.0 / np.float32(10000.0) ** (np.arange(0, HD, 2, dtype=np.float32) / HD)))
    ang = np.tile(ang[:, (r % HD) // 2].T, (1, B)).astype(np.float32)
    mask = np.zeros((P, MP), np.int32)
    mask[:, :M] = np.concatenate([f("mask_SxS2_ik0")] * 2)
    return {
        "x": feat(f("x")), "ctxN": ctx.reshape(B, MT, P, D).transpose(0, 2, 1, 3),
        "ctxT": ctx.reshape(B, MP, KC, P).transpose(0, 3, 2, 1), "mask": mask,
        "tiles": np.stack([_tiles(w)[0] for w in tiles]),
        "experts3": experts(f(f0 + "w1"), f(f0 + "w2")),
        "experts6": experts(f("L1_ffn_w1"), f("L1_ffn_w2")).reshape(E_ // 2, 16, P, KC, D),
        "vecs": vecs, "rows": rows, "gates": gates, "abc": abc,
        "squares": squares.transpose(1, 0, 2), "trig": np.stack([np.cos(ang), np.sin(ang)], axis=1),
    }


def kernel(**inputs):
    import concourse.bacc as bacc
    from concourse.bass_utils import run_bass_kernel_spmd

    arrays = {n: np.ascontiguousarray(a) for n, a in layout(inputs).items()}

    def program(marks):
        nc = bacc.Bacc("TRN2", target_bir_lowering=False, num_devices=1)
        t = {n: nc.dram_tensor(f"in_{n}", a.shape, mybir.dt.from_np(a.dtype), kind="ExternalInput").ap() for n, a in arrays.items()}
        t["out"] = nc.dram_tensor("out_x", (P, KC, T), FP32, kind="ExternalOutput").ap()
        new = Marks()
        build(nc, marks, new, t)
        return nc, new

    _, counted = program(Marks())
    nc, _ = program(counted)
    r = run_bass_kernel_spmd(nc, [{f"in_{n}": a for n, a in arrays.items()}], core_ids=[0])
    y = r.results[0]["out_x"]
    return np.ascontiguousarray(y.transpose(1, 0, 2).reshape(D, T).T).reshape(B, S, D)
```

```python
import numpy as np
import concourse.bass as bass
from concourse import mybir
from contextlib import ExitStack, contextmanager

FP32, BF16, I32 = mybir.dt.float32, mybir.dt.bfloat16, mybir.dt.int32
FP32R = mybir.dt.float32r
ALU, ACT, AX = mybir.AluOpType, mybir.ActivationFunctionType, mybir.AxisListType

B, S, D = 8, 64, 512
T = B * S
P = 128
KC = D // P
M = 1601
MT = -(-M // P)
MP = MT * P
MLAST = M - (MT - 1) * P
HALF = [(0, 7), (7, MT - 7)]
H, HD = 16, 32
G = H // KC
E_, F = 8, 2048
FS = F // D
CAP = T // E_
N_STATE = 16
RING = 4
MB = MP // 4
NEG = -1e30
AHEAD = 100

S1_TILES = ["wq", "wk", "wv"] + [f"{w}{g}" for g in (0, 2, 1) for w in ("whh", "wih")]
SMALL = [f"s1.{n}" for n in S1_TILES]
SMALL += ["s2.out"] + [f"s2.{w}{j}" for j in range(FS) for w in ("ffn1_", "ffn2_")]
SMALL += [f"s3.conv{k}" for k in range(3)] + ["s3.wq", "s3.wk", "s3.wv", "s3.wo"]
SMALL += ["s4.wq", "s4.wk", "s4.wv", "s4.wo", "s5.wq", "s5.wk", "s5.wv", "s5.wo"]
AT = {n: i for i, n in enumerate(SMALL)}

VECS = [("slot_w", 4), ("in_w", 4), ("bih", 12), ("bhh", 12), ("ln_w", 4), ("ln_b", 4), ("D", 4), ("out_b", 4),
        ("ln2_w", 4), ("ln2_b", 4), ("ffn1_b", 16), ("ffn2_b", 4), ("conv_b", 4), ("bqkv", 12), ("bo3", 4),
        ("ln1_g", 4), ("ln1_b", 4), ("ln2_g", 4), ("ln2b3", 4), ("b1", 16 * E_), ("b2", 4 * E_),
        ("bq4", 4), ("bk4", 4), ("bo4", 4), ("bq5", 4), ("bk5", 4), ("bo5", 4)]
VAT, _n = {}, 0
for _k, _w in VECS:
    VAT[_k] = _n
    _n += _w
NVEC = _n
ROWS = [("gate_b", 8), ("bv3", D), ("bv4", D), ("bv5", D), ("iota_slot", D), ("iota_e", 4 * E_), ("in_last", 1), ("eps5", 1), ("eps6", 1)]
RAT, _n = {}, 0
for _k, _w in ROWS:
    RAT[_k] = _n
    _n += _w
NROW = _n
SQ = ["ident", "ones_d", "ones", "blockmask", "causal", "earlier", "rot"]


class Marks:

    def __init__(self):
        self.at, self.per = {}, {}


class Steps:

    def __init__(self, sems, own_key, marks, new):
        self.sems, self.own_key, self.marks, self.new = sems, own_key, marks, new
        self.count, self.i, self.inside = {}, None, None

    def load(self, key, name=None, by=16):
        self.count[key] = self.count.get(key, 0) + by
        if name:
            self.new.at[name] = (key, self.count[key], self.inside)
        return self.sems[key], by

    def step(self, name=None, by=1):
        return self.load(self.own_key, name, by)

    def same(self, name, other=None):
        self.new.at[name] = self.new.at[other] if other else (self.own_key, self.count[self.own_key], self.inside)

    def done(self, name, back=0):
        key, n, loop = self.marks.at.get(name, (self.own_key, 1, None))
        per, reps = self.marks.per.get((loop, key), (0, 1))
        if loop is None:
            return self.sems[key], n
        if loop == self.inside:
            assert n - per * back >= 0, (name, n, per)
            return self.sems[key], n - per * back + self.i * per
        return self.sems[key], n + per * (reps - 1)

    def last(self, *names, back=0):
        last = {}
        for name in names:
            key, n, _ = self.marks.at.get(name, (self.own_key, 1, None))
            if n >= last.get(key, (0, None))[0]:
                last[key] = n, name
        return [self.done(name, back) for _, name in last.values()]

    def own(self):
        n = self.count.get(self.own_key, 0)
        if self.inside is not None:
            n = n + self.i * self.marks.per.get((self.inside, self.own_key), (0, 1))[0]
        return self.sems[self.own_key], n

    @contextmanager
    def loop(self, eng, name, reps):
        before = dict(self.count)
        with eng.Fori(0, reps) as i:
            self.i, self.inside = i, name
            yield i
        self.i, self.inside = None, None
        for key, n in list(self.count.items()):
            per = n - before.get(key, 0)
            if per:
                self.new.per[name, key] = (per, reps)
                self.count[key] = n + per * (reps - 1)


def sem_names():
    return (["tensor_done", "scalar_done", "vector_done", "pool_done", "consts_loaded", "mask_loaded", "out_stored"]
            + [f"weights_loaded{s}" for s in range(RING)]
            + [f"{c}_loaded{h}" for c in ("ctxT", "ctxN") for h in (0, 1)])


def build(nc, marks, new, t, stages=(1, 2, 3, 4, 5, 6)):
    ctx = ExitStack()
    with ctx:
        address = {}

        def sb(name, shape, dt=FP32):
            address[name] = nc.sbuf_base
            return ctx.enter_context(nc.sbuf_tensor(name, shape, dt))

        def part(name, of, k=0, n=D):
            return nc.alloc_sbuf_tensor_at(name, [P, KC, n], FP32R, offset=address[of] + round(4 * k * KC * D))

        X = sb("X", [P, KC, T])
        TS = [sb(f"T{k}", [P, KC, T]) for k in range(6)]
        ring = [sb(f"ring{s}", [P, KC, D]) for s in range(RING)]
        RA, RB, RC = (sb(n, [P, MT * D]) for n in ("RA", "RB", "RC"))
        n0 = HALF[0][1]
        CT = [RA[:, 0:KC * n0 * P].rearrange("p (c m) -> p c m", c=KC),
              RA[:, KC * n0 * P:KC * MP].rearrange("p (c m) -> p c m", c=KC)]
        CN = [RB[:, 0:n0 * D].rearrange("p (m d) -> p m d", d=D),
              RB[:, n0 * D:MT * D].rearrange("p (m d) -> p m d", d=D)]
        RA4 = [RA[:, k * 2048:(k + 1) * 2048].rearrange("p (c m) -> p c m", c=KC) for k in range(3)]
        RB4 = [RB[:, k * 2048:(k + 1) * 2048].rearrange("p (c m) -> p c m", c=KC) for k in range(3)]
        RC4 = [RC[:, k * 2048:(k + 1) * 2048].rearrange("p (c m) -> p c m", c=KC) for k in range(3)]
        sq = sb("sq", [P, len(SQ), P])
        C = {n: sq[:, k, :] for k, n in enumerate(SQ)}
        vec = sb("vec", [P, NVEC])
        rows = sb("rows", [P, NROW])
        gw = sb("gw", [P, 2, KC, E_])
        kconv = sb("kconv", [P, KC, S])
        RN = sb("RN", [P, B, MT])
        bsum = sb("bsum", [P, 12])
        inws = sb("inws", [P, 4])
        rstd = sb("rstd", [P, T])
        misc = sb("misc", [P, 512])
        unread = sb("unread", [P, 1])
        idb = sb("idb", [P, P], BF16)
        PR = sb("PR", [P, 2, MP])
        PTs = sb("PTs", [P, MT, P])
        maskneg = sb("maskneg", [P, MP], BF16)
        assert address["maskneg"] == address["PTs"] + 4 * MP
        ring_part = [part(f"W_part{s}", f"ring{s}") for s in range(RING)]
        WH = [part("W_high0", "RB", 2), part("W_high1", "RC", 2), part("W_high2", "RA", 2)]
        XH, XL = part("X_high", "T4"), part("X_low", "T5")
        HH = [part("H_high0", "RB", 0), part("H_high1", "RB", 1)]
        HL = [part("H_low0", "RC", 0), part("H_low1", "RC", 1)]
        CL = [part("C_low0", "RA", 0, n0 * P), part("C_low1", "RA", n0 * P / D, HALF[1][1] * P)]
        CH = [part("C_high0", "T4", 0, n0 * P), part("C_high1", "T0", 0, HALF[1][1] * P)]
        assert address["T5"] == address["T4"] + 4 * KC * T and address["T1"] == address["T0"] + 4 * KC * T
        GH = [part("G_high0", "RA", 0), part("G_high1", "RA", 1)]
        SLH, SLL = part("state_high", "RA", 2), part("state_low", "PTs")
        SNH, SNL = part("update_high", "T5"), part("update_low", "T1")
        QB = PR[:, 1, 0:KC * P].rearrange("p (c k) -> p c k", c=KC)
        PS = ctx.enter_context(nc.psum_tensor("PS", [P, 8, 512], FP32))

        def v(name, c=0):
            k = VAT[name] + c
            return vec[:, k:k + 1]

        def row(name, n):
            return rows[:, RAT[name]:RAT[name] + n]

        sems = {n: ctx.enter_context(nc.semaphore(n)) for n in sem_names()}
        block = ctx.enter_context(nc.Block())

        def bank(k, n=512):
            return PS[:, k, 0:n]

        EXPERT = ["a0", "a1", "b0", "a2", "b1", "a3", "b2", "b3"]
        order = []
        if 1 in stages:
            order += [(f"s1.{it}.{n}", AT[f"s1.{n}"]) for it in range(3) for n in S1_TILES]
        if 2 in stages:
            order += [(n, AT[n]) for n in ["s2.out"] + [f"s2.ffn{1 if x[0] == 'a' else 2}_{x[1]}" for x in EXPERT]]
        if 3 in stages:
            order += [(n, AT[n]) for n in SMALL if n.startswith("s3.")] + [("s3.moe", None)]
        for st in (4, 5):
            if st in stages:
                order += [(n, AT[n]) for n in SMALL if n.startswith(f"s{st}.")]
        if 6 in stages:
            order += [("s6.moe", None)]
        slot, before, place = {}, {}, 0
        last = [None] * RING
        for name, tile in order:
            if tile is None:
                place = -(-place // RING) * RING
                before[name] = [x for x in last if x]
                tiles = EXPERT if name == "s3.moe" else [f"{k}.{x}" for k in (0, 1) for x in EXPERT]
                for k, x in enumerate(tiles):
                    slot[f"{name}.{x}"] = k % RING
                    last[k % RING] = f"{name}.{x}"
            else:
                slot[name] = place % RING
                before[name] = last[place % RING]
                last[place % RING] = name
                place += 1

        before_wk_high = before.get("s4.wo")
        if 4 in stages:
            before["s4.wo"] = "s4.wk"
            if 5 in stages:
                before["s5.wq"] = "s4.wk"

        def wt(name):
            return ring[slot[name]]

        bank_reader = {}

        def linear_pe(pe, at, tag, terms, banks, outs, after=(), chunks=None):
            for due in at.last(*after):
                pe.wait_ge(*due)
            for n, oc in enumerate(outs):
                k = banks[n % len(banks)]
                if bank_reader.get(k):
                    pe.wait_ge(*at.done(bank_reader[k]))
                for a, (w, x) in enumerate(terms):
                    if n == 0:
                        pe.wait_ge(*at.done(w))
                    for c in range(KC):
                        if chunks and n == 0 and a == 0:
                            pe.wait_ge(*at.done(f"{chunks}.{c}"))
                        mm = pe.matmul(bank(k), wt(w)[:, c, oc * P:(oc + 1) * P], x[:, c, :],
                                          start=(a == 0 and c == 0), stop=(a == len(terms) - 1 and c == KC - 1))
                mm.then_inc(*at.step(f"{tag}.{oc}"))
                bank_reader[k] = f"{tag}.{oc}.out"
            for w, _ in terms:
                at.same(w + ".used")

        def linear_out(act, at, tag, banks, outs, op):
            for n, oc in enumerate(outs):
                act.wait_ge(*at.done(f"{tag}.{oc}"))
                op(bank(banks[n % len(banks)]), oc).then_inc(*at.step(f"{tag}.{oc}.out"))

        def chunk_steps(name, suffix=""):
            return [f"{name}{c}{suffix}" for c in range(KC)]

        def norm_pe(pe, at, tag, x, after, centred=True):
            if centred:
                if bank_reader.get(7):
                    pe.wait_ge(*at.done(bank_reader[7]))
                for c in range(KC):
                    if c < len(after):
                        pe.wait_ge(*at.done(after[c]))
                    mm = pe.matmul(bank(7), C["ones_d"], x[:, c, :], start=(c == 0), stop=(c == KC - 1))
                mm.then_inc(*at.step(f"{tag}.mean"))
                bank_reader[7] = f"{tag}.centred.{KC - 1}"
            if bank_reader.get(6):
                pe.wait_ge(*at.done(bank_reader[6]))
            for c in range(KC):
                pe.wait_ge(*at.done(f"{tag}.square.{c}"))
                mm = pe.matmul(bank(6), C["ones_d"], TS[5][:, c, :], start=(c == 0), stop=(c == KC - 1))
            mm.then_inc(*at.step(f"{tag}.var"))
            bank_reader[6] = f"{tag}.root"

        def norm_act(act, at, tag, x, eps, after=(), centred=True, xc=None):
            xc = xc if centred else x
            act.activation(unread[:, :], C["ident"][:, 0:1], ACT.Sqrt).then_inc(*at.step())
            for c in range(KC):
                if c < len(after):
                    act.wait_ge(*at.done(after[c]))
                if centred:
                    act.wait_ge(*at.done(f"{tag}.centred.{c}"))
                act.activation(TS[5][:, c, :], xc[:, c, :], ACT.Square).then_inc(*at.step(f"{tag}.square.{c}"))
            act.wait_ge(*at.done("consts"))
            act.wait_ge(*at.done(f"{tag}.var"))
            act.activation(rstd[:, :], bank(6), ACT.Sqrt, bias=row(eps, 1)).then_inc(*at.step(f"{tag}.root"))

        def norm_dve(dve, at, tag, x, y, w=None, b=None, centred=True, xc=None):
            if centred:
                dve.wait_ge(*at.done(f"{tag}.mean"))
                for c in range(KC):
                    dve.tensor_tensor(xc[:, c, :], x[:, c, :], bank(7), ALU.subtract).then_inc(*at.step(f"{tag}.centred.{c}"))
            else:
                xc = x
            dve.wait_ge(*at.done(f"{tag}.root"))
            dve.reciprocal(rstd[:, :], rstd[:, :]).then_inc(*at.step())
            dve.wait_ge(*at.own())
            for c in range(KC):
                if w:
                    op = dve.scalar_tensor_tensor(out=y[:, c, :], in0=xc[:, c, :], scalar=v(w, c), in1=rstd[:, :],
                                                    op0=ALU.mult, op1=ALU.mult)
                else:
                    op = dve.tensor_tensor(y[:, c, :], xc[:, c, :], rstd[:, :], ALU.mult)
                op.then_inc(*at.step(f"{tag}.done.{c}"))
                if b:
                    dve.wait_ge(*at.own())
                    dve.tensor_scalar(y[:, c, :], y[:, c, :], v(b, c), None, ALU.add).then_inc(*at.step(f"{tag}.done.{c}"))
            at.same(f"{tag}.done")

        def triple(pe, ps, high, w, c, oc, xh, xl, start, stop):
            a, b = high[:, c, oc * P:(oc + 1) * P], ring_part[slot[w]][:, c, oc * P:(oc + 1) * P]
            pe.matmul(ps, a, xh, start=start, stop=False)
            pe.matmul(ps, a, xl, start=False, stop=False)
            return pe.matmul(ps, b, xh, start=False, stop=stop)

        SL, SN, UP, RG, ZG = TS[0], TS[1], TS[2], TS[3], TS[4]
        ss = PR[0:S, 0, :]
        W1 = MT * S
        ptf = PTs[:, :, :].rearrange("p m k -> p (m k)")
        rgf = RG[:, :, :].rearrange("p c t -> p (c t)")
        A_ = [ptf[:, u * W1:(u + 1) * W1].rearrange("p (m k) -> p m k", k=S) for u in (0, 1)]
        AR = [rgf[:, u * W1:(u + 1) * W1].rearrange("p (m k) -> p m k", k=S) for u in (0, 1)]
        UN = [RC[0:S, u * D:(u + 1) * D] for u in (0, 1)]
        asum = [RC[:, 1024 + u * S:1088 + u * S] for u in (0, 1)]
        stat = [[misc[:, 64 * u + 8 * k:64 * u + 8 * k + 8] for k in range(4)] for u in (0, 1)]
        ssq = [misc[:, 128 + 16 * u:128 + 16 * u + MT] for u in (0, 1)]
        rden = [misc[0:S, 160 + u:161 + u] for u in (0, 1)]
        GRU = [("whh0", "r", 0, True, False), ("wih0", "r", 0, False, True), ("whh2", "gh", 0, True, True),
               ("wih2", "gx", 4, True, True), ("whh1", "z", 0, True, False), ("wih1", "z", 0, False, True)]
        sqs = TS[5][:, 0, :]
        qb = [QB[:, :, u * S:(u + 1) * S] for u in (0, 1)]
        SPLIT = MT - 4
        CNB = RC[:, 1792:1792 + SPLIT * D].rearrange("p (m d) -> p m d", d=D)
        cn_all = RB[:, 0:MT * D].rearrange("p (m d) -> p m d", d=D)

        def cn(u, m):
            if u == 0:
                return cn_all[:, m, :]
            return CNB[:, m, :] if m < SPLIT else ZG[:, m - SPLIT, :]

        def s1_pool(pool, at):
            for it in range(3):
                L = f"s1.{it}.loop"
                if it:
                    for due in at.last(*(f"s1.{it - 1}.z.{c}.out" for c in range(KC)), f"s1.{it - 1}.sl"):
                        pool.wait_ge(*due)
                with at.loop(pool, L, B // 2) as b:
                    for u in (0, 1):
                        for h in (0, 1):
                            m0, mt = HALF[h]
                            pool.wait_ge(*at.done(f"{L}.S{h}.{1 - u}", back=1 - u))
                            pool.nop(nofuse=True)
                            pool.dma_start(CT[h][:, :, :], t["ctxT"][b * 2 + u, :, :, m0 * P:(m0 + mt) * P])\
                                .then_inc(*at.load(f"ctxT_loaded{h}", f"{L}.ct{h}.{u}"))
                        pool.wait_ge(*at.done(f"{L}.U.{u}", back=1))
                        pool.nop(nofuse=True)
                        if u == 0:
                            pool.dma_start(cn_all, t["ctxN"][b * 2]).then_inc(*at.load("ctxN_loaded0", f"{L}.cn.0"))
                        else:
                            pool.dma_start(CNB, t["ctxN"][b * 2 + 1, :, 0:SPLIT, :]).then_inc(*at.load("ctxN_loaded1"))
                            pool.dma_start(ZG[:, :, :], t["ctxN"][b * 2 + 1, :, SPLIT:MT, :])\
                                .then_inc(*at.load("ctxN_loaded1", f"{L}.cn.1"))

        def s1_pe(pe, at):
            norm_pe(pe, at, "s1.ln", X, ["x"])
            for it in range(3):
                p, L = f"s1.{it}", f"s1.{it}.loop"
                norm_pe(pe, at, f"{p}.rms", SL, [], centred=False)
                linear_pe(pe, at, f"{p}.q", [(f"{p}.wq", SN)], (0, 1, 2, 3), range(KC), chunks=f"{p}.rms.done")
                linear_pe(pe, at, f"{p}.qk", [(f"{p}.wk", UP)], (0, 1, 2, 3), range(KC), [f"{p}.q.{c}.out" for c in range(KC)])

                def scores(u, h):
                    m0, mt = HALF[h]
                    w = mt * S
                    if h == 0:
                        pe.wait_ge(*at.done(f"{L}.qb.{u}"))
                    pe.wait_ge(*at.done(f"{L}.ct{h}.{u}"))
                    if u == 0:
                        pe.wait_ge(*at.done(f"{p}.qk.3.out"))
                    pe.wait_ge(*at.done(f"{L}.S{h}.{1 - u}.out", back=1 - u))
                    for j in (0, 1):
                        for c in range(KC):
                            mm = pe.matmul(PS[0:S, 2 * h + j, 0:w], qb[u][:, c, :], CT[h][:, c, j * w:(j + 1) * w],
                                           start=(c == 0), stop=(c == KC - 1))
                    mm.then_inc(*at.step(f"{L}.S{h}.{u}"))

                def transposes(u, h):
                    m0, mt = HALF[h]
                    pe.wait_ge(*at.done(f"{L}.S{h}.{u}.out"))
                    if u:
                        pe.wait_ge(*at.done(f"{L}.st{h}.0"))
                    else:
                        pe.wait_ge(*at.done(f"{L}.ut.{h}", back=1))
                    pe.nop(nofuse=True)
                    for j in range(mt):
                        mm = pe.transpose(PS[:, 4 + h, j * S:(j + 1) * S], ss[:, (m0 + j) * P:(m0 + j + 1) * P],
                                          C["ident"][0:S, 0:S])
                    mm.then_inc(*at.step(f"{L}.T{h}.{u}"))

                def updates(u, h):
                    m0, mt = HALF[h]
                    pe.wait_ge(*at.done(f"{L}.ar{h}.{u}"))
                    if h == 0:
                        pe.wait_ge(*at.done(f"{L}.cn.{u}"))
                        pe.wait_ge(*at.done(f"{L}.un.{u}", back=1))
                    for m in range(m0, m0 + mt):
                        mm = pe.matmul(PS[0:S, 6 + u, :], AR[u][:, m, :], cn(u, m), start=(m == 0), stop=(m == MT - 1))
                    if h:
                        mm.then_inc(*at.step(f"{L}.U.{u}"))

                def totals(u):
                    pe.wait_ge(*at.done(f"{L}.asum.{u}"))
                    pe.wait_ge(*at.done(f"{L}.st{u}.1"))
                    pe.matmul(PS[0:S, 4 + u, 448:449], asum[u], C["ones"][:, 0:1], start=True, stop=True)\
                        .then_inc(*at.step(f"{L}.den.{u}"))

                def turn(u):
                    pe.wait_ge(*at.done(f"{L}.un.{u}"))
                    pe.nop(nofuse=True)
                    for c in range(KC):
                        mm = pe.transpose(PS[:, 4 + u, c * S:(c + 1) * S], UN[u][:, c * P:(c + 1) * P], C["ident"][0:S, 0:S])
                    mm.then_inc(*at.step(f"{L}.UT.{u}"))

                with at.loop(pe, L, B // 2) as b:
                    scores(0, 0)
                    scores(0, 1)
                    transposes(0, 0)
                    scores(1, 0)
                    transposes(0, 1)
                    scores(1, 1)
                    transposes(1, 0)
                    updates(0, 0)
                    transposes(1, 1)
                    updates(0, 1)
                    totals(0)
                    updates(1, 0)
                    turn(0)
                    totals(1)
                    updates(1, 1)
                    turn(1)
                bank_reader.update({k: f"{L}.S{k // 2}.1.out" for k in range(4)})
                bank_reader.update({4: f"{L}.ut.0", 5: f"{L}.ut.1", 6: f"{L}.un.0", 7: f"{L}.un.1"})
                linear_pe(pe, at, f"{p}.v", [(f"{p}.wv", UP)], (0, 1, 2, 3), range(KC), [f"{p}.utw"])
                for k, (w, tag, banks, first, last) in enumerate(GRU):
                    xh, xl, ready = (SLH, SLL, "state") if w[:3] == "whh" else (SNH, SNL, "update")
                    pe.wait_ge(*at.done(f"{p}.{w}.low"))
                    for oc in range(KC):
                        if first and bank_reader.get(banks + oc):
                            pe.wait_ge(*at.done(bank_reader[banks + oc]))
                        for c in range(KC):
                            if oc == 0 and tag == "r":
                                pe.wait_ge(*at.done(f"{p}.{ready}.low{c}"))
                            mm = triple(pe, bank(banks + oc), GH[k % 2], f"{p}.{w}", c, oc, xh[:, c, :], xl[:, c, :],
                                        first and c == 0, last and c == KC - 1)
                        if last:
                            mm.then_inc(*at.step(f"{p}.{tag}.{oc}"))
                            bank_reader[banks + oc] = f"{p}.{tag}.{oc}.out"
                    if last:
                        at.same(f"{p}.{w}.used")
                    else:
                        mm.then_inc(*at.step(f"{p}.{w}.used"))
                if it < 2:
                    pe.wait_ge(*at.done(f"{p}.sl"))

        def s1_act(act, at):
            norm_act(act, at, "s1.ln", X, "eps5", xc=SN)
            for it in range(3):
                p, L = f"s1.{it}", f"s1.{it}.loop"
                norm_act(act, at, f"{p}.rms", SL, "eps6",
                         [f"s1.ln.done.{c}" if it == 0 else f"s1.{it - 1}.sl.{c}" for c in range(KC)], centred=False)
                linear_out(act, at, f"{p}.q", (0, 1, 2, 3), range(KC),
                           lambda ps, c: act.activation(UP[:, c, :], ps, ACT.Copy))
                if it == 0:
                    act.wait_ge(*at.done("s1.inws"))
                linear_out(act, at, f"{p}.qk", (0, 1, 2, 3), range(KC),
                           lambda ps, c: act.activation(SN[:, c, :], ps, ACT.Copy, scale=inws[:, c:c + 1]))

                def squares(u):
                    act.wait_ge(*at.done(f"{L}.cn.{u}"))
                    for m in range(MT):
                        act.wait_ge(*at.own())
                        act.activation(sqs, cn(u, m), ACT.Square, accum_out=ssq[u][:, m:m + 1]).then_inc(*at.step(f"{L}.ssq.{u}"))
                    act.wait_ge(*at.done(f"{L}.msq.{u}"))
                    act.activation(ssq[u], ssq[u], ACT.Sqrt).then_inc(*at.step(f"{L}.rms.{u}"))

                def scores_out(u, h):
                    m0, mt = HALF[h]
                    w = mt * S
                    act.wait_ge(*at.done(f"{L}.S{h}.{u}"))
                    act.wait_ge(*at.done(f"{L}.T{h}.{1 - u}", back=1 - u))
                    act.activation(ss[:, m0 * P:(m0 + mt) * P].rearrange("p (a m) -> p a m", a=2),
                                   PS[0:S, 2 * h:2 * h + 2, 0:w], ACT.Copy).then_inc(*at.step(f"{L}.S{h}.{u}.out"))

                def exps(u, h):
                    m0, mt = HALF[h]
                    x = A_[u][:, m0:m0 + mt, :]
                    act.wait_ge(*at.done(f"{L}.sub{h}.{u}"))
                    act.activation(x, x, ACT.Exp).then_inc(*at.step(f"{L}.exp{h}.{u}"))

                def updates_out(b, u):
                    act.wait_ge(*at.done(f"{L}.UT.{u}"))
                    act.activation(UP[:, :, bass.ds(b * (2 * S) + u * S, S)],
                                   PS[:, 4 + u, 0:KC * S].rearrange("p (c k) -> p c k", c=KC), ACT.Copy)\
                        .then_inc(*at.step(f"{L}.ut.{u}"))

                with at.loop(act, L, B // 2) as b:
                    if it == 0:
                        squares(0)
                    scores_out(0, 0)
                    scores_out(0, 1)
                    exps(0, 0)
                    scores_out(1, 0)
                    exps(0, 1)
                    scores_out(1, 1)
                    if it == 0:
                        squares(1)
                    exps(1, 0)
                    exps(1, 1)
                    updates_out(b, 0)
                    updates_out(b, 1)

                def high(k):
                    w = f"{p}.{GRU[k][0]}"
                    act.wait_ge(*at.done(w))
                    if k >= 2:
                        act.wait_ge(*at.done(f"{p}.{GRU[k - 2][0]}.used"))
                    act.activation(GH[k % 2][:, :, :], wt(w)[:, :, :], ACT.Copy).then_inc(*at.step(w + ".high"))

                for c in range(KC):
                    act.activation(SLH[:, c, :], SL[:, c, :], ACT.Copy).then_inc(*at.step(f"{p}.state.high{c}"))
                high(0)
                high(1)
                for c in range(KC):
                    act.wait_ge(*at.done(f"{p}.v.{c}"))
                    act.activation(SN[:, c, :], bank(c), ACT.Copy).then_inc(*at.step())
                    act.activation(SNH[:, c, :], bank(c), ACT.Copy).then_inc(*at.step(f"{p}.v.{c}.out"))
                high(2)
                for c in range(KC):
                    act.wait_ge(*at.done(f"{p}.r.{c}"))
                    act.wait_ge(*at.done("s1.bsum"))
                    act.activation(RG[:, c, :], bank(c), ACT.Sigmoid, bias=bsum[:, c:c + 1]).then_inc(*at.step(f"{p}.r.{c}.out"))
                for k in (3, 4, 5):
                    high(k)
                for c in range(KC):
                    act.wait_ge(*at.done(f"{p}.pre.{c}"))
                    act.activation(UP[:, c, :], UP[:, c, :], ACT.Tanh, bias=v("bih", 8 + c)).then_inc(*at.step(f"{p}.n.{c}"))
                if it == 2 and 2 in stages:
                    diagonals_act(act, at, range(DIAGS))
                for c in range(KC):
                    act.wait_ge(*at.done(f"{p}.z.{c}"))
                    act.activation(ZG[:, c, :], bank(c), ACT.Sigmoid, bias=bsum[:, 4 + c:5 + c]).then_inc(*at.step(f"{p}.z.{c}.out"))

        pw = RC[:, 2560:2560 + S * KC * N_STATE].rearrange("p (j c n) -> p j c n", j=S, c=KC)

        CONV_DVE = 2
        CONV_PE = range(CONV_DVE, KC)
        SHARED = 1
        dve_shares = [(c, 0, B) for c in range(CONV_DVE)] + [(CONV_DVE, 0, SHARED)]
        pe_from = {c: SHARED if c == CONV_DVE else 0 for c in CONV_PE}
        LAGS = 8
        DIAGS = 6
        lag_groups = [(c, g) for c in CONV_PE for g in range(S // LAGS)]

        def diag(c, j):
            k = ((c - CONV_DVE) * S + j) % (DIAGS * LAGS)
            return RB[:, k * P:(k + 1) * P]

        def diagonals_act(act, at, which):
            act.wait_ge(*at.done("s2.response"))
            for n in which:
                c, g = lag_groups[n]
                if n >= DIAGS:
                    act.wait_ge(*at.done("s2.lags.{}.{}".format(*lag_groups[n - DIAGS])))
                for j in range(g * LAGS, (g + 1) * LAGS):
                    act.activation(diag(c, j), C["ident"], ACT.Copy, scale=kconv[:, c, j:j + 1]).then_inc(*at.step(f"s2.diag.{c}.{g}"))

        def response_dve(dve, at):
            dve.wait_ge(*at.done("s2.powers"))
            dve.tensor_reduce(kconv[:, :, :].rearrange("p c j -> p j c"), pw, AX.X, ALU.add).then_inc(*at.step())
            dve.wait_ge(*at.own())
            dve.tensor_tensor(kconv[:, :, 0:1], kconv[:, :, 0:1], vec[:, VAT["D"]:VAT["D"] + 4].unsqueeze(2), ALU.add).then_inc(*at.step("s2.response"))
            dve.wait_ge(*at.own())

        def s1_dve(dve, at):
            dve.wait_ge(*at.done("consts"))
            dve.tensor_tensor(bsum[:, :], vec[:, VAT["bih"]:VAT["bih"] + 12], vec[:, VAT["bhh"]:VAT["bhh"] + 12], ALU.add)\
                .then_inc(*at.step("s1.bsum"))
            dve.tensor_scalar(inws[:, :], vec[:, VAT["in_w"]:VAT["in_w"] + 4], D ** -0.5, None, ALU.mult)\
                .then_inc(*at.step("s1.inws"))
            norm_dve(dve, at, "s1.ln", X, SL, xc=SN)
            for it in range(3):
                p, L = f"s1.{it}", f"s1.{it}.loop"
                norm_dve(dve, at, f"{p}.rms", SL, SN, w="slot_w", centred=False)
                for c in range(KC):
                    dve.wait_ge(*at.done(f"{p}.qk.{c}.out"))

                def slots(b, u):
                    dve.wait_ge(*at.done(f"{L}.S1.{u}", back=1))
                    dve.tensor_copy(qb[u], SN[:, :, bass.ds(b * (2 * S) + u * S, S)]).then_inc(*at.step(f"{L}.qb.{u}"))

                def inverse_rms(b, u):
                    dve.wait_ge(*at.done(f"{L}.ssq.{u}"))
                    dve.tensor_scalar(ssq[u], ssq[u], 1.0 / D, 1e-6, ALU.mult, ALU.add).then_inc(*at.step(f"{L}.msq.{u}"))
                    dve.wait_ge(*at.done(f"{L}.rms.{u}"))
                    dve.reciprocal(RN[:, b * 2 + u, :], ssq[u]).then_inc(*at.step(f"{L}.rinv.{u}"))
                    dve.wait_ge(*at.own())

                def spread(a, mt):
                    return a.unsqueeze(2).broadcast_to([P, mt, S])

                def shifted(b, u, h):
                    m0, mt = HALF[h]
                    x, mx = A_[u][:, m0:m0 + mt, :], stat[u][h][:, 0:mt]
                    dve.wait_ge(*at.done(f"{L}.T{h}.{u}"))
                    dve.wait_ge(*at.done(f"{L}.den.{u}", back=1))
                    dve.tensor_tensor(x, PS[:, 4 + h, 0:mt * S].rearrange("p (m k) -> p m k", k=S),
                                      spread(RN[:, b * 2 + u, m0:m0 + mt], mt), ALU.mult).then_inc(*at.step(f"{L}.st{h}.{u}"))
                    dve.wait_ge(*at.own())
                    dve.tensor_reduce(mx, x, AX.X, ALU.max).then_inc(*at.step())
                    dve.wait_ge(*at.own())
                    dve.tensor_tensor(x, x, spread(mx, mt), ALU.subtract).then_inc(*at.step(f"{L}.sub{h}.{u}"))

                def weights(b, u, h):
                    m0, mt = HALF[h]
                    x, sm = A_[u][:, m0:m0 + mt, :], stat[u][2 + h][:, 0:mt]
                    dve.wait_ge(*at.done(f"{L}.exp{h}.{u}"))
                    dve.tensor_reduce(sm, x, AX.X, ALU.add).then_inc(*at.step())
                    dve.wait_ge(*at.own())
                    dve.reciprocal(sm, sm).then_inc(*at.step())
                    dve.wait_ge(*at.own())
                    if h:
                        dve.tensor_tensor(sm[:, mt - 1:mt], sm[:, mt - 1:mt], row("in_last", 1), ALU.mult).then_inc(*at.step())
                        dve.wait_ge(*at.own())
                    dve.tensor_tensor(x, x, spread(sm, mt), ALU.mult).then_inc(*at.step())
                    dve.wait_ge(*at.own())
                    dve.wait_ge(*at.done(f"{L}.U.{u}", back=1))
                    dve.tensor_tensor(AR[u][:, m0:m0 + mt, :], x, spread(RN[:, b * 2 + u, m0:m0 + mt], mt), ALU.mult)\
                        .then_inc(*at.step(f"{L}.ar{h}.{u}"))
                    if h:
                        dve.tensor_reduce(asum[u], A_[u].rearrange("p m k -> p k m"), AX.X, ALU.add)\
                            .then_inc(*at.step(f"{L}.asum.{u}"))

                def normalise(u):
                    dve.wait_ge(*at.done(f"{L}.den.{u}"))
                    dve.tensor_scalar(rden[u], PS[0:S, 4 + u, 448:449], 1e-6, None, ALU.add).then_inc(*at.step())
                    dve.wait_ge(*at.own())
                    dve.reciprocal(rden[u], rden[u]).then_inc(*at.step())
                    dve.wait_ge(*at.own())
                    dve.wait_ge(*at.done(f"{L}.U.{u}"))
                    dve.wait_ge(*at.done(f"{L}.UT.{u}", back=1))
                    dve.tensor_scalar(UN[u], PS[0:S, 6 + u, :], rden[u], None, ALU.mult).then_inc(*at.step(f"{L}.un.{u}"))

                with at.loop(dve, L, B // 2) as b:
                    slots(b, 0)
                    slots(b, 1)
                    if it == 0:
                        inverse_rms(b, 0)
                    shifted(b, 0, 0)
                    shifted(b, 0, 1)
                    weights(b, 0, 0)
                    weights(b, 0, 1)
                    if it == 0:
                        inverse_rms(b, 1)
                    shifted(b, 1, 0)
                    shifted(b, 1, 1)
                    weights(b, 1, 0)
                    normalise(0)
                    weights(b, 1, 1)
                    normalise(1)
                dve.wait_ge(*at.done(f"{L}.ut.1"))
                for c in range(KC):
                    dve.tensor_scalar(UP[:, c, :], UP[:, c, :], v("in_w", c), None, ALU.mult).then_inc(*at.step(f"{p}.utw"))

                def low(k):
                    w = f"{p}.{GRU[k][0]}"
                    dve.wait_ge(*at.done(w + ".high"))
                    dve.tensor_tensor(ring_part[slot[w]][:, :, :], wt(w)[:, :, :], GH[k % 2][:, :, :].bitcast(FP32),
                                      ALU.subtract).then_inc(*at.step(w + ".low"))

                for c in range(KC):
                    dve.wait_ge(*at.done(f"{p}.state.high{c}"))
                    dve.tensor_tensor(SLL[:, c, :], SL[:, c, :], SLH[:, c, :].bitcast(FP32), ALU.subtract).then_inc(*at.step(f"{p}.state.low{c}"))
                low(0)
                low(1)
                for c in range(KC):
                    dve.wait_ge(*at.done(f"{p}.v.{c}.out"))
                    dve.tensor_tensor(SNL[:, c, :], SN[:, c, :], SNH[:, c, :].bitcast(FP32), ALU.subtract).then_inc(*at.step(f"{p}.update.low{c}"))
                low(2)
                low(3)
                if it == 2 and 2 in stages:
                    response_dve(dve, at)
                for c in range(KC):
                    dve.wait_ge(*at.done(f"{p}.gh.{c}"))
                    dve.wait_ge(*at.done(f"{p}.r.{c}.out"))
                    dve.scalar_tensor_tensor(out=UP[:, c, :], in0=bank(c), scalar=v("bhh", 8 + c), in1=RG[:, c, :],
                                             op0=ALU.add, op1=ALU.mult).then_inc(*at.step(f"{p}.gh.{c}.out"))
                low(4)
                for c in range(KC):
                    dve.wait_ge(*at.own())
                    dve.wait_ge(*at.done(f"{p}.gx.{c}"))
                    dve.tensor_tensor(UP[:, c, :], UP[:, c, :], bank(4 + c), ALU.add).then_inc(*at.step(f"{p}.pre.{c}"))
                    at.same(f"{p}.gx.{c}.out", f"{p}.pre.{c}")
                low(5)
                for c in range(KC):
                    dve.wait_ge(*at.done(f"{p}.n.{c}"))
                    dve.tensor_tensor(RG[:, c, :], SL[:, c, :], UP[:, c, :], ALU.subtract).then_inc(*at.step())
                for c in range(KC):
                    dve.wait_ge(*at.done(f"{p}.z.{c}.out"))
                    dve.wait_ge(*at.own())
                    dve.tensor_tensor(RG[:, c, :], RG[:, c, :], ZG[:, c, :], ALU.mult).then_inc(*at.step())
                dve.wait_ge(*at.done(f"{p}.z.3"))
                dve.wait_ge(*at.own())
                for c in range(KC):
                    dve.tensor_tensor(SL[:, c, :], UP[:, c, :], RG[:, c, :], ALU.add).then_inc(*at.step(f"{p}.sl.{c}"))
                at.same(f"{p}.sl")
            dve.wait_ge(*at.own())
            for c in range(KC):
                dve.tensor_tensor(X[:, c, :], X[:, c, :], SL[:, c, :], ALU.add).then_inc(*at.step(f"x1.{c}"))
            at.same("x1")

        def high_at(k):
            return WH[2] if k == 0 else WH[k % 2]

        def expert_pe(pe, at, tag, w, inloop):
            def hidden(s, k):
                pe.wait_ge(*at.done(w(k) + ".low"))
                for oc in range(KC):
                    if s:
                        pe.wait_ge(*at.done(f"{tag}.h{s - 1}.{oc}.out"))
                    elif inloop:
                        pe.wait_ge(*at.done(f"{tag}.h3.{oc}.out", back=1))
                    for c in range(KC):
                        mm = triple(pe, bank(oc), high_at(k), w(k), c, oc, XH[:, c, :], XL[:, c, :], c == 0, c == KC - 1)
                    mm.then_inc(*at.step(f"{tag}.h{s}.{oc}"))
                at.same(w(k) + ".used", f"{tag}.h{s}.3")

            def output(s, k):
                pe.wait_ge(*at.done(w(k) + ".low"))
                for oc in range(KC):
                    if s == 0 and inloop:
                        pe.wait_ge(*at.done(f"{tag}.y{oc}.out", back=1))
                    for c in range(KC):
                        if oc == 0:
                            pe.wait_ge(*at.done(f"{tag}.h{s}.{c}.low"))
                        mm = triple(pe, bank(4 + oc), high_at(k), w(k), c, oc, HH[s % 2][:, c, :], HL[s % 2][:, c, :],
                                    s == 0 and c == 0, s == FS - 1 and c == KC - 1)
                    if s == FS - 1:
                        mm.then_inc(*at.step(f"{tag}.y{oc}"))
                if s < FS - 1:
                    mm.then_inc(*at.step(f"{tag}.Y{s}"))
                else:
                    at.same(f"{tag}.Y{s}", f"{tag}.y3")
                at.same(w(k) + ".used", f"{tag}.Y{s}")

            for k, x in enumerate(EXPERT):
                (hidden if x[0] == "a" else output)(int(x[1]), k)

        def expert_act(act, at, tag, w, func, bias, raw, inloop):
            def high(k):
                act.wait_ge(*at.done(w(k)))
                if k >= 3:
                    act.wait_ge(*at.done(w(k - 2) + ".used"))
                elif inloop:
                    act.wait_ge(*at.done(w((0, 7, 6)[k]) + ".used", back=1))
                act.activation(high_at(k)[:, :, :], wt(w(k))[:, :, :], ACT.Copy).then_inc(*at.step(w(k) + ".high"))

            high(0)
            for k, x in enumerate(EXPERT):
                if k + 1 < len(EXPERT):
                    high(k + 1)
                if x[0] != "a":
                    continue
                s = int(x[1])
                if s >= 2:
                    act.wait_ge(*at.done(f"{tag}.Y{s - 2}"))
                elif inloop:
                    act.wait_ge(*at.done(f"{tag}.Y{s + 2}", back=1))
                for oc in range(KC):
                    act.wait_ge(*at.done(f"{tag}.h{s}.{oc}"))
                    if s:
                        act.wait_ge(*at.done(f"{tag}.h{s - 1}.{oc}.low"))
                    elif inloop:
                        act.wait_ge(*at.done(f"{tag}.h3.{oc}.low", back=1))
                    act.activation(raw[:, oc, :], bank(oc), func, bias=bias(4 * s + oc)).then_inc(*at.step())
                    act.activation(HH[s % 2][:, oc, :], bank(oc), func, bias=bias(4 * s + oc)).then_inc(*at.step(f"{tag}.h{s}.{oc}.out"))

        def first_low_pool(pool, at, w):
            pool.wait_ge(*at.done(w(0) + ".high"))
            pool.tensor_tensor(ring_part[slot[w(0)]][:, :, :], wt(w(0))[:, :, :], high_at(0)[:, :, :].bitcast(FP32),
                               ALU.subtract).then_inc(*at.step(w(0) + ".low"))

        def expert_dve(dve, at, tag, w, raw):
            for k, x in enumerate(EXPERT):
                if k + 1 < len(EXPERT):
                    dve.wait_ge(*at.done(w(k + 1) + ".high"))
                    dve.tensor_tensor(ring_part[slot[w(k + 1)]][:, :, :], wt(w(k + 1))[:, :, :], high_at(k + 1)[:, :, :].bitcast(FP32),
                                      ALU.subtract).then_inc(*at.step(w(k + 1) + ".low"))
                if x[0] == "a":
                    s = int(x[1])
                    for oc in range(KC):
                        dve.wait_ge(*at.done(f"{tag}.h{s}.{oc}.out"))
                        dve.tensor_tensor(HL[s % 2][:, oc, :], raw[:, oc, :], HH[s % 2][:, oc, :].bitcast(FP32),
                                          ALU.subtract).then_inc(*at.step(f"{tag}.h{s}.{oc}.low"))

        def split_act(act, at, tag, x, ready):
            for c in range(KC):
                act.wait_ge(*at.done(f"{ready}.{c}"))
                act.activation(XH[:, c, :], x[:, c, :], ACT.Copy).then_inc(*at.step(f"{tag}.high{c}"))

        def split_dve(dve, at, tag, x):
            for c in range(KC):
                dve.wait_ge(*at.done(f"{tag}.high{c}"))
                dve.tensor_tensor(XL[:, c, :], x[:, c, :], XH[:, c, :].bitcast(FP32), ALU.subtract).then_inc(*at.step(f"{tag}.split"))

        abc = RC[:, 1600:1792].rearrange("p (a c n) -> p a c n", a=3, c=KC)
        R2, N2, Y2 = TS[0], TS[1], TS[2]
        xn, y = (a[:, :, :].rearrange("p c (b s) -> p c b s", b=B) for a in (N2, Y2))


        def FFN(k):
            return f"s2.ffn{1 if EXPERT[k][0] == 'a' else 2}_{EXPERT[k][1]}"

        def s2_pool(pool, at):
            pool.wait_ge(*at.done("s2.decay"))
            pool.tensor_tensor(pw[:, 0], abc[:, 1], abc[:, 2], ALU.mult).then_inc(*at.step())
            for j in range(1, S):
                pool.wait_ge(*at.own())
                pool.tensor_tensor(pw[:, j], pw[:, j - 1], abc[:, 0], ALU.mult).then_inc(*at.step("s2.powers"))
            first_low_pool(pool, at, FFN)

        def s2_pe(pe, at):
            norm_pe(pe, at, "s2.ln", X, chunk_steps("x1.") if 1 in stages else ["x"])
            norm_pe(pe, at, "s2.ln1", R2, chunk_steps("s2.ln.done."))
            pe.wait_ge(*at.done("s2.ln1.done"))
            for c in CONV_PE:
                if bank_reader.get(c):
                    pe.wait_ge(*at.done(bank_reader[c]))
                y = bank(c).rearrange("p (b s) -> p b s", b=B)
                for j in range(S):
                    if j % LAGS == 0:
                        pe.wait_ge(*at.done(f"s2.diag.{c}.{j // LAGS}"))
                    mm = pe.matmul(y[:, pe_from[c]:B, j:S], diag(c, j), xn[:, c, pe_from[c]:B, 0:S - j], start=(j == 0), stop=(j == S - 1))
                    if j % LAGS == LAGS - 1:
                        mm.then_inc(*at.step(f"s2.lags.{c}.{j // LAGS}"))
                bank_reader[c] = "s2.silu"
            linear_pe(pe, at, "s2.out", [("s2.out", Y2)], (0, 1, 2, 3), range(KC), ["s2.silu"])
            norm_pe(pe, at, "s2.ln2", R2, chunk_steps("s2.out.", ".out"))
            for due in at.last("s2.split", *(f"s2.out.{c}.out" for c in range(KC))):
                pe.wait_ge(*due)
            expert_pe(pe, at, "s2.ffn", FFN, False)
            bank_reader.update({k: f"s2.ffn.h3.{k}.out" for k in range(4)})
            bank_reader.update({4 + k: f"s2.ffn.y{k}.out" for k in range(4)})

        def s2_act(act, at):
            if 1 not in stages:
                diagonals_act(act, at, range(DIAGS))
            norm_act(act, at, "s2.ln", X, "eps5", xc=N2)
            norm_act(act, at, "s2.ln1", R2, "eps5", xc=N2)
            diagonals_act(act, at, range(DIAGS, len(lag_groups)))
            for c in CONV_PE:
                act.wait_ge(*at.done(f"s2.lags.{c}.{S // LAGS - 1}"))
                n = pe_from[c] * S
                act.activation(Y2[:, c, n:T], bank(c)[:, n:T], ACT.Silu).then_inc(*at.step())
            act.wait_ge(*at.done("s2.conv"))
            for c, b0, b1 in dve_shares:
                act.activation(Y2[:, c, b0 * S:b1 * S], Y2[:, c, b0 * S:b1 * S], ACT.Silu).then_inc(*at.step("s2.silu"))
            norm_act(act, at, "s2.ln2", R2, "eps5", xc=N2)
            split_act(act, at, "s2", N2, "s2.ln2.done")
            expert_act(act, at, "s2.ffn", FFN, ACT.Gelu, lambda k: v("ffn1_b", k), TS[3], False)

        def s2_dve(dve, at):
            if 1 not in stages:
                response_dve(dve, at)
            norm_dve(dve, at, "s2.ln", X, R2, xc=N2)
            dve.wait_ge(*at.own())
            norm_dve(dve, at, "s2.ln1", R2, N2, w="ln_w", b="ln_b", xc=N2)
            for c, b0, b1 in dve_shares:
                dve.tensor_scalar(Y2[:, c, b0 * S:b1 * S], N2[:, c, b0 * S:b1 * S], kconv[:, c, 0:1], None, ALU.mult).then_inc(*at.step("s2.conv"))
            for j in range(1, S):
                for c, b0, b1 in dve_shares:
                    dve.wait_ge(sems["vector_done"], at.count["vector_done"] - len(dve_shares) + 1)
                    dve.scalar_tensor_tensor(out=y[:, c, b0:b1, j:S], in0=xn[:, c, b0:b1, 0:S - j], scalar=kconv[:, c, j:j + 1],
                                                 in1=y[:, c, b0:b1, j:S], op0=ALU.mult, op1=ALU.add).then_inc(*at.step("s2.conv"))
            for c in range(KC):
                dve.wait_ge(*at.done(f"s2.out.{c}"))
                dve.scalar_tensor_tensor(out=R2[:, c, :], in0=bank(c), scalar=v("out_b", c), in1=R2[:, c, :],
                                             op0=ALU.add, op1=ALU.add).then_inc(*at.step(f"s2.out.{c}.out"))
            at.same("s2.res", "s2.out.3.out")
            dve.wait_ge(*at.own())
            norm_dve(dve, at, "s2.ln2", R2, N2, w="ln2_w", b="ln2_b", xc=N2)
            split_dve(dve, at, "s2", N2)
            for c in range(KC):
                dve.tensor_tensor(X[:, c, :], X[:, c, :], R2[:, c, :], ALU.add).then_inc(*at.step())
            expert_dve(dve, at, "s2.ffn", FFN, TS[3])
            for c in range(KC):
                dve.wait_ge(*at.done(f"s2.ffn.y{c}"))
                dve.wait_ge(*at.own())
                dve.scalar_tensor_tensor(out=X[:, c, :], in0=bank(4 + c), scalar=v("ffn2_b", c), in1=X[:, c, :],
                                             op0=ALU.add, op1=ALU.add).then_inc(*at.step(f"s2.ffn.y{c}.out"))
            at.same("x2", "s2.ffn.y3.out")

        KBD = [RB4[0], RB4[1]]
        PT = RC4[1]
        probs = [x.rearrange("p c (h k) -> p (c h) k", k=P) for x in (RC4[0], RA4[0])]
        least = [misc[:, 0:H], misc[:, 16:16 + H]]
        sums = [misc[:, 32:32 + H], misc[:, 48:48 + H]]
        probsT = PT.rearrange("p c (h k) -> p (c h) k", k=P)
        NBP = T // P
        HALF_H = H // 2

        def attn_pool(pool, at, tag, K, ready):
            for x in KBD:
                pool.memset(x[:, :, :], 0.0).then_inc(*at.step(f"{tag}.zero"))
            pool.wait_ge(*at.own())
            for due in at.last(*ready):
                pool.wait_ge(*due)
            for bp in range(1, NBP):
                if bp >= 2:
                    pool.wait_ge(*at.done(f"{tag}.S{bp - 2}"))
                for a in range(G):
                    pool.tensor_copy(KBD[bp % 2][a * HD:(a + 1) * HD, :, a * P:(a + 1) * P],
                                        K[a * HD:(a + 1) * HD, :, bp * P:(bp + 1) * P]).then_inc(*at.step(f"{tag}.kb{bp}"))

        def attn_pe(pe, at, tag, Q, V, ready):
            def scores(bp):
                pe.wait_ge(*at.done(f"{tag}.kb{bp}"))
                for g in range(KC):
                    if bp:
                        pe.wait_ge(*at.done(f"{tag}.masked{bp - 1}.{g // 2}"))
                    elif bank_reader.get(g):
                        pe.wait_ge(*at.done(bank_reader[g]))
                    mm = pe.matmul(bank(g), Q[:, g, bp * P:(bp + 1) * P], KBD[bp % 2][:, g, :], start=True, stop=True)
                    if g % 2:
                        mm.then_inc(*at.step(f"{tag}.S{bp}.{g // 2}"))
                at.same(f"{tag}.S{bp}")

            def values(bp):
                for g in range(KC):
                    pe.wait_ge(*at.done(f"{tag}.p{bp}.{g // 2}"))
                    k = 4 + g % 3
                    if bank_reader.get(k):
                        pe.wait_ge(*at.done(bank_reader[k]))
                    for a in range(G):
                        mm = pe.transpose(PS[:, k, a * P:(a + 1) * P], probs[bp % 2][:, G * g + a, :], C["ident"])
                    mm.then_inc(*at.step(f"{tag}.T{bp}.{g}"))
                    bank_reader[k] = f"{tag}.T{bp}.{g}.out"
                if bank_reader.get(7):
                    pe.wait_ge(*at.done(bank_reader[7]))
                for g in range(KC):
                    pe.wait_ge(*at.done(f"{tag}.T{bp}.{g}.out"))
                    for a in range(G):
                        h = G * g + a
                        mm = pe.matmul(PS[a * HD:(a + 1) * HD, 7, g * P:(g + 1) * P], V[:, bp, h * HD:(h + 1) * HD],
                                          probsT[:, h, :], start=True, stop=True)
                mm.then_inc(*at.step(f"{tag}.O{bp}"))
                bank_reader[7] = f"{tag}.O{bp}.out"

            for due in at.last(*ready):
                pe.wait_ge(*due)
            scores(0)
            scores(1)
            for bp in range(NBP):
                values(bp)
                if bp + 2 < NBP:
                    scores(bp + 2)
            for g in range(KC):
                bank_reader[g] = f"{tag}.masked{NBP - 1}.1"

        def attn_act(act, at, tag):
            def exps(bp):
                for h in range(H):
                    if h % HALF_H == 0:
                        act.wait_ge(*at.done(f"{tag}.least{bp}.{h // HALF_H}"))
                    act.activation(probs[bp % 2][:, h, :], probs[bp % 2][:, h, :], ACT.Exp, bias=least[bp % 2][:, h:h + 1],
                                   accum_out=sums[bp % 2][:, h:h + 1]).then_inc(*at.step(f"{tag}.exp{bp}.{h // HALF_H}"))

            exps(0)
            exps(1)
            for bp in range(NBP):
                for g in range(KC):
                    act.wait_ge(*at.done(f"{tag}.T{bp}.{g}"))
                    if bp:
                        act.wait_ge(*at.done(f"{tag}.O{bp - 1}"))
                    act.activation(PT[:, g, :], bank(4 + g % 3), ACT.Copy).then_inc(*at.step(f"{tag}.T{bp}.{g}.out"))
                if bp and bp + 1 < NBP:
                    exps(bp + 1)

        def attn_dve(dve, at, tag, K, ready, O, mask):
            dve.wait_ge(*at.done(f"{tag}.zero"))
            for due in at.last(*ready):
                dve.wait_ge(*due)
            for a in range(G):
                dve.tensor_copy(KBD[0][a * HD:(a + 1) * HD, :, a * P:(a + 1) * P],
                                K[a * HD:(a + 1) * HD, :, 0:P]).then_inc(*at.step(f"{tag}.kb0"))

            def maxima(bp):
                if bp >= 2:
                    dve.wait_ge(*at.done(f"{tag}.T{bp - 2}.3"))
                for q in (0, 1):
                    dve.wait_ge(*at.done(f"{tag}.S{bp}.{q}"))
                    x, m = probs[bp % 2][:, q * HALF_H:(q + 1) * HALF_H, :], least[bp % 2][:, q * HALF_H:(q + 1) * HALF_H]
                    dve.scalar_tensor_tensor(out=x, in0=PS[:, 2 * q:2 * q + 2, :].rearrange("p g (a k) -> p (g a) k", k=P),
                                                 scalar=HD ** -0.5, in1=mask.unsqueeze(1).broadcast_to([P, HALF_H, P]),
                                                 op0=ALU.mult, op1=ALU.add).then_inc(*at.step(f"{tag}.masked{bp}.{q}"))
                    dve.wait_ge(*at.own())
                    dve.tensor_reduce(m, x, AX.X, ALU.max).then_inc(*at.step())
                    dve.wait_ge(*at.own())
                    dve.tensor_scalar(m, m, -1.0, None, ALU.mult).then_inc(*at.step(f"{tag}.least{bp}.{q}"))

            def out(bp):
                dve.wait_ge(*at.done(f"{tag}.O{bp}"))
                dve.tensor_copy(O[:, :, bp * P:(bp + 1) * P], PS[:, 7, :].rearrange("p (g k) -> p g k", k=P)).then_inc(*at.step(f"{tag}.O{bp}.out"))

            maxima(0)
            maxima(1)
            for bp in range(NBP):
                for q in (0, 1):
                    x, sm = probs[bp % 2][:, q * HALF_H:(q + 1) * HALF_H, :], sums[bp % 2][:, q * HALF_H:(q + 1) * HALF_H]
                    dve.wait_ge(*at.done(f"{tag}.exp{bp}.{q}"))
                    dve.reciprocal(sm, sm).then_inc(*at.step())
                    dve.wait_ge(*at.own())
                    dve.tensor_tensor(x, x, sm.unsqueeze(2).broadcast_to([P, HALF_H, P]), ALU.mult).then_inc(*at.step(f"{tag}.p{bp}.{q}"))
                if bp:
                    out(bp - 1)
                    if bp + 1 < NBP:
                        maxima(bp + 1)
            out(NBP - 1)

        def values_pe(pe, at, tag, w, x, banks):
            for tt in range(T // P):
                k = banks[tt % len(banks)]
                if bank_reader.get(k):
                    pe.wait_ge(*at.done(bank_reader[k]))
                if tt == 0:
                    pe.wait_ge(*at.done(w))
                for c in range(KC):
                    mm = pe.matmul(bank(k), x[:, c, tt * P:(tt + 1) * P], wt(w)[:, c, :], start=(c == 0), stop=(c == KC - 1))
                mm.then_inc(*at.step(f"{tag}.{tt}"))
                bank_reader[k] = f"{tag}.{tt}.out"
            at.same(w + ".used", f"{tag}.3")

        def values_dve(dve, at, tag, V, bias, banks):
            for tt in range(T // P):
                dve.wait_ge(*at.done(f"{tag}.{tt}"))
                dve.tensor_tensor(V[:, tt, :], bank(banks[tt % len(banks)]), row(bias, D), ALU.add).then_inc(*at.step(f"{tag}.{tt}.out"))

        XPAD = RC[:, 4200:4200 + KC * B * (S + 2)].rearrange("p (c b s) -> p c b s", c=KC, b=B)
        X3, Q3, K3, V3, O3 = TS[1], TS[2], TS[3], TS[4], TS[0]

        def MOE(k):
            return f"s3.moe.{EXPERT[k]}"

        PB = RA[:, 0:E_ * T].rearrange("p (e t) -> p e t", e=E_)
        gl = misc[:, 64:96].rearrange("p (a e) -> p a e", e=E_)
        gm, gs = misc[:, 96:100], misc[:, 100:104]
        gT = misc[0:E_, 0:0 + 512]
        ga = RC[:, 0:32].rearrange("p (a e) -> p a e", e=E_)
        gst = RC[:, 64:128]

        def gate_pe(pe, at, tag, x, w, after):
            for due in at.last(*after):
                pe.wait_ge(*due)
            if bank_reader.get(0):
                pe.wait_ge(*at.done(bank_reader[0]))
            for tt in range(T // P):
                for c in range(KC):
                    mm = pe.matmul(PS[:, 0, tt * E_:(tt + 1) * E_], x[:, c, tt * P:(tt + 1) * P], gw[:, w, c, :],
                                      start=(c == 0), stop=(c == KC - 1))
            mm.then_inc(*at.step(f"{tag}.logits"))
            bank_reader[0] = f"{tag}.logits.out"

        def gate_act(act, at, tag):
            act.wait_ge(*at.done(f"{tag}.sub"))
            act.activation(ga, ga, ACT.Exp).then_inc(*at.step(f"{tag}.exp"))

        def gate_dve(dve, at, tag, bias):
            ps = PS[:, 0, 0:32].rearrange("p (a e) -> p a e", e=E_)
            bc = lambda a: a.unsqueeze(2).broadcast_to([P, 4, E_])
            dve.wait_ge(*at.done(f"{tag}.logits"))
            if bias:
                dve.tensor_tensor(ga, ps, row("gate_b", E_).unsqueeze(1).broadcast_to([P, 4, E_]), ALU.add).then_inc(*at.step(f"{tag}.logits.out"))
            else:
                dve.tensor_copy(ga, ps).then_inc(*at.step(f"{tag}.logits.out"))
            dve.wait_ge(*at.own())
            dve.tensor_reduce(gst[:, 0:4], ga, AX.X, ALU.max).then_inc(*at.step())
            dve.wait_ge(*at.own())
            dve.tensor_tensor(ga, ga, bc(gst[:, 0:4]), ALU.subtract).then_inc(*at.step(f"{tag}.sub"))
            dve.wait_ge(*at.done(f"{tag}.exp"))
            dve.tensor_reduce(gst[:, 4:8], ga, AX.X, ALU.add).then_inc(*at.step())
            dve.wait_ge(*at.own())
            dve.reciprocal(gst[:, 4:8], gst[:, 4:8]).then_inc(*at.step())
            dve.wait_ge(*at.own())
            dve.tensor_tensor(ga, ga, bc(gst[:, 4:8]), ALU.mult).then_inc(*at.step(f"{tag}.probs"))

        def s3_pool(pool, at):
            if 2 in stages:
                pool.wait_ge(*at.done("x2"))
            pool.memset(XPAD[:, :, :, 0:1], 0.0).then_inc(*at.step())
            pool.memset(XPAD[:, :, :, S + 1:S + 2], 0.0).then_inc(*at.step("s3.pad"))
            attn_pool(pool, at, "s3.at", K3, [f"s3.k.{c}.out" for c in range(KC)])
            with at.loop(pool, "s3.loop", E_) as i:
                first_low_pool(pool, at, MOE)

        def s3_pe(pe, at):
            norm_pe(pe, at, "s3.ln", X, chunk_steps("s2.ffn.y", ".out") if 2 in stages else ["x"])
            for due in at.last("s3.padded", "s3.pad"):
                pe.wait_ge(*due)
            for oc in range(KC):
                if bank_reader.get(oc):
                    pe.wait_ge(*at.done(bank_reader[oc]))
                for k in range(3):
                    if oc == 0:
                        pe.wait_ge(*at.done(f"s3.conv{k}"))
                    for c in range(KC):
                        mm = pe.matmul(bank(oc), wt(f"s3.conv{k}")[:, c, oc * P:(oc + 1) * P], XPAD[:, c, :, k:k + S],
                                          start=(k == 0 and c == 0), stop=(k == 2 and c == KC - 1))
                mm.then_inc(*at.step(f"s3.cv.{oc}"))
                bank_reader[oc] = f"s3.cv.{oc}.out"
            for k in range(3):
                at.same(f"s3.conv{k}.used", "s3.cv.3")
            cv = [f"s3.cv.{c}.out" for c in range(KC)]
            linear_pe(pe, at, "s3.q", [("s3.wq", X3)], (4, 5, 6, 7), range(KC), cv)
            linear_pe(pe, at, "s3.k", [("s3.wk", X3)], (0, 1, 2, 3), range(KC))
            values_pe(pe, at, "s3.v", "s3.wv", X3, (4, 5, 6, 7))
            attn_pe(pe, at, "s3.at", Q3, V3, [f"s3.q.{c}.out" for c in range(KC)] + [f"s3.v.{c}.out" for c in range(4)])
            linear_pe(pe, at, "s3.o", [("s3.wo", O3)], (0, 1, 2, 3), range(KC), ["s3.at.O3.out"])
            norm_pe(pe, at, "s3.ln1", X3, [f"s3.o.{c}.out" for c in range(KC)])
            gate_pe(pe, at, "s3.g", X3, 0, ["s3.ln1.done"])
            pe.wait_ge(*at.done("s3.g.probs"))
            for tt in range(4):
                mm = pe.transpose(PS[0:E_, 1, tt * P:(tt + 1) * P], ga[:, tt, :], C["ident"])
            mm.then_inc(*at.step("s3.gT"))
            pe.wait_ge(*at.done("s3.gT.out"))
            for x in range(E_):
                k = 2 + x % 2
                if x >= 2:
                    pe.wait_ge(*at.done(f"s3.pb.{x - 2}.out"))
                mm = pe.matmul(bank(k), C["ident"][0:E_, x:x + 1].broadcast_to([E_, P]), gT, start=True, stop=True)
                mm.then_inc(*at.step(f"s3.pb.{x}"))
            for due in at.last("s3.pb.6.out", "s3.pb.7.out", "s3.split"):
                pe.wait_ge(*due)
            with at.loop(pe, "s3.loop", E_) as i:
                expert_pe(pe, at, "s3.moe", MOE, True)
            bank_reader.update({k: f"s3.moe.h3.{k}.out" for k in range(4)})
            bank_reader.update({4 + k: f"s3.moe.y{k}.out" for k in range(4)})
            norm_pe(pe, at, "s3.ln2", X3, chunk_steps("s3.x5."))

        def s3_act(act, at):
            norm_act(act, at, "s3.ln", X, "eps5", xc=TS[0])
            linear_out(act, at, "s3.cv", (0, 1, 2, 3), range(KC), lambda ps, c: act.activation(X3[:, c, :], ps, ACT.Identity, bias=v("conv_b", c)))
            linear_out(act, at, "s3.q", (4, 5, 6, 7), range(KC), lambda ps, c: act.activation(Q3[:, c, :], ps, ACT.Identity, bias=v("bqkv", c)))
            linear_out(act, at, "s3.k", (0, 1, 2, 3), range(KC), lambda ps, c: act.activation(K3[:, c, :], ps, ACT.Identity, bias=v("bqkv", 4 + c)))
            attn_act(act, at, "s3.at")
            norm_act(act, at, "s3.ln1", X3, "eps5", xc=X3)
            split_act(act, at, "s3", X3, "s3.ln1.done")
            gate_act(act, at, "s3.g")
            act.wait_ge(*at.done("s3.gT"))
            act.activation(gT, PS[0:E_, 1, :], ACT.Copy).then_inc(*at.step("s3.gT.out"))
            for x in range(E_):
                act.wait_ge(*at.done(f"s3.pb.{x}"))
                act.activation(PB[:, x, :], bank(2 + x % 2), ACT.Copy).then_inc(*at.step(f"s3.pb.{x}.out"))
            with at.loop(act, "s3.loop", E_) as i:
                expert_act(act, at, "s3.moe", MOE, ACT.Relu, lambda k: vec[:, bass.ds(i * 16 + (VAT["b1"] + k), 1)], TS[0], True)
            norm_act(act, at, "s3.ln2", X3, "eps5", xc=X3)

        def s3_dve(dve, at):
            norm_dve(dve, at, "s3.ln", X, TS[0], xc=TS[0])
            dve.wait_ge(*at.own())
            dve.tensor_copy(XPAD[:, :, :, 1:S + 1].rearrange("p c b s -> p (c b) s"),
                                TS[0][:, :, :].rearrange("p c (b s) -> p (c b) s", s=S)).then_inc(*at.step("s3.padded"))
            values_dve(dve, at, "s3.v", V3, "bv3", (4, 5, 6, 7))
            attn_dve(dve, at, "s3.at", K3, [f"s3.k.{c}.out" for c in range(KC)], O3, C["blockmask"])
            for c in range(KC):
                dve.wait_ge(*at.done(f"s3.o.{c}"))
                dve.scalar_tensor_tensor(out=X3[:, c, :], in0=bank(c), scalar=v("bo3", c), in1=X3[:, c, :],
                                             op0=ALU.add, op1=ALU.add).then_inc(*at.step(f"s3.o.{c}.out"))
            dve.wait_ge(*at.own())
            norm_dve(dve, at, "s3.ln1", X3, X3, w="ln1_g", b="ln1_b", xc=X3)
            gate_dve(dve, at, "s3.g", True)
            split_dve(dve, at, "s3", X3)
            acc, tmp = TS[2], TS[3]
            dve.memset(acc[:, :, :], 0.0).then_inc(*at.step("s3.acc0"))
            dve.wait_ge(*at.done("s3.pb.7.out"))
            with at.loop(dve, "s3.loop", E_) as i:
                expert_dve(dve, at, "s3.moe", MOE, TS[0])
                for c in range(KC):
                    dve.wait_ge(*at.done(f"s3.moe.y{c}"))
                    dve.wait_ge(*at.own())
                    dve.scalar_tensor_tensor(out=tmp[:, c, :], in0=bank(4 + c), scalar=vec[:, bass.ds(i * 4 + (VAT["b2"] + c), 1)],
                                                 in1=PB[:, i, :], op0=ALU.add, op1=ALU.mult).then_inc(*at.step(f"s3.moe.y{c}.out"))
                    dve.wait_ge(*at.own())
                    dve.tensor_tensor(acc[:, c, :], acc[:, c, :], tmp[:, c, :], ALU.add).then_inc(*at.step())
            dve.wait_ge(*at.own())
            dve.wait_ge(*at.done("s3.moe.y3"))
            for c in range(KC):
                dve.tensor_tensor(X3[:, c, :], X3[:, c, :], acc[:, c, :], ALU.add).then_inc(*at.step(f"s3.x5.{c}"))
            at.same("s3.x5")
            dve.wait_ge(*at.own())
            norm_dve(dve, at, "s3.ln2", X3, acc, w="ln2_g", b="ln2b3", xc=X3)
            dve.wait_ge(*at.own())
            for c in range(KC):
                dve.tensor_tensor(X[:, c, :], X[:, c, :], acc[:, c, :], ALU.add).then_inc(*at.step(f"x3.{c}"))
            at.same("x3")

        KT = RC[:, 0:KC * MP].rearrange("p (g m) -> p g m", g=KC)
        VT = RB[:, 0:MT * D].rearrange("p (m d) -> p m d", d=D)
        N4, Q4, O4 = TS[0], TS[2], TS[3]
        qd = TS[1][:, 2:4, :].rearrange("p a b -> p (a b)").rearrange("p (g h q) -> p g h q", g=KC, h=G)
        QD = TS[1][:, 2:4, :].rearrange("p a b -> p (a b)").rearrange("p (g r) -> p g r", g=KC)
        keep, flag = PTs[:, :, :].rearrange("p m k -> p (m k)"), misc[:, 0:1]
        NP = H // 2
        minus_max = [misc[:, 4:5], misc[:, 5:6]]
        top = [[misc[:, 8 + 2 * a + h:9 + 2 * a + h] for h in (0, 1)] for a in (0, 1)]
        total = [[misc[:, 12 + 2 * a + h:13 + 2 * a + h] for h in (0, 1)] for a in (0, 1)]
        TG = [(k, min(4, MT - k)) for k in range(0, MT, 4)]
        SCALE = HD ** -0.5
        W4 = {}
        if 4 in stages:
            W4 = {"wk": (ring_part[slot["s4.wo"]], ring_part[slot["s4.wk"]]), "wv": (ring_part[slot["s4.wq"]], ring_part[slot["s4.wv"]])}

        def s4_pool(pool, at):
            if 3 in stages:
                pool.wait_ge(*at.done("s3.x5"))
            with at.loop(pool, "s4.loop", B) as b:
                for h in (0, 1):
                    m0, mt = HALF[h]
                    pool.wait_ge(*at.done(f"s4.V{h}", back=1))
                    pool.nop(nofuse=True)
                    pool.dma_start(CT[h][:, :, :], t["ctxT"][b, :, :, m0 * P:(m0 + mt) * P]).then_inc(*at.load(f"ctxT_loaded{h}", f"s4.ct{h}"))
                pool.wait_ge(*at.done("s4.ct0"))
                pool.wait_ge(*at.done("s4.ln.done"))
                pool.wait_ge(*at.done("s4.V0", back=1))
                pool.nop(nofuse=True)
                pool.tensor_copy(CH[0][:, :, :], CT[0][:, :, :]).then_inc(*at.step("s4.high0"))
                pool.wait_ge(*at.own())
                pool.tensor_tensor(CL[0][:, :, :], CT[0][:, :, :], CH[0][:, :, :].bitcast(FP32), ALU.subtract).then_inc(*at.step("s4.low0"))

        def s4_pe(pe, at):
            norm_pe(pe, at, "s4.ln", X, chunk_steps("x3.") if 3 in stages else ["x"])
            linear_pe(pe, at, "s4.q", [("s4.wq", N4)], (0, 1, 2, 3), range(KC), chunks="s4.ln.done")
            for due in at.last("s4.wk.low", "s4.wv.low", *(f"s4.q.{c}.out" for c in range(KC))):
                pe.wait_ge(*due)
            (wkh, wkl), (wvh, wvl) = W4["wk"], W4["wv"]

            def keys_values(h):
                m0, mt = HALF[h]
                w = mt * S
                pe.wait_ge(*at.done(f"s4.low{h}"))
                for oc in range(KC):
                    for j in (0, 1):
                        n = 2 * oc + j
                        if n >= 4:
                            pe.wait_ge(*at.done(f"s4.K{h}.{n - 4}.out"))
                        elif h:
                            pe.wait_ge(*at.done(f"s4.K0.{n + 4}.out"))
                        else:
                            pe.wait_ge(*at.done("s4.exp7.1", back=1))
                        for c in range(KC):
                            f, m = slice(oc * P, (oc + 1) * P), slice(j * w, (j + 1) * w)
                            pe.matmul(bank(n % 4, w), wkh[:, c, f], CH[h][:, c, m], start=(c == 0), stop=False)
                            pe.matmul(bank(n % 4, w), wkh[:, c, f], CL[h][:, c, m], start=False, stop=False)
                            mm = pe.matmul(bank(n % 4, w), wkl[:, c, f], CH[h][:, c, m], start=False, stop=(c == KC - 1))
                        mm.then_inc(*at.step(f"s4.K{h}.{n}"))
                for j in range(mt):
                    if j >= 2:
                        pe.wait_ge(*at.done(f"s4.V{h}.{j - 2}.out"))
                    elif h:
                        pe.wait_ge(*at.done(f"s4.V0.{HALF[0][1] - 2 + j}.out"))
                    else:
                        for due in at.last("s4.pt7.2.out", "s4.pt7.3.out", back=1):
                            pe.wait_ge(*due)
                    for c in range(KC):
                        k, m = 4 + (m0 + j) % 2, slice(j * P, (j + 1) * P)
                        pe.matmul(bank(k), CH[h][:, c, m], wvh[:, c, :], start=(c == 0), stop=False)
                        pe.matmul(bank(k), CH[h][:, c, m], wvl[:, c, :], start=False, stop=False)
                        mm = pe.matmul(bank(k), CL[h][:, c, m], wvh[:, c, :], start=False, stop=(c == KC - 1))
                    mm.then_inc(*at.step(f"s4.V{h}.{j}"))
                at.same(f"s4.V{h}", f"s4.V{h}.{mt - 1}")

            def scores(p):
                g, a = p // 2, p % 2
                if not p:
                    for due in at.last(*(f"s4.K{h}.{n}.out" for n in range(8) for h in (0, 1))):
                        pe.wait_ge(*due)
                    pe.wait_ge(*at.done("s4.qd"))
                for j in range(4):
                    if p and j % 2 == 0:
                        pe.wait_ge(*at.done(f"s4.exp{p - 1}.{j // 2}"))
                    pe.matmul(bank(j, MB), QD[:, g, a * P:(a + 1) * P], KT[:, g, j * MB:(j + 1) * MB], start=True, stop=False)
                    mm = pe.matmul(bank(j, MB), idb[:, :], maskneg[:, j * MB:(j + 1) * MB], start=False, stop=True)
                    if j % 2:
                        mm.then_inc(*at.step(f"s4.S{p}.{j // 2}"))
                at.same(f"s4.S{p}")

            def values(p):
                pe.wait_ge(*at.done(f"s4.p{p}"))
                a = p % 2

                def transposes(k):
                    m0, n = TG[k]
                    if k >= 2:
                        pe.wait_ge(*at.done(f"s4.pt{p}.{k - 2}.out"))
                    elif p:
                        pe.wait_ge(*at.done(f"s4.pt{p - 1}.{k + 2}.out"))
                    else:
                        for j in range(HALF[1][1] - 2, HALF[1][1]):
                            pe.wait_ge(*at.done(f"s4.V1.{j}.out"))
                    for j in range(n):
                        mm = pe.transpose(PS[:, 4 + k % 2, j * P:(j + 1) * P], PR[:, a, (m0 + j) * P:(m0 + j + 1) * P], C["ident"])
                    mm.then_inc(*at.step(f"s4.pt{p}.{k}"))

                transposes(0)
                transposes(1)
                if p >= 2:
                    pe.wait_ge(*at.done(f"s4.o{p - 2}.out"))
                else:
                    pe.wait_ge(*at.done(f"s4.o{p + 6}.out", back=1))
                for k, (m0, n) in enumerate(TG):
                    pe.wait_ge(*at.done(f"s4.pt{p}.{k}.out"))
                    for m in range(m0, m0 + n):
                        mm = pe.matmul(PS[a * 64:a * 64 + 64, 6 + a, 0:P], VT[:, m, p * 64:(p + 1) * 64], PTs[:, m, :],
                                          start=(m == 0), stop=(m == MT - 1))
                    if k + 2 < len(TG):
                        transposes(k + 2)
                mm.then_inc(*at.step(f"s4.o{p}"))

            with at.loop(pe, "s4.loop", B) as b:
                keys_values(0)
                keys_values(1)
                scores(0)
                for p in range(NP):
                    if p + 1 < NP:
                        scores(p + 1)
                    values(p)
            at.same("s4.wk.used", "s4.o7"); at.same("s4.wv.used", "s4.o7")
            bank_reader.update({k: "s4.exp7.1" for k in range(4)})
            bank_reader.update({4: "s4.pt7.2.out", 5: "s4.pt7.3.out", 6: "s4.o6.out", 7: "s4.o7.out"})
            linear_pe(pe, at, "s4.wo_", [("s4.wo", O4)], (0, 1, 2, 3), range(KC), ["s4.o7.out"])

        def s4_act(act, at):
            norm_act(act, at, "s4.ln", X, "eps5", xc=TS[0])
            act.wait_ge(*at.done("s4.wk"))
            if before_wk_high:
                act.wait_ge(*at.done(before_wk_high + ".used"))
            act.activation(W4["wk"][0][:, :, :], wt("s4.wk")[:, :, :], ACT.Copy).then_inc(*at.step("s4.wk.high"))
            linear_out(act, at, "s4.q", (0, 1, 2, 3), range(KC), lambda ps, c: act.activation(Q4[:, c, :], ps, ACT.Identity, bias=v("bq4", c)))
            act.wait_ge(*at.done("s4.wv"))
            act.activation(W4["wv"][0][:, :, :], wt("s4.wv")[:, :, :], ACT.Copy).then_inc(*at.step("s4.wv.high"))
            act.wait_ge(*at.done("s4.flag"))
            with at.loop(act, "s4.loop", B) as b:
                for h in (0, 1):
                    m0, mt = HALF[h]
                    w = mt * S
                    act.wait_ge(*at.done("s4.S7", back=1))
                    for n in range(8):
                        act.wait_ge(*at.done(f"s4.K{h}.{n}"))
                        act.activation(KT[:, n // 2, m0 * P + (n % 2) * w:m0 * P + (n % 2 + 1) * w], bank(n % 4, w),
                                           ACT.Identity, bias=v("bk4", n // 2)).then_inc(*at.step(f"s4.K{h}.{n}.out"))
                        if h == 0 and n < KC:
                            act.wait_ge(*at.done("s4.ct1"))
                            act.wait_ge(*at.done("s4.V1", back=1))
                            act.activation(CH[1][:, n, :], CT[1][:, n, :], ACT.Copy).then_inc(*at.step(f"s4.high1.{n}"))
                for p in range(NP):
                    act.wait_ge(*at.done(f"s4.max{p}"))
                    if p >= 2:
                        act.wait_ge(*at.done(f"s4.pt{p - 2}.3"))
                    else:
                        act.wait_ge(*at.done(f"s4.pt{p + 6}.3", back=1))
                    for h in (0, 1):
                        act.activation(PR[:, p % 2, 2 * h * MB:2 * (h + 1) * MB].rearrange("p (a m) -> p a m", a=2), PS[:, 2 * h:2 * h + 2, 0:MB],
                                       ACT.Exp, bias=minus_max[p % 2], scale=SCALE, accum_out=total[p % 2][h]).then_inc(*at.step(f"s4.exp{p}.{h}"))
                    for k, (m0, n) in enumerate(TG[:2]):
                        act.wait_ge(*at.done(f"s4.pt{p}.{k}"))
                        if p:
                            act.wait_ge(*at.done(f"s4.o{p - 1}"))
                        act.activation(PTs[:, m0:m0 + n, :], PS[:, 4 + k % 2, 0:n * P].rearrange("p (m q) -> p m q", q=P),
                                           ACT.Copy).then_inc(*at.step(f"s4.pt{p}.{k}.out"))

        def s4_dve(dve, at):
            dve.wait_ge(*at.done("mask"))
            if 1 in stages:
                dve.wait_ge(*at.done("x1"))
            dve.tensor_scalar(keep, PR[:, 0, :].bitcast(I32), 0, None, ALU.not_equal).then_inc(*at.step())
            dve.wait_ge(*at.own())
            dve.tensor_scalar(maskneg[:, :], keep, -NEG, NEG, ALU.mult, ALU.add).then_inc(*at.step())
            dve.tensor_reduce(flag, keep, AX.X, ALU.max).then_inc(*at.step())
            dve.memset(TS[1][:, 2:4, :], 0.0).then_inc(*at.step("s4.flag"))
            norm_dve(dve, at, "s4.ln", X, N4, xc=N4)
            for w in ("wk", "wv"):
                dve.wait_ge(*at.done(f"s4.{w}.high"))
                dve.tensor_tensor(W4[w][1][:, :, :], wt(f"s4.{w}")[:, :, :], W4[w][0][:, :, :].bitcast(FP32), ALU.subtract).then_inc(*at.step(f"s4.{w}.low"))
            for c in range(KC):
                dve.wait_ge(*at.done(f"s4.q.{c}.out"))
            with at.loop(dve, "s4.loop", B) as b:
                dve.wait_ge(*at.done("s4.S7", back=1))
                for a in range(G):
                    dve.tensor_copy(qd[a * HD:(a + 1) * HD, :, a, :], Q4[a * HD:(a + 1) * HD, :, bass.ds(b * S, S)]).then_inc(*at.step("s4.qd"))
                dve.wait_ge(*at.done("s4.o7", back=1))
                for h in (0, 1):
                    m0, mt = HALF[h]
                    for j in range(mt):
                        dve.wait_ge(*at.done(f"s4.V{h}.{j}"))
                        dve.tensor_tensor(VT[:, m0 + j, :], bank(4 + (m0 + j) % 2), row("bv4", D), ALU.add).then_inc(*at.step(f"s4.V{h}.{j}.out"))
                        if h == 0 and j < KC:
                            dve.wait_ge(*at.done(f"s4.high1.{j}"))
                            dve.tensor_tensor(CL[1][:, j, :], CT[1][:, j, :], CH[1][:, j, :].bitcast(FP32), ALU.subtract).then_inc(*at.step("s4.low1"))

                def out(p):
                    a = (p % 2) * 64
                    dve.wait_ge(*at.done(f"s4.o{p}"))
                    for r in (0, 1):
                        q = a + r * HD
                        dve.tensor_copy(O4[q:q + HD, p // 2, bass.ds(b * S, S)], PS[q:q + HD, 6 + p % 2, r * S:(r + 1) * S]).then_inc(*at.step(f"s4.o{p}.out"))

                def transposed(p):
                    for k, (m0, n) in list(enumerate(TG))[2:]:
                        dve.wait_ge(*at.done(f"s4.pt{p}.{k}"))
                        if p:
                            dve.wait_ge(*at.done(f"s4.o{p - 1}"))
                        dve.tensor_copy(PTs[:, m0:m0 + n, :], PS[:, 4 + k % 2, 0:n * P].rearrange("p (m q) -> p m q", q=P)).then_inc(*at.step(f"s4.pt{p}.{k}.out"))

                for p in range(NP):
                    a = p % 2
                    for h in (0, 1):
                        dve.wait_ge(*at.done(f"s4.S{p}.{h}"))
                        dve.tensor_reduce(top[a][h], PS[:, 2 * h:2 * h + 2, 0:MB], AX.XY, ALU.max).then_inc(*at.step())
                    dve.wait_ge(*at.own())
                    dve.tensor_scalar(minus_max[a], top[a][0], top[a][1], -SCALE, ALU.max, ALU.mult).then_inc(*at.step(f"s4.max{p}"))
                    if p:
                        transposed(p - 1)
                    sm = total[a][0]
                    dve.wait_ge(*at.done(f"s4.exp{p}.1"))
                    dve.tensor_tensor(sm, sm, total[a][1], ALU.add).then_inc(*at.step())
                    dve.wait_ge(*at.own())
                    dve.reciprocal(sm, sm).then_inc(*at.step())
                    dve.wait_ge(*at.own())
                    dve.tensor_tensor(sm, sm, flag, ALU.mult).then_inc(*at.step())
                    dve.wait_ge(*at.own())
                    dve.tensor_scalar(PR[:, p % 2, :], PR[:, p % 2, :], sm, None, ALU.mult).then_inc(*at.step(f"s4.p{p}"))
                    if p:
                        out(p - 1)
                transposed(NP - 1)
                out(7)
            for c in range(KC):
                dve.wait_ge(*at.done(f"s4.wo_.{c}"))
                dve.scalar_tensor_tensor(out=X[:, c, :], in0=bank(c), scalar=v("bo4", c), in1=X[:, c, :],
                                             op0=ALU.add, op1=ALU.add).then_inc(*at.step(f"s4.wo_.{c}.out"))
            at.same("x4", "s4.wo_.3.out")

        N5, Q5, K5, V5, O5 = TS[0], TS[1], TS[2], TS[3], TS[4]
        trig = RC[:, 4200:4200 + 2 * T].rearrange("p (a s) -> p a s", a=2)

        def rotate_pe(pe, at, tag, x, outs, banks):
            for c in range(KC):
                pe.wait_ge(*at.done(outs[c]))
                if bank_reader.get(banks[c]):
                    pe.wait_ge(*at.done(bank_reader[banks[c]]))
                pe.matmul(bank(banks[c]), C["rot"], x[:, c, :], start=True, stop=True).then_inc(*at.step(f"{tag}.{c}"))
                bank_reader[banks[c]] = f"{tag}.{c}.out"

        def rotate_dve(dve, at, tag, x, tmp, banks):
            for c in range(KC):
                dve.wait_ge(*at.done(f"{tag}.{c}"))
                dve.tensor_tensor(tmp[:, c, :], bank(banks[c]), trig[:, 1, :], ALU.mult).then_inc(*at.step(f"{tag}.{c}.out"))
                dve.tensor_tensor(x[:, c, :], x[:, c, :], trig[:, 0, :], ALU.mult).then_inc(*at.step())
                dve.wait_ge(*at.own())
                dve.tensor_tensor(x[:, c, :], x[:, c, :], tmp[:, c, :], ALU.add).then_inc(*at.step(f"{tag}.done"))

        def s5_pool(pool, at):
            if 4 in stages:
                pool.wait_ge(*at.done("s4.S7"))
            pool.dma_start(trig, t["trig"]).then_inc(*at.load("mask_loaded", "trig"))
            if 4 in stages:
                pool.wait_ge(*at.done("s4.o7"))
            attn_pool(pool, at, "s5.at", K5, ["s5.kr.done"])

        def s5_pe(pe, at):
            norm_pe(pe, at, "s5.ln", X, chunk_steps("s4.wo_.", ".out") if 4 in stages else ["x"])
            linear_pe(pe, at, "s5.q", [("s5.wq", N5)], (0, 1, 2, 3), range(KC), chunks="s5.ln.done")
            linear_pe(pe, at, "s5.k", [("s5.wk", N5)], (4, 5, 6, 7), range(KC))
            rotate_pe(pe, at, "s5.qr", Q5, [f"s5.q.{c}.out" for c in range(KC)], (0, 1, 2, 3))
            rotate_pe(pe, at, "s5.kr", K5, [f"s5.k.{c}.out" for c in range(KC)], (4, 5, 6, 7))
            values_pe(pe, at, "s5.v", "s5.wv", N5, (0, 1, 2, 3))
            attn_pe(pe, at, "s5.at", Q5, V5, ["s5.qr.done"] + [f"s5.v.{c}.out" for c in range(4)])
            linear_pe(pe, at, "s5.o", [("s5.wo", O5)], (0, 1, 2, 3), range(KC), ["s5.at.O3.out"])

        def s5_act(act, at):
            norm_act(act, at, "s5.ln", X, "eps5", xc=N5)
            linear_out(act, at, "s5.q", (0, 1, 2, 3), range(KC), lambda ps, c: act.activation(Q5[:, c, :], ps, ACT.Identity, bias=v("bq5", c)))
            linear_out(act, at, "s5.k", (4, 5, 6, 7), range(KC), lambda ps, c: act.activation(K5[:, c, :], ps, ACT.Identity, bias=v("bk5", c)))
            attn_act(act, at, "s5.at")

        def s5_dve(dve, at):
            norm_dve(dve, at, "s5.ln", X, N5, xc=N5)
            dve.wait_ge(*at.done("trig"))
            rotate_dve(dve, at, "s5.qr", Q5, TS[4], (0, 1, 2, 3))
            rotate_dve(dve, at, "s5.kr", K5, TS[5], (4, 5, 6, 7))
            values_dve(dve, at, "s5.v", V5, "bv5", (0, 1, 2, 3))
            attn_dve(dve, at, "s5.at", K5, ["s5.kr.done"], O5, C["causal"])
            for c in range(KC):
                dve.wait_ge(*at.done(f"s5.o.{c}"))
                dve.scalar_tensor_tensor(out=X[:, c, :], in0=bank(c), scalar=v("bo5", c), in1=X[:, c, :],
                                             op0=ALU.add, op1=ALU.add).then_inc(*at.step(f"s5.o.{c}.out"))
            at.same("x5", "s5.o.3.out")

        N6, XT, SEL, SELG, SELT, EIN = TS[0], TS[1], TS[2], TS[3], TS[4], TS[5]
        YS = TS[1]
        EB = [QB[:, :, 0:S], QB[:, :, S:2 * S]]
        HS = [RC[0:S, 2048:2560], RC[0:S, 2560:3072]]
        HT = [RC[:, 3072 + 256 * k:3328 + 256 * k].rearrange("p (c s) -> p c s", c=KC) for k in (0, 1)]
        oh = RC[:, 128:160].rearrange("p (a e) -> p a e", e=E_)
        val = RC[:, 160:192].rearrange("p (a e) -> p a e", e=E_)
        gate6, idx6, pos6, over6, slot6 = (RC[:, 192 + 4 * k:196 + 4 * k] for k in range(5))

        def s6_pe(pe, at):
            norm_pe(pe, at, "s6.ln", X, chunk_steps("s5.o.", ".out") if 5 in stages else ["x"])
            gate_pe(pe, at, "s6.g", N6, 1, ["s6.ln.done"])
            for tt in range(4):
                k = 4 + tt
                if bank_reader.get(k):
                    pe.wait_ge(*at.done(bank_reader[k]))
                for c in range(KC):
                    mm = pe.transpose(PS[:, k, c * P:(c + 1) * P], N6[:, c, tt * P:(tt + 1) * P], C["ident"])
                mm.then_inc(*at.step(f"s6.xt{tt}"))
            pe.wait_ge(*at.done("s6.onehot"))
            if bank_reader.get(1):
                pe.wait_ge(*at.done(bank_reader[1]))
            for tt in range(4):
                for u in range(tt + 1):
                    mm = pe.matmul(PS[:, 1, tt * E_:(tt + 1) * E_], C["earlier"] if u == tt else C["ones"], oh[:, u, :],
                                      start=(u == 0), stop=(u == tt))
            mm.then_inc(*at.step("s6.pos"))
            for due in at.last("s6.sel", "s6.pos.out", *(f"s6.xt{k}.out" for k in range(4))):
                pe.wait_ge(*due)
            for dc in range(KC):
                if bank_reader.get(dc) and dc > 1:
                    pe.wait_ge(*at.done(bank_reader[dc]))
                for tt in range(4):
                    mm = pe.matmul(bank(dc), XT[:, tt, dc * P:(dc + 1) * P], SEL[:, tt, :], start=(tt == 0), stop=(tt == 3))
                mm.then_inc(*at.step(f"s6.ein{dc}"))
            for j in range(4):
                for tt in range(4):
                    mm = pe.transpose(PS[:, 4 + j, tt * P:(tt + 1) * P], SELG[:, tt, j * P:(j + 1) * P], C["ident"])
                mm.then_inc(*at.step(f"s6.selt{j}"))
            for due in at.last(*(f"s6.ein{k}.out" for k in range(4)), *(f"s6.selt{k}.out" for k in range(4))):
                pe.wait_ge(*due)
            with at.loop(pe, "s6.loop", E_ // 2) as j:
                for k in (0, 1):
                    q = f"s6.{k}"

                    def hidden(s):
                        w = f"s6.moe.{k}.a{s}"
                        pe.wait_ge(*at.done(w))
                        if s >= 2:
                            pe.wait_ge(*at.done(f"{q}.h{s - 2}.out"))
                        elif k:
                            pe.wait_ge(*at.done(f"s6.0.h{s + 2}.out"))
                        else:
                            pe.wait_ge(*at.done(f"s6.1.h{s + 2}.out", back=1))
                        for c in range(KC):
                            mm = pe.matmul(PS[0:S, s % 2, :], EB[k][:, c, :], wt(w)[:, c, :], start=(c == 0), stop=(c == KC - 1))
                        mm.then_inc(*at.step(f"{q}.h{s}"))
                        at.same(w + ".used", f"{q}.h{s}")

                    def output(s):
                        w = f"s6.moe.{k}.b{s}"
                        pe.wait_ge(*at.done(f"{q}.h{s}.out"))
                        if s >= 2:
                            pe.wait_ge(*at.done(f"{q}.ht{s - 2}.out"))
                        elif k:
                            pe.wait_ge(*at.done(f"s6.0.ht{s + 2}.out"))
                        else:
                            pe.wait_ge(*at.done(f"s6.1.ht{s + 2}.out", back=1))
                        pe.nop(nofuse=True)
                        for c in range(KC):
                            mm = pe.transpose(PS[:, 2 + s % 2, c * S:(c + 1) * S], HS[s % 2][:, c * P:(c + 1) * P],
                                                 C["ident"][0:S, 0:S])
                        mm.then_inc(*at.step(f"{q}.ht{s}"))
                        for due in at.last(w, f"{q}.ht{s}.out"):
                            pe.wait_ge(*due)
                        if s == 0:
                            pe.wait_ge(*at.done(f"{q}.y.out", back=1))
                        for c in range(KC):
                            mm = pe.matmul(PS[k * S:(k + 1) * S, 4 + k, :], HT[s % 2][:, c, :], wt(w)[:, c, :],
                                              start=(s == 0 and c == 0), stop=(s == FS - 1 and c == KC - 1))
                        mm.then_inc(*at.step(f"{q}.y{s}"))
                        at.same(w + ".used", f"{q}.y{s}")

                    pe.wait_ge(*at.done(f"{q}.eb"))
                    hidden(0)
                    for s in range(FS):
                        if s + 1 < FS:
                            hidden(s + 1)
                        output(s)
            for due in at.last("s6.0.y.out", "s6.1.y.out"):
                pe.wait_ge(*due)
            rd = {0: "s6.1.h2.out", 1: "s6.1.h3.out", 2: "s6.1.ht2.out", 3: "s6.1.ht3.out"}
            for dc in range(KC):
                pe.wait_ge(*at.done(rd[dc]))
                for j in range(4):
                    mm = pe.matmul(bank(dc), YS[:, j, dc * P:(dc + 1) * P], SELT[:, j, :], start=(j == 0), stop=(j == 3))
                mm.then_inc(*at.step(f"s6.out{dc}"))

        def s6_act(act, at):
            norm_act(act, at, "s6.ln", X, "eps5", xc=N6)
            gate_act(act, at, "s6.g")
            for dc in range(KC):
                act.wait_ge(*at.done(f"s6.ein{dc}"))
                act.activation(EIN[:, dc, :], bank(dc), ACT.Copy).then_inc(*at.step(f"s6.ein{dc}.out"))
            for j in range(4):
                act.wait_ge(*at.done(f"s6.selt{j}"))
                act.activation(SELT[:, j, :], bank(4 + j), ACT.Copy).then_inc(*at.step(f"s6.selt{j}.out"))
            with at.loop(act, "s6.loop", E_ // 2) as j:
                for k in (0, 1):
                    q = f"s6.{k}"
                    for s in range(FS):
                        act.wait_ge(*at.done(f"{q}.h{s}"))
                        if s >= 2:
                            act.wait_ge(*at.done(f"{q}.ht{s - 2}"))
                        elif k:
                            act.wait_ge(*at.done(f"s6.0.ht{s + 2}"))
                        else:
                            act.wait_ge(*at.done(f"s6.1.ht{s + 2}", back=1))
                        act.activation(HS[s % 2], PS[0:S, s % 2, :], ACT.Gelu_apprx_tanh).then_inc(*at.step(f"{q}.h{s}.out"))

        def s6_dve(dve, at):
            norm_dve(dve, at, "s6.ln", X, N6, xc=N6)
            gate_dve(dve, at, "s6.g", False)
            for tt in range(4):
                dve.wait_ge(*at.done(f"s6.xt{tt}"))
                dve.tensor_copy(XT[:, tt, :], bank(4 + tt)).then_inc(*at.step(f"s6.xt{tt}.out"))
            bc = lambda a: a.unsqueeze(2).broadcast_to([P, 4, E_])
            iota_e = row("iota_e", 32).rearrange("p (a e) -> p a e", e=E_)
            dve.wait_ge(*at.own())
            dve.tensor_reduce(gate6, ga, AX.X, ALU.max).then_inc(*at.step())
            dve.wait_ge(*at.own())
            dve.tensor_tensor(val, ga, bc(gate6), ALU.is_equal).then_inc(*at.step())
            dve.wait_ge(*at.own())
            dve.scalar_tensor_tensor(out=val, in0=val, scalar=-128.0, in1=iota_e, op0=ALU.mult, op1=ALU.add).then_inc(*at.step())
            dve.wait_ge(*at.own())
            dve.tensor_reduce(idx6, val, AX.X, ALU.min).then_inc(*at.step())
            dve.wait_ge(*at.own())
            dve.tensor_tensor(oh, val, bc(idx6), ALU.is_equal).then_inc(*at.step("s6.onehot"))
            dve.wait_ge(*at.done("s6.pos"))
            dve.tensor_tensor(val, PS[:, 1, 0:32].rearrange("p (a e) -> p a e", e=E_), oh, ALU.mult).then_inc(*at.step("s6.pos.out"))
            dve.wait_ge(*at.own())
            dve.tensor_reduce(pos6, val, AX.X, ALU.add).then_inc(*at.step())
            dve.wait_ge(*at.own())
            dve.tensor_scalar(over6, pos6, float(CAP), 16384.0, ALU.is_ge, ALU.mult).then_inc(*at.step())
            dve.tensor_scalar(slot6, idx6, float(CAP), 128.0 * CAP, ALU.mult, ALU.add).then_inc(*at.step())
            dve.wait_ge(*at.own())
            dve.tensor_tensor(slot6, slot6, pos6, ALU.add).then_inc(*at.step())
            dve.wait_ge(*at.own())
            dve.tensor_tensor(slot6, slot6, over6, ALU.add).then_inc(*at.step())
            dve.wait_ge(*at.own())
            for tt in range(4):
                dve.tensor_scalar(SEL[:, tt, :], row("iota_slot", D), slot6[:, tt:tt + 1], None, ALU.is_equal).then_inc(*at.step())
            dve.wait_ge(*at.own())
            for tt in range(4):
                dve.tensor_scalar(SELG[:, tt, :], SEL[:, tt, :], gate6[:, tt:tt + 1], None, ALU.mult).then_inc(*at.step("s6.sel"))
            for due in at.last(*(f"s6.ein{k}.out" for k in range(4))):
                dve.wait_ge(*due)
            with at.loop(dve, "s6.loop", E_ // 2) as j:
                for k in (0, 1):
                    q = f"s6.{k}"
                    dve.wait_ge(*at.done(f"{q}.h3", back=1))
                    dve.tensor_copy(EB[k], EIN[:, :, bass.ds(j * (2 * S) + k * S, S)]).then_inc(*at.step(f"{q}.eb"))
                for k in (0, 1):
                    q = f"s6.{k}"
                    for s in range(FS):
                        dve.wait_ge(*at.done(f"{q}.ht{s}"))
                        if s >= 2:
                            dve.wait_ge(*at.done(f"{q}.y{s - 2}"))
                        elif k:
                            dve.wait_ge(*at.done(f"s6.0.y{s + 2}"))
                        else:
                            dve.wait_ge(*at.done(f"s6.1.y{s + 2}", back=1))
                        dve.tensor_copy(HT[s % 2], PS[:, 2 + s % 2, 0:KC * S].rearrange("p (c s) -> p c s", c=KC)).then_inc(*at.step(f"{q}.ht{s}.out"))
                    dve.wait_ge(*at.done(f"{q}.y3"))
                    dve.tensor_copy(YS[k * S:(k + 1) * S, j, :], PS[k * S:(k + 1) * S, 4 + k, :]).then_inc(*at.step(f"{q}.y.out"))
            for dc in range(KC):
                dve.wait_ge(*at.done(f"s6.out{dc}"))
                dve.tensor_tensor(X[:, dc, :], X[:, dc, :], bank(dc), ALU.add).then_inc(*at.step("x6"))

        @block.sync
        def _(sync):
            at = Steps(sems, "out_stored", marks, new)
            for dst, src, name in ((X[:, :, :], t["x"], "x"), (sq[:, :, :], t["squares"], "x"), (vec[:, :], t["vecs"], "consts"),
                                   (rows[:, :], t["rows"], "consts"), (gw[:, :, :, :], t["gates"], "consts"), (RC[:, 1600:1792].rearrange("p (a b) -> p a b", a=3), t["abc"], "consts")):
                sync.dma_start(dst, src).then_inc(*at.load("consts_loaded", name))
            at.same("abc", "consts"); at.same("x", "consts")
            for name, tile in order:
                if tile is not None:
                    if before[name]:
                        sync.wait_ge(*at.done(before[name] + ".used"))
                    sync.dma_start(ring[slot[name]][:, :, :], t["tiles"][tile]).then_inc(*at.load(f"weights_loaded{slot[name]}", name))
                    continue
                for x in before[name]:
                    sync.wait_ge(*at.done(x + ".used"))
                if name == "s3.moe":
                    with at.loop(sync, "s3.loop", E_) as i:
                        for k, x in enumerate(EXPERT):
                            prev = EXPERT[(k - RING) % 8]
                            sync.wait_ge(*at.done(f"{name}.{prev}.used", back=0 if k >= RING else 1))
                            sync.dma_start(ring[k % RING][:, :, :], t["experts3"][i, k]).then_inc(*at.load(f"weights_loaded{k % RING}", f"{name}.{x}"))
                else:
                    with at.loop(sync, "s6.loop", E_ // 2) as i:
                        for n in range(16):
                            prev = (n - RING) % 16
                            sync.wait_ge(*at.done(f"{name}.{prev // 8}.{EXPERT[prev % 8]}.used", back=0 if n >= RING else 1))
                            sync.dma_start(ring[n % RING][:, :, :], t["experts6"][i, n]).then_inc(*at.load(f"weights_loaded{n % RING}", f"{name}.{n // 8}.{EXPERT[n % 8]}"))
            sync.wait_ge(*at.done(f"x{max(stages)}"))
            sync.dma_start(t["out"], X[:, :, :]).then_inc(*at.load("out_stored", "stored"))
            sync.wait_ge(sems["out_stored"], 16)

        @block.gpsimd
        def _(pool):
            at = Steps(sems, "pool_done", marks, new)
            if 1 in stages:
                s1_pool(pool, at)
                pool.wait_ge(*at.done("s1.2.loop.UT.1"))
            pool.dma_start(PR[:, 0, :].bitcast(I32), t["mask"]).then_inc(*at.load("mask_loaded", "mask"))
            for s, part in ((2, s2_pool), (3, s3_pool), (4, s4_pool), (5, s5_pool)):
                if s in stages:
                    part(pool, at)

        @block.scalar
        def _(act):
            at = Steps(sems, "scalar_done", marks, new)
            act.wait_ge(*at.done("x"))
            act.activation(rstd[:, 0:1], C["ident"][:, 0:1], ACT.Copy).then_inc(*at.step(by=AHEAD))
            act.wait_ge(*at.done("abc"))
            act.activation(abc[:, 0], abc[:, 0], ACT.Sigmoid).then_inc(*at.step("s2.decay"))
            for s, part in ((1, s1_act), (2, s2_act), (3, s3_act), (4, s4_act), (5, s5_act), (6, s6_act)):
                if s in stages:
                    part(act, at)

        @block.tensor
        def _(pe):
            at = Steps(sems, "tensor_done", marks, new)
            bank_reader.clear()
            pe.wait_ge(*at.done("x"))
            pe.matmul(bank(7, 1), C["ident"], C["ident"][:, 0:1], start=True, stop=True).then_inc(*at.step(by=AHEAD))
            for s, part in ((1, s1_pe), (2, s2_pe), (3, s3_pe), (4, s4_pe), (5, s5_pe), (6, s6_pe)):
                if s in stages:
                    part(pe, at)

        @block.vector
        def _(dve):
            at = Steps(sems, "vector_done", marks, new)
            dve.wait_ge(*at.done("x"))
            dve.tensor_copy(idb[:, :], C["ident"]).then_inc(*at.step("idb", AHEAD))
            for s, part in ((1, s1_dve), (2, s2_dve), (3, s3_dve), (4, s4_dve), (5, s5_dve), (6, s6_dve)):
                if s in stages:
                    part(dve, at)


def _tiles(w, n=None):
    a, b = w.shape[0] // D, w.shape[1] // D
    return w.reshape(a, KC, P, b, D).transpose(0, 3, 2, 1, 4).reshape(a * b, P, KC, D)


def layout(i):
    f = lambda n: np.asarray(i[n])
    feat = lambda a: a.reshape(T, D).T.reshape(KC, P, T).transpose(1, 0, 2)
    ctx = np.zeros((B, MP, D), np.float32)
    ctx[:, :M] = f("ctx_1024")
    g, a0, f0 = "L0_xattn_", "L0_attn_", "L0_ffn_"
    tiles = [f(g + "Wq").T, f(g + "Wk"), f(g + "Wv").T]
    for k in (0, 2, 1):
        tiles += [f(g + "gru_whh")[k * D:(k + 1) * D].T, f(g + "gru_wih")[k * D:(k + 1) * D].T]
    tiles += [f(a0 + "out_w").T]
    for j in range(FS):
        tiles += [f(a0 + "ffn1_w")[j * D:(j + 1) * D].T, f(a0 + "ffn2_w")[:, j * D:(j + 1) * D].T]
    tiles += [f(f0 + "conv_w")[:, :, k].T for k in range(3)]
    tiles += [f(f0 + "wqkv")[k * D:(k + 1) * D].T for k in range(3)] + [f(f0 + "wo").T]
    tiles += [f("L1_xattn_" + n) for n in ("Wq", "Wk", "Wv", "Wo")] + [f("L1_attn_" + n).T for n in ("Wq", "Wk", "Wv", "Wo")]
    experts = lambda w1, w2: np.stack([np.concatenate([(_tiles(w1[x]) if ab == "a" else _tiles(w2[x]))[int(s):int(s) + 1]
                                       for ab, s in ("a0", "a1", "b0", "a2", "b1", "a3", "b2", "b3")]) for x in range(E_)])
    src = dict(slot_w=g + "slot_norm_w", in_w=g + "input_norm_w", bih=g + "gru_bih", bhh=g + "gru_bhh", ln_w=a0 + "ln_w",
               ln_b=a0 + "ln_b", D=a0 + "D_vec", out_b=a0 + "out_b", ln2_w=a0 + "ln2_w", ln2_b=a0 + "ln2_b",
               ffn1_b=a0 + "ffn1_b", ffn2_b=a0 + "ffn2_b", conv_b=f0 + "conv_b", bqkv=f0 + "bqkv", bo3=f0 + "bo",
               ln1_g=f0 + "ln1_g", ln1_b=f0 + "ln1_b", ln2_g=f0 + "ln2_g", ln2b3=f0 + "ln2_b", b1=f0 + "b1", b2=f0 + "b2",
               bq4="L1_xattn_bq", bk4="L1_xattn_bk", bo4="L1_xattn_bo", bq5="L1_attn_bq", bk5="L1_attn_bk", bo5="L1_attn_bo")
    vecs = np.concatenate([f(src[n]).reshape(-1, P).T for n, _ in VECS], axis=1)
    rep = lambda a: np.broadcast_to(a, (P, a.shape[-1]))
    rows = np.concatenate([rep(f(f0 + "gate_b")), rep(f(f0 + "bqkv")[2 * D:]), rep(f("L1_xattn_bv")), rep(f("L1_attn_bv")),
                           rep(np.arange(D, dtype=np.float32)), rep(np.tile(np.arange(E_, dtype=np.float32), 4)),
                           (np.arange(P)[:, None] < MLAST).astype(np.float32),
                           np.full((P, 1), 1e-5, np.float32), np.full((P, 1), 1e-6, np.float32)], axis=1)
    gates = np.stack([f(f0 + "gate_w").reshape(KC, P, E_), f("L1_ffn_router_w").reshape(KC, P, E_)]).transpose(2, 0, 1, 3)
    abc = np.stack([f(a0 + n).reshape(KC, P, N_STATE) for n in ("A_log", "B_mat", "C_mat")]).transpose(2, 0, 1, 3).reshape(P, 3, -1)
    r = np.arange(P)
    same = (r[:, None] // S) == (r[None] // S)
    rot = np.zeros((P, P), np.float32)
    rot[r[1::2], r[::2]] = -1
    rot[r[::2], r[1::2]] = 1
    squares = np.stack([np.eye(P), np.full((P, P), 1 / D), np.ones((P, P)), np.where(same, 0, NEG),
                        np.where(same & (r[None] <= r[:, None]), 0, NEG), r[:, None] < r[None], rot]).astype(np.float32)
    ang = np.outer(np.arange(S, dtype=np.float32), (1.0 / np.float32(10000.0) ** (np.arange(0, HD, 2, dtype=np.float32) / HD)))
    ang = np.tile(ang[:, (r % HD) // 2].T, (1, B)).astype(np.float32)
    mask = np.zeros((P, MP), np.int32)
    mask[:, :M] = np.concatenate([f("mask_SxS2_ik0")] * 2)
    return {
        "x": feat(f("x")), "ctxN": ctx.reshape(B, MT, P, D).transpose(0, 2, 1, 3),
        "ctxT": ctx.reshape(B, MP, KC, P).transpose(0, 3, 2, 1), "mask": mask,
        "tiles": np.stack([_tiles(w)[0] for w in tiles]),
        "experts3": experts(f(f0 + "w1"), f(f0 + "w2")),
        "experts6": experts(f("L1_ffn_w1"), f("L1_ffn_w2")).reshape(E_ // 2, 16, P, KC, D),
        "vecs": vecs, "rows": rows, "gates": gates, "abc": abc,
        "squares": squares.transpose(1, 0, 2), "trig": np.stack([np.cos(ang), np.sin(ang)], axis=1),
    }


def kernel(**inputs):
    import concourse.bacc as bacc
    from concourse.bass_utils import run_bass_kernel_spmd

    arrays = {n: np.ascontiguousarray(a) for n, a in layout(inputs).items()}

    def program(marks):
        nc = bacc.Bacc("TRN2", target_bir_lowering=False, num_devices=1)
        t = {n: nc.dram_tensor(f"in_{n}", a.shape, mybir.dt.from_np(a.dtype), kind="ExternalInput").ap() for n, a in arrays.items()}
        t["out"] = nc.dram_tensor("out_x", (P, KC, T), FP32, kind="ExternalOutput").ap()
        new = Marks()
        build(nc, marks, new, t)
        return nc, new

    _, counted = program(Marks())
    nc, _ = program(counted)
    r = run_bass_kernel_spmd(nc, [{f"in_{n}": a for n, a in arrays.items()}], core_ids=[0])
    y = r.results[0]["out_x"]
    return np.ascontiguousarray(y.transpose(1, 0, 2).reshape(D, T).T).reshape(B, S, D)
```
